# Optimizing a Trainium2 kernel written in Bass

```python
import numpy as np
import jax
import jax.numpy as jnp

def _softmax(x, axis=-1):
    return jax.nn.softmax(x, axis=axis)

def _gelu(x):
    return jax.nn.gelu(x, approximate=True)

def _silu(x):
    return jax.nn.silu(x)

def _sigmoid(x):
    return jax.nn.sigmoid(x)

def _layernorm(x, axis=-1, eps=1e-05):
    m = jnp.mean(x, axis=axis, keepdims=True)
    v = jnp.var(x, axis=axis, keepdims=True)
    return (x - m) / jnp.sqrt(v + eps)

def _scatter_add(tgt, idx, src, axis=0):
    return tgt.at[idx].add(src)

def _segment_sum(src, seg, n):
    return jax.ops.segment_sum(src, seg, n)
kernel_name = 'mk_gnn_preln_d4_gnn_r32_76f5c8'

def setup_inputs(seed: int=0):
    np.random.seed(seed)
    _w = jnp.asarray

    def _rec_inputs():
        import jax
        import jax.numpy as jnp
        _gk = jax.random.key(seed)
        x = -0.0002117 + 1 * jax.random.normal(jax.random.fold_in(_gk, 1), (3125, 256), jnp.float32)
        _s = jax.random.randint(jax.random.fold_in(_gk, 2), (25000,), 0, 3125, jnp.int32)
        _d = jax.random.randint(jax.random.fold_in(_gk, 3), (25000,), 0, 3125, jnp.int32)
        _loop = jnp.arange(3125, dtype=jnp.int32)
        src = jnp.concatenate([_s, _d, _loop])
        dst = jnp.concatenate([_d, _s, _loop])
        _o = jnp.argsort(dst, stable=True)
        src = src[_o]
        dst = dst[_o]
        edge_attr_16 = 0.000398945 + 1.00003 * jax.random.normal(jax.random.fold_in(_gk, 13), (53125, 16), jnp.float32)
        node_vec1 = -0.00396605 + 0.997609 * jax.random.normal(jax.random.fold_in(_gk, 15), (3125, 1), jnp.float32)
        return (x, src, dst, edge_attr_16, node_vec1)
    x, src, dst, edge_attr_16, node_vec1 = _rec_inputs()

    def _L0_gnn_setup():
        import jax, jax.numpy as jnp
        import numpy as np
        N = 3125
        H = 256
        E = 100000
        OUT = 2
        NEG_SLOPE = 0.2

        def _gat_conv(feat, edge_src, edge_dst, W, attn_l, attn_r, bias):
            z = feat @ W
            el = z @ attn_l
            er = z @ attn_r
            e = jax.nn.leaky_relu(el[edge_src] + er[edge_dst], NEG_SLOPE)
            m = jax.ops.segment_max(e, edge_dst, num_segments=N)
            ex = jnp.exp(e - m[edge_dst])
            denom = jax.ops.segment_sum(ex, edge_dst, num_segments=N)
            alpha = ex / denom[edge_dst]
            out = jax.ops.segment_sum(alpha[:, None] * z[edge_src], edge_dst, num_segments=N)
            return out + bias
        key = jax.random.key(seed)
        ks = jax.random.split(key, 8)
        return {'input': jax.random.normal(ks[0], (N, H), dtype=jnp.float32), 'x': jax.random.normal(ks[1], (N, 1), dtype=jnp.float32), 'degree': jnp.ones((N, 1), dtype=jnp.float32), 'edge_src': jax.random.randint(ks[2], (E,), 0, N, dtype=jnp.int32), 'edge_dst': jax.random.randint(ks[3], (E,), 0, N, dtype=jnp.int32), 'W': jax.random.normal(ks[4], (H, OUT), dtype=jnp.float32) * (1.0 / np.sqrt(H)), 'attn_l': jax.random.normal(ks[5], (OUT,), dtype=jnp.float32), 'attn_r': jax.random.normal(ks[6], (OUT,), dtype=jnp.float32), 'bias': jax.random.normal(ks[7], (OUT,), dtype=jnp.float32) * 0.02}
    _L0_gnn_all = _L0_gnn_setup()
    _L0_gnn_in = {k: v for k, v in _L0_gnn_all.items() if k in ('W', 'attn_l', 'attn_r', 'bias')}
    del _L0_gnn_all

    def _L1_gnn_setup():
        import jax, jax.numpy as jnp
        import numpy as np
        BN_EPS = 1e-05
        key = jax.random.key(seed)
        ks = jax.random.split(key, 4)
        N, E, H = (10000, 10000, 256)
        x = jax.random.normal(ks[0], (N, H), dtype=jnp.float32)
        edge_index = jax.random.randint(ks[1], (2, E), 0, N, dtype=jnp.int64)
        weight = jax.random.normal(ks[2], (H, H), dtype=jnp.float32) * (1.0 / np.sqrt(H))
        bias = jax.random.normal(ks[3], (H,), dtype=jnp.float32) * 0.02
        gamma = jnp.ones((H,), dtype=jnp.float32)
        beta = jnp.zeros((H,), dtype=jnp.float32)
        running_mean = jnp.zeros((H,), dtype=jnp.float32)
        running_var = jnp.ones((H,), dtype=jnp.float32)
        return {'x': x, 'edge_index': edge_index, 'weight': weight, 'bias': bias, 'gamma': gamma, 'beta': beta, 'running_mean': running_mean, 'running_var': running_var}
    _L1_gnn_all = _L1_gnn_setup()
    _L1_gnn_in = {k: v for k, v in _L1_gnn_all.items() if k in ('weight', 'bias', 'gamma', 'beta', 'running_mean', 'running_var')}
    del _L1_gnn_all

    def _L2_gnn_setup():
        import jax, jax.numpy as jnp
        import numpy as np
        N, IN_CH, HEADS, OUT_CH, E = (50000, 256, 4, 64, 25000)
        key = jax.random.key(seed)
        k1, k2, k3, k4, k5 = jax.random.split(key, 5)
        x = jax.random.normal(k1, (N, IN_CH), dtype=jnp.float32)
        edge_index = jax.random.randint(k2, (2, E), 0, N, dtype=jnp.int64)
        bw = float(np.sqrt(6.0 / (IN_CH + HEADS * OUT_CH)))
        ba = float(np.sqrt(6.0 / (HEADS + OUT_CH)))
        weight = jax.random.uniform(k3, (IN_CH, HEADS * OUT_CH), jnp.float32, -bw, bw)
        attn_l = jax.random.uniform(k4, (HEADS, OUT_CH), jnp.float32, -ba, ba)
        attn_r = jax.random.uniform(k5, (HEADS, OUT_CH), jnp.float32, -ba, ba)
        return {'x': x, 'edge_index': edge_index, 'weight': weight, 'attn_l': attn_l, 'attn_r': attn_r}
    _L2_gnn_all = _L2_gnn_setup()
    _L2_gnn_in = {k: v for k, v in _L2_gnn_all.items() if k in ('weight', 'attn_l', 'attn_r')}
    del _L2_gnn_all

    def _L3_gnn_setup():
        import jax, jax.numpy as jnp
        import numpy as np
        N, E = (50000, 12500)
        HEADS, DIMS, EDGE_DIM = (4, 64, 16)
        FEAT = HEADS * DIMS
        NEG_SLOPE = 0.2

        def _gatv2(x, edge_index, edge_attr, W_l, b_l, W_r, b_r, W_e, att, bias):
            n = x.shape[0]
            src, dst = (edge_index[0], edge_index[1])
            x_l = (x @ W_l.T + b_l).reshape(n, HEADS, DIMS)
            x_r = (x @ W_r.T + b_r).reshape(n, HEADS, DIMS)
            ones = jnp.ones((src.shape[0],), x.dtype)
            deg = jax.ops.segment_sum(ones, dst, num_segments=n)
            loop_attr = jax.ops.segment_sum(edge_attr, dst, num_segments=n)
            loop_attr = loop_attr / jnp.clip(deg, 1.0, None)[:, None]
            loop = jnp.arange(n, dtype=src.dtype)
            src = jnp.concatenate([src, loop])
            dst = jnp.concatenate([dst, loop])
            e_attr = jnp.concatenate([edge_attr, loop_attr], axis=0)
            e_feat = (e_attr @ W_e.T).reshape(-1, HEADS, DIMS)
            s = x_l[src] + x_r[dst] + e_feat
            s = jax.nn.leaky_relu(s, NEG_SLOPE)
            alpha = jnp.einsum('ehc,hc->eh', s, att)
            amax = jax.ops.segment_max(alpha, dst, num_segments=n)
            ex = jnp.exp(alpha - amax[dst])
            denom = jax.ops.segment_sum(ex, dst, num_segments=n)
            alpha = ex / (denom[dst] + 1e-16)
            out = jax.ops.segment_sum(alpha[..., None] * x_l[src], dst, num_segments=n)
            return out.reshape(n, FEAT) + bias
        key = jax.random.key(seed)
        ks = jax.random.split(key, 10)
        s = 0.05
        return {'x': jax.random.normal(ks[0], (N, FEAT), jnp.float32), 'edge_index': jax.random.randint(ks[1], (2, E), 0, N, jnp.int64), 'edge_attr': jax.random.normal(ks[2], (E, EDGE_DIM), jnp.float32), 'W_l': jax.random.normal(ks[3], (FEAT, FEAT), jnp.float32) * s, 'b_l': jnp.zeros((FEAT,), jnp.float32), 'W_r': jax.random.normal(ks[4], (FEAT, FEAT), jnp.float32) * s, 'b_r': jnp.zeros((FEAT,), jnp.float32), 'W_e': jax.random.normal(ks[5], (FEAT, EDGE_DIM), jnp.float32) * s, 'att': jax.random.normal(ks[6], (HEADS, DIMS), jnp.float32) * s, 'bias': jnp.zeros((FEAT,), jnp.float32)}
    _L3_gnn_all = _L3_gnn_setup()
    _L3_gnn_in = {k: v for k, v in _L3_gnn_all.items() if k in ('W_l', 'b_l', 'W_r', 'b_r', 'W_e', 'att', 'bias')}
    del _L3_gnn_all
    return {'x': x, 'src': src, 'dst': dst, 'edge_attr_16': edge_attr_16, 'node_vec1': node_vec1, 'L0_gnn_W': _L0_gnn_in['W'], 'L0_gnn_attn_l': _L0_gnn_in['attn_l'], 'L0_gnn_attn_r': _L0_gnn_in['attn_r'], 'L0_gnn_bias': _L0_gnn_in['bias'], 'L1_gnn_weight': _L1_gnn_in['weight'], 'L1_gnn_bias': _L1_gnn_in['bias'], 'L1_gnn_gamma': _L1_gnn_in['gamma'], 'L1_gnn_beta': _L1_gnn_in['beta'], 'L1_gnn_running_mean': _L1_gnn_in['running_mean'], 'L1_gnn_running_var': _L1_gnn_in['running_var'], 'L2_gnn_weight': _L2_gnn_in['weight'], 'L2_gnn_attn_l': _L2_gnn_in['attn_l'], 'L2_gnn_attn_r': _L2_gnn_in['attn_r'], 'L3_gnn_W_l': _L3_gnn_in['W_l'], 'L3_gnn_b_l': _L3_gnn_in['b_l'], 'L3_gnn_W_r': _L3_gnn_in['W_r'], 'L3_gnn_b_r': _L3_gnn_in['b_r'], 'L3_gnn_W_e': _L3_gnn_in['W_e'], 'L3_gnn_att': _L3_gnn_in['att'], 'L3_gnn_bias': _L3_gnn_in['bias']}

def reference(x, src, dst, edge_attr_16, node_vec1, L0_gnn_W, L0_gnn_attn_l, L0_gnn_attn_r, L0_gnn_bias, L1_gnn_weight, L1_gnn_bias, L1_gnn_gamma, L1_gnn_beta, L1_gnn_running_mean, L1_gnn_running_var, L2_gnn_weight, L2_gnn_attn_l, L2_gnn_attn_r, L3_gnn_W_l, L3_gnn_b_l, L3_gnn_W_r, L3_gnn_b_r, L3_gnn_W_e, L3_gnn_att, L3_gnn_bias):
    import jax
    import jax.numpy as jnp

    def _L0_gnn_ref(input, x, degree, edge_src, edge_dst, W, attn_l, attn_r, bias):
        import jax, jax.numpy as jnp
        import numpy as np
        N = 3125
        H = 256
        E = 100000
        OUT = 2
        NEG_SLOPE = 0.2

        def _gat_conv(feat, edge_src, edge_dst, W, attn_l, attn_r, bias):
            z = feat @ W
            el = z @ attn_l
            er = z @ attn_r
            e = jax.nn.leaky_relu(el[edge_src] + er[edge_dst], NEG_SLOPE)
            m = jax.ops.segment_max(e, edge_dst, num_segments=N)
            ex = jnp.exp(e - m[edge_dst])
            denom = jax.ops.segment_sum(ex, edge_dst, num_segments=N)
            alpha = ex / denom[edge_dst]
            out = jax.ops.segment_sum(alpha[:, None] * z[edge_src], edge_dst, num_segments=N)
            return out + bias
        coff = _gat_conv(input, edge_src, edge_dst, W, attn_l, attn_r, bias)
        std = jax.nn.relu(coff[:, 0:1])
        mean = jax.nn.relu(coff[:, 1:2])
        return input * jax.nn.sigmoid(x * std + mean)

    def _L1_gnn_ref(x, edge_index, weight, bias, gamma, beta, running_mean, running_var):
        import jax, jax.numpy as jnp
        import numpy as np
        BN_EPS = 1e-05
        N = x.shape[0]
        xb = (x - running_mean) * jax.lax.rsqrt(running_var + BN_EPS) * gamma + beta
        loop = jnp.arange(N, dtype=edge_index.dtype)
        src = jnp.concatenate([edge_index[0], loop])
        dst = jnp.concatenate([edge_index[1], loop])
        deg = jax.ops.segment_sum(jnp.ones(src.shape[0], dtype=xb.dtype), dst, num_segments=N)
        dinv = jax.lax.rsqrt(deg)
        norm = dinv[src] * dinv[dst]
        h = xb @ weight
        msg = norm[:, None] * h[src]
        out = jax.ops.segment_sum(msg, dst, num_segments=N) + bias
        return jax.nn.relu(out)

    def _L2_gnn_ref(x, edge_index, weight, attn_l, attn_r):
        import jax, jax.numpy as jnp
        import numpy as np
        N, IN_CH, HEADS, OUT_CH, E = (50000, 256, 4, 64, 25000)
        heads, out_ch = attn_l.shape
        n = x.shape[0]
        xt = jnp.matmul(x, weight).reshape(-1, heads, out_ch)
        row, col = (edge_index[0], edge_index[1])
        alpha_l = jnp.einsum('ehd,hd->eh', xt[row], attn_l)
        alpha_r = jnp.einsum('ehd,hd->eh', xt[col], attn_r)
        alpha = jax.nn.softmax(jax.nn.leaky_relu(alpha_l + alpha_r, 0.01), axis=1)
        tmp = jnp.einsum('nh,nhd->nd', alpha[:n], xt[col[:n]])
        out = jnp.broadcast_to(tmp[:, None, :], (n, heads, out_ch))
        return out.reshape(n, heads * out_ch)

    def _L3_gnn_ref(x, edge_index, edge_attr, W_l, b_l, W_r, b_r, W_e, att, bias):
        import jax, jax.numpy as jnp
        import numpy as np
        N, E = (50000, 12500)
        HEADS, DIMS, EDGE_DIM = (4, 64, 16)
        FEAT = HEADS * DIMS
        NEG_SLOPE = 0.2

        def _gatv2(x, edge_index, edge_attr, W_l, b_l, W_r, b_r, W_e, att, bias):
            n = x.shape[0]
            src, dst = (edge_index[0], edge_index[1])
            x_l = (x @ W_l.T + b_l).reshape(n, HEADS, DIMS)
            x_r = (x @ W_r.T + b_r).reshape(n, HEADS, DIMS)
            ones = jnp.ones((src.shape[0],), x.dtype)
            deg = jax.ops.segment_sum(ones, dst, num_segments=n)
            loop_attr = jax.ops.segment_sum(edge_attr, dst, num_segments=n)
            loop_attr = loop_attr / jnp.clip(deg, 1.0, None)[:, None]
            loop = jnp.arange(n, dtype=src.dtype)
            src = jnp.concatenate([src, loop])
            dst = jnp.concatenate([dst, loop])
            e_attr = jnp.concatenate([edge_attr, loop_attr], axis=0)
            e_feat = (e_attr @ W_e.T).reshape(-1, HEADS, DIMS)
            s = x_l[src] + x_r[dst] + e_feat
            s = jax.nn.leaky_relu(s, NEG_SLOPE)
            alpha = jnp.einsum('ehc,hc->eh', s, att)
            amax = jax.ops.segment_max(alpha, dst, num_segments=n)
            ex = jnp.exp(alpha - amax[dst])
            denom = jax.ops.segment_sum(ex, dst, num_segments=n)
            alpha = ex / (denom[dst] + 1e-16)
            out = jax.ops.segment_sum(alpha[..., None] * x_l[src], dst, num_segments=n)
            return out.reshape(n, FEAT) + bias
        h = _gatv2(x, edge_index, edge_attr, W_l, b_l, W_r, b_r, W_e, att, bias)
        h = jax.nn.silu(h)
        return x + h
    edge_index = jnp.stack([src, dst])
    deg = jnp.maximum(jax.ops.segment_sum(jnp.ones(dst.shape, jnp.float32), dst, num_segments=3125), 1.0)
    deg_isqrt = deg ** (-0.5)
    h = jnp.maximum(_layernorm(x, axis=-1), 0.0)
    x = x + _L0_gnn_ref(h, node_vec1, deg_isqrt[:, None], src, dst, L0_gnn_W, L0_gnn_attn_l, L0_gnn_attn_r, L0_gnn_bias)
    h = jnp.maximum(_layernorm(x, axis=-1), 0.0)
    x = x + _L1_gnn_ref(h, edge_index, L1_gnn_weight, L1_gnn_bias, L1_gnn_gamma, L1_gnn_beta, L1_gnn_running_mean, L1_gnn_running_var)
    h = jnp.maximum(_layernorm(x, axis=-1), 0.0)
    x = x + _L2_gnn_ref(h, edge_index, L2_gnn_weight, L2_gnn_attn_l, L2_gnn_attn_r)
    h = jnp.maximum(_layernorm(x, axis=-1), 0.0)
    x = x + _L3_gnn_ref(h, edge_index, edge_attr_16, L3_gnn_W_l, L3_gnn_b_l, L3_gnn_W_r, L3_gnn_b_r, L3_gnn_W_e, L3_gnn_att, L3_gnn_bias)
    return x

_drawn_inputs = setup_inputs


def setup_inputs(seed=0):
    import zlib

    import numpy as np

    out = dict(_drawn_inputs(seed))
    spreads = {'L1_gnn_gamma': (1.0, 0.2),
     'L1_gnn_beta': (0.0, 0.1),
     'L1_gnn_running_mean': (0.0, 0.1),
     'L1_gnn_running_var': (1.0, 0.6),
     'L3_gnn_b_l': (0.0, 0.332),
     'L3_gnn_b_r': (0.0, 2.0),
     'L3_gnn_bias': (0.0, 0.331)}
    factors = {'edge_attr_16': 8.0,
     'node_vec1': 8.0,
     'L0_gnn_W': 7.782,
     'L0_gnn_attn_l': 8.0,
     'L0_gnn_attn_r': 8.0,
     'L0_gnn_bias': 32.913,
     'L1_gnn_bias': 5.911,
     'L3_gnn_W_r': 8.0,
     'L3_gnn_W_e': 8.0,
     'L3_gnn_att': 8.0}
    for name, (base, spread) in spreads.items():
        noise = np.random.default_rng([zlib.crc32(name.encode()), seed]).standard_normal(out[name].shape)
        drawn = base * np.exp(spread * noise) if base else spread * noise
        out[name] = jnp.asarray(drawn.astype(out[name].dtype))
    for name, factor in factors.items():
        out[name] = (out[name] * factor).astype(out[name].dtype)
    return out
```

```python
from contextlib import ExitStack

import concourse.bass as bass
from concourse import mybir

F32 = mybir.dt.float32
BF16 = mybir.dt.bfloat16
I32 = mybir.dt.int32
ALU = mybir.AluOpType
ACT = mybir.ActivationFunctionType
X_AXIS = mybir.AxisListType.X

P = 128
NODES = 3125
EDGES = 53125
FEAT = 256
CHUNKS = FEAT // P
HEADS = 4
HEAD_DIM = FEAT // HEADS
EDGE_DIM = 16
NODE_TILES = -(-NODES // P)
LAST_ROWS = NODES - (NODE_TILES - 1) * P
EDGE_TILES = -(-EDGES // P)
ITEMS = EDGE_TILES + NODE_TILES - 1
BLOCKS = 4
IPB = ITEMS // BLOCKS
BIG = 1.0e30
LN_EPS = 1e-5
BN_EPS = 1e-5
GCN_COLS = FEAT + EDGE_DIM
L2_COLS = FEAT + 2 * HEADS
L3_COLS = FEAT + HEADS
OUT_COLS = FEAT + 2 * HEADS
NEG_GAT, NEG_L2 = 0.2, 0.01
PAIRS = P // EDGE_DIM
ATTR_COLS = EDGE_TILES * EDGE_DIM

assert IPB * BLOCKS == ITEMS and IPB <= P


def flat(ap):
    return ap.rearrange("p a b -> p (a b)")


def tile_loop(eng, count, unroll, body, first=0):
    main = count // unroll
    with eng.Fori(0, main) as i:
        for u in range(unroll):
            body(i * unroll + (first + u), (first + u) % unroll, i + (first + u) // unroll)
    for t in range(first + main * unroll, first + count):
        body(t, t % unroll, t // unroll)


def build(nc, io, out):
    ctx = ExitStack()

    def sb(name, shape, dt=F32):
        return ctx.enter_context(nc.sbuf_tensor(name, shape, dt))

    stage_sems = []

    def sem(name, kept=False):
        s = nc.alloc_semaphore(name=name)
        if not kept:
            stage_sems.append(s)
        return s

    def clear_sems():
        cleared = list(stage_sems)
        stage_sems.clear()
        for s in cleared:
            nc.sync.sem_clear(s)
        return cleared

    def free_sems(cleared):
        for s in cleared:
            nc.release_semaphore(s)

    def dram(name, shape, dt=F32):
        return nc.dram_tensor(name, shape, dt, kind="Internal").ap()

    class Chain:

        def __init__(self, eng, name):
            self.eng, self.sem, self.n = eng, sem(name), 0

        def mark(self, ins):
            self.n += 1
            ins.then_inc(self.sem, 1)

        def link(self, ins):
            self.mark(ins)
            self.eng.wait_ge(self.sem, self.n)

    idle = {e: sem(f"idle_{e}", kept=True) for e in ("act", "pool", "pe", "dve")}

    def hold(eng, who, s, value):
        eng.wait_ge(s, value)
        eng.sem_inc(idle[who], 1)

    with ctx:
        bank = [ctx.enter_context(nc.psum_tensor(f"bank{i}", [P, 512], F32)) for i in range(8)]
        x = sb("x", [P, NODE_TILES, FEAT])
        h = sb("h", [P, NODE_TILES, FEAT])
        acc = sb("acc", [P, NODE_TILES, GCN_COLS])
        xr_parts = sb("xr_parts", [P, NODE_TILES, 3, L3_COLS], BF16)
        ident = sb("ident", [P, P])
        ones = sb("ones", [P, P])
        p_index = sb("p_index", [P, 1])
        iota_b = sb("iota_b", [P, P], BF16)
        iota_t = sb("iota_t", [P, NODE_TILES])
        dst_col = sb("dst_col", [P, ITEMS])
        on_col = sb("on_col", [P, ITEMS])
        last_col = sb("last_col", [P, ITEMS])
        hi_col = sb("hi_col", [P, ITEMS])
        tile_col = sb("tile_col", [P, ITEMS])
        src_idx = sb("src_idx", [P, ITEMS], I32)
        item_tile = sb("item_tile", [1, ITEMS], I32)
        off_col = sb("off_col", [P, ITEMS])
        starts = sb("starts", [IPB, BLOCKS, P])
        keeps = sb("keeps", [IPB, BLOCKS, P])
        lasts = sb("lasts", [IPB, BLOCKS, P])
        starts_row = sb("starts_row", [1, ITEMS])
        keeps_row = sb("keeps_row", [1, ITEMS])
        tile_onehot = sb("tile_onehot", [IPB, BLOCKS, NODE_TILES])
        item_vals = sb("item_vals", [P, 2, ITEMS * HEADS])
        logits = item_vals[:, 0, :].rearrange("p (w h) -> p w h", h=HEADS)
        maxima = item_vals[:, 1, :].rearrange("p (w h) -> p w h", h=HEADS)
        sums_rhs = sb("sums_rhs", [P, ITEMS, 2 * HEADS])
        idx_ring = sb("idx_ring", [P, 2, 8], I32)
        stat = sb("stat", [P, NODE_TILES, 6])
        mean = sb("mean", [P, NODE_TILES])
        rstd = sb("rstd", [P, NODE_TILES])
        shift = sb("shift", [P, NODE_TILES])
        small = [sb(f"small{i}", [P, NODE_TILES]) for i in range(4)]
        eps_col = sb("eps_col", [P, 1])
        dinv = sb("dinv", [P, NODE_TILES])
        g_ring = sb("g_ring", [P, 8, GCN_COLS])
        rings = flat(g_ring[:])
        h_ring = rings[:, 0:2 * FEAT].rearrange("p (s f) -> p s f", s=2)
        ht_ring = rings[:, 512:1024].rearrange("p (s k n) -> p s k n", s=2, k=CHUNKS)
        wbuf = sb("wbuf", [P, CHUNKS, 2 * L3_COLS])
        row_ring = rings[:, 1024:1024 + 2 * L2_COLS].rearrange("p (s f) -> p s f", s=2)
        spare = xr_parts[:].rearrange("p t k f -> p (t k f)")[:, 0:4 * 4096].bitcast(F32)
        work = [spare[:, i * 2048:(i + 1) * 2048] for i in range(4)] + [flat(h[:])[:, 0:2048]]

        item_tile_d = dram("item_tile_d", [ITEMS])
        edge_tile_d = dram("edge_tile_d", [ITEMS], I32)
        dst_rows_d = dram("dst_rows_d", [ITEMS * P], BF16)
        src_rows_d = dram("src_rows_d", [ITEMS * P], BF16)
        edge_attr_d = dram("edge_attr_d", [ITEMS * P, EDGE_DIM])
        attr_parts_d = dram("attr_parts_d", [PAIRS, P, ATTR_COLS], BF16)
        gcn_table = dram("gcn_table", [NODE_TILES * P, FEAT])
        l2_table = dram("l2_table", [NODE_TILES * P, L2_COLS])
        l3_table = dram("l3_table", [NODE_TILES * P, L3_COLS])

        loads = sem("loads", kept=True)
        dst_loaded = sem("dst_loaded")
        consts_i = sem("consts_i")
        pool_chain_s = sem("pool_chain")
        counts_ready = sem("counts_ready")
        sums_ready = sem("sums_ready")
        tile_ready = sem("tile_ready")
        tile_stored = sem("tile_stored")
        group_ready = sem("group_ready")
        lists_in = [sem(f"lists_in{b}", kept=True) for b in range(BLOCKS)]
        attrs_in = [sem(f"attrs_in{b}", kept=True) for b in range(BLOCKS)]
        attrs_out = [sem(f"attrs_out{b}", kept=True) for b in range(BLOCKS)]
        rows_ready = sem("rows_ready")
        rows_stored = sem("rows_stored")
        cols_ready = sem("cols_ready")
        cols_used = sem("cols_used")
        tile_back = sem("tile_back")
        edge_tile_stored = sem("edge_tile_stored")
        conv_done = sem("conv_done")

        dst_all_i = work[0][:, 0:EDGE_TILES].bitcast(I32)
        dst_all = work[0][:, 512:512 + EDGE_TILES]
        counted = work[0][:, 1024:1024 + EDGE_TILES]
        iota_i = sb("iota_i", [P, P], I32)
        items_i = sb("items_i", [IPB, BLOCKS], I32)
        items_f = sb("items_f", [IPB, BLOCKS])
        pidx_i = sb("pidx_i", [P, 1], I32)
        below = sb("below", [P, NODE_TILES])
        below_i = sb("below_i", [P, NODE_TILES], I32)
        passed = work[1][0:IPB, 0:BLOCKS * NODE_TILES].rearrange("p (b t) -> p b t", b=BLOCKS)
        tile_of = sb("tile_of", [IPB, BLOCKS])
        base_of = sb("base_of", [IPB, BLOCKS])
        group_i = sb("group_i", [IPB, BLOCKS], I32)
        lists = flat(h[:])[0:IPB, 2048:6400]
        dst_ext_i = lists[:, 0:520].bitcast(I32).rearrange("p (b e) -> p b e", b=BLOCKS)
        dst_ext = lists[:, 520:1040].rearrange("p (b e) -> p b e", b=BLOCKS)
        src_i = lists[:, 1040:1552].bitcast(I32).rearrange("p (b e) -> p b e", b=BLOCKS)
        lo_i = work[1][0:IPB, 512:1024].bitcast(I32).rearrange("p (b e) -> p b e", b=BLOCKS)
        hi_i = work[1][0:IPB, 1024:1536].bitcast(I32).rearrange("p (b e) -> p b e", b=BLOCKS)
        src_f = work[2][0:IPB, 0:512].rearrange("p (b e) -> p b e", b=BLOCKS)
        hi_f = work[2][0:IPB, 512:1024].rearrange("p (b e) -> p b e", b=BLOCKS)
        loc = work[2][0:IPB, 1024:1536].rearrange("p (b e) -> p b e", b=BLOCKS)
        on = work[2][0:IPB, 1536:2048].rearrange("p (b e) -> p b e", b=BLOCKS)
        tmp = work[1][0:IPB, 1536:2048].rearrange("p (b e) -> p b e", b=BLOCKS)
        lo_b = lists[:, 1600:1856].bitcast(BF16).rearrange("p (b e) -> p b e", b=BLOCKS)
        loc_b = lists[:, 1856:2112].bitcast(BF16).rearrange("p (b e) -> p b e", b=BLOCKS)
        attr_stage = [work[3][0:IPB, :], work[4][0:IPB, :]]
        item_least = sb("item_least", [IPB, 2, BLOCKS])

        with nc.Block() as block:
            @block.sync
            def _(sp):
                sp.dma_start(dst_all_i, io["dst_all"]).then_inc(dst_loaded, 16)
                for t in range(5):
                    n = NODE_TILES // 5
                    if t < 4:
                        sp.dma_start(x[:, t * n:(t + 1) * n, :],
                                     io["x"][t * n * P:(t + 1) * n * P, :].rearrange("(t p) f -> p t f", p=P)
                                     ).then_inc(loads, 16)
                sp.dma_start(x[:, 20:24, :],
                             io["x"][20 * P:24 * P, :].rearrange("(t p) f -> p t f", p=P)).then_inc(loads, 16)
                sp.wait_ge(conv_done, 1)
                sp.dma_start(x[0:LAST_ROWS, NODE_TILES - 1, :], io["x"][(NODE_TILES - 1) * P:NODES, :]
                             ).then_inc(loads, 16)
                sp.wait_ge(tile_ready, 1)
                with nc.allow_non_contiguous_dma(reason="440 numbers, once"):
                    sp.dma_start(item_tile_d.rearrange("(b p) -> p b", b=BLOCKS), tile_of[:]).then_inc(tile_stored, 16)
                sp.wait_ge(tile_stored, 16)
                sp.dma_start(tile_col[:], item_tile_d.unsqueeze(0).broadcast_to([P, ITEMS])).then_inc(tile_back, 16)
                sp.wait_ge(group_ready, 1)
                with nc.allow_non_contiguous_dma(reason="440 numbers, once"):
                    sp.dma_start(edge_tile_d.rearrange("(b p) -> p b", b=BLOCKS), group_i[:]).then_inc(edge_tile_stored, 16)
                sp.wait_ge(edge_tile_stored, 16)
                for b in range(BLOCKS):
                    sp.wait_ge(attrs_in[b], 16)
                    sp.dma_start(edge_attr_d[b * IPB * P:(b + 1) * IPB * P, :].rearrange("(p e) f -> p (e f)", e=P),
                                 attr_stage[b % 2]).then_inc(attrs_out[b], 16)
                sp.wait_ge(rows_ready, 2)
                for d, s in ((dst_rows_d, loc_b), (src_rows_d, lo_b)):
                    sp.dma_start(d.rearrange("(b p e) -> p b e", b=BLOCKS, e=P), s).then_inc(rows_stored, 16)
                sp.wait_ge(rows_stored, 32)
                for b in range(BLOCKS):
                    sp.wait_ge(attrs_out[b], 16)
                sp.wait_ge(loads, 16 * 6)

            @block.gpsimd
            def _(pool):
                pool.iota(iota_i[:], [[1, P]], base=0, channel_multiplier=0).then_inc(consts_i, 1)
                pool.iota(pidx_i[:], [[0, 1]], base=0, channel_multiplier=1).then_inc(consts_i, 1)
                pool.iota(items_i[:], [[IPB, BLOCKS]], base=0, channel_multiplier=1).then_inc(consts_i, 1)
                pool.memset(ident[:], 0.0).then_inc(pool_chain_s, 1)
                pool.wait_ge(pool_chain_s, 1)
                pool.affine_select(out=ident[:], in_=ident[:], compare_op=ALU.not_equal, fill=1.0, base=0,
                                   pattern=[[-1, P]], channel_multiplier=1).then_inc(consts_i, 1)
                pool.wait_ge(group_ready, 1)
                for b in range(BLOCKS):
                    rows = bass.IndirectOffsetOnAxis(ap=group_i[:, b:b + 1], axis=0)
                    pool.indirect_dma_start(dst_ext_i[:, b, :], None, io["dst_ext"], rows).then_inc(lists_in[b], 16)
                    pool.indirect_dma_start(src_i[:, b, :], None, io["src_tiles"], rows).then_inc(lists_in[b], 16)
                for b in range(BLOCKS):
                    rows = bass.IndirectOffsetOnAxis(ap=group_i[:, b:b + 1], axis=0)
                    if b >= 2:
                        pool.wait_ge(attrs_out[b - 2], 16)
                    pool.indirect_dma_start(attr_stage[b % 2], None, io["edge_attr"], rows).then_inc(attrs_in[b], 16)

            @block.vector
            def _(dve):
                c = Chain(dve, "stage1_dve")
                c.mark(dve.memset(ones[:], 1.0))
                c.mark(dve.memset(eps_col[:], LN_EPS))
                dve.memset(x[:, NODE_TILES - 1, :], 0.0).then_inc(conv_done, 1)
                dve.wait_ge(consts_i, 4)
                c.mark(dve.tensor_copy(iota_b[:], iota_i[:]))
                c.mark(dve.tensor_copy(iota_t[:], iota_i[:, 0:NODE_TILES]))
                c.mark(dve.tensor_copy(p_index[:], pidx_i[:]))
                c.mark(dve.tensor_copy(items_f[:], items_i[:]))
                dve.wait_ge(dst_loaded, 16)
                c.link(dve.tensor_copy(dst_all, dst_all_i))
                for t in range(1, NODE_TILES):
                    c.link(dve.tensor_scalar(counted, dst_all, float(t * P), 0.0, ALU.is_lt, ALU.add,
                                             accum_out=below[:, t - 1:t]))
                dve.sem_inc(counts_ready, 1)
                dve.wait_ge(sums_ready, 1)
                last = NODE_TILES - 1
                c.link(dve.tensor_scalar(below_i[:, 0:last], bank[0][:, 0:last], float(P - 1), None, ALU.add))
                c.link(dve.tensor_scalar(below_i[:, 0:last], below_i[:, 0:last], 7, None, ALU.arith_shift_right))
                c.link(dve.tensor_copy(below[:, 0:last], below_i[:, 0:last]))
                c.link(dve.tensor_scalar(below[:, 0:last], below[:, 0:last], -1.0, 0.0, ALU.add, ALU.max))
                c.link(dve.tensor_tensor(below[:, 0:last], below[:, 0:last], iota_t[:, 0:last], ALU.add))
                c.link(dve.tensor_tensor(passed[:, :, 0:last], items_f[:].unsqueeze(2).broadcast_to([IPB, BLOCKS, last]),
                                         below[0:IPB, 0:last].unsqueeze(1).broadcast_to([IPB, BLOCKS, last]), ALU.is_gt))
                c.link(dve.tensor_reduce(tile_of[:], passed[:, :, 0:last], X_AXIS, ALU.add))
                dve.sem_inc(tile_ready, 1)
                c.link(dve.tensor_tensor(group_i[:], items_f[:], tile_of[:], ALU.subtract))
                dve.sem_inc(group_ready, 1)
                c.mark(dve.tensor_tensor(tile_onehot[:], tile_of[:].unsqueeze(2).broadcast_to([IPB, BLOCKS, NODE_TILES]),
                                         iota_t[0:IPB, :].unsqueeze(1).broadcast_to([IPB, BLOCKS, NODE_TILES]), ALU.is_equal))
                c.link(dve.tensor_scalar(base_of[:], tile_of[:], float(P), None, ALU.mult))
                for b in range(BLOCKS):
                    dve.wait_ge(lists_in[b], 32)
                c.link(dve.tensor_copy(dst_ext, dst_ext_i))
                cur = dst_ext[:, :, 1:P + 1]
                c.mark(dve.tensor_copy(src_f, src_i))
                c.mark(dve.tensor_scalar(lo_i, src_i, P - 1, None, ALU.bitwise_and))
                c.mark(dve.tensor_scalar(hi_i, src_i, 7, None, ALU.arith_shift_right))
                c.link(dve.tensor_tensor(loc, cur, base_of[:].unsqueeze(2).broadcast_to([IPB, BLOCKS, P]), ALU.subtract))
                dve.tensor_copy(lo_b, lo_i).then_inc(rows_ready, 1)
                c.mark(dve.tensor_copy(hi_f, hi_i))
                c.link(dve.tensor_scalar(tmp, loc, 0.0, None, ALU.is_ge))
                c.link(dve.scalar_tensor_tensor(out=on, in0=loc, scalar=float(P), in1=tmp, op0=ALU.is_lt, op1=ALU.mult))
                c.link(dve.scalar_tensor_tensor(out=loc, in0=loc, scalar=1.0, in1=on, op0=ALU.add, op1=ALU.mult))
                c.link(dve.tensor_scalar(loc, loc, -1.0, None, ALU.add))
                dve.tensor_copy(loc_b, loc).then_inc(rows_ready, 1)
                c.link(dve.tensor_tensor(tmp, cur, dst_ext[:, :, 0:P], ALU.not_equal))
                c.link(dve.scalar_tensor_tensor(out=starts[:], in0=tmp, scalar=-BIG, in1=on, op0=ALU.mult, op1=ALU.mult))
                c.link(dve.tensor_tensor(tmp, cur, dst_ext[:, :, 2:P + 2], ALU.not_equal))
                c.link(dve.tensor_tensor(lasts[:], tmp, on, ALU.mult))
                c.link(dve.tensor_scalar(keeps[:], lasts[:], -1.0, 1.0, ALU.mult, ALU.add))
                c.mark(dve.tensor_reduce(item_least[:, 0, :], starts[:], X_AXIS, ALU.min))
                c.link(dve.tensor_reduce(item_least[:, 1, :], keeps[:], X_AXIS, ALU.min))
                dve.sem_inc(cols_ready, 1)
                for n, table in enumerate((dst_col, on_col, last_col, src_idx, hi_col)):
                    dve.wait_ge(cols_used, n + 1)
                    c.mark(dve.tensor_copy(table[:], bank[1 + n][:, 0:ITEMS]))
                dve.wait_ge(cols_used, 6)
                c.mark(dve.tensor_copy(starts_row[:], bank[6][0:1, 0:ITEMS]))
                c.mark(dve.tensor_copy(keeps_row[:], bank[7][0:1, 0:ITEMS]))
                dve.wait_ge(c.sem, c.n)
                c.mark(dve.tensor_scalar(off_col[:], on_col[:], BIG, -BIG, ALU.mult, ALU.add))
                dve.wait_ge(tile_back, 16)
                c.link(dve.tensor_copy(item_tile[:], tile_col[0:1, :]))

            @block.tensor
            def _(pe):
                pe.wait_ge(counts_ready, 1)
                pe.matmul(bank[0][:, 0:NODE_TILES - 1], ones[:], below[:, 0:NODE_TILES - 1], start=True, stop=True
                          ).then_inc(sums_ready, 1)
                pe.wait_ge(cols_ready, 1)
                for n, rows in enumerate((loc, on, lasts[:], src_f, hi_f)):
                    for b in range(BLOCKS):
                        ins = pe.transpose(bank[1 + n][:, b * IPB:(b + 1) * IPB], rows[:, b, :], ident[0:IPB, 0:IPB])
                    ins.then_inc(cols_used, 1)
                for n in range(2):
                    for b in range(BLOCKS):
                        ins = pe.transpose(bank[6 + n][0:1, b * IPB:(b + 1) * IPB], item_least[:, n, b:b + 1],
                                           ident[0:IPB, 0:IPB])
                ins.then_inc(cols_used, 1)

        class Norm:

            def __init__(self, layer):
                self.var_ready = sem(f"var_ready{layer}")
                self.std_ready = sem(f"std_ready{layer}")
                self.norm_ready = sem(f"norm_ready{layer}")
                self.rows_ready = sem(f"rows_ready{layer}")
                self.turned = sem(f"turned{layer}")
                self.turn_free = sem(f"turn_free{layer}")
                self.cols_ready = sem(f"cols_ready{layer}")
                self.projected = sem(f"projected{layer}")
                self.out_free = sem(f"out_free{layer}")

        def norm_statistics(dve, c, s):
            stat_done = c.sem
            before = c.n

            def one(t, slot, rnd):
                dve.bn_stats(stat[:, bass.ds(t, 1), :].rearrange("p a k -> p (a k)"),
                             x[:, bass.ds(t, 1), :].rearrange("p a f -> p (a f)")).then_inc(stat_done, 1)
            tile_loop(dve, NODE_TILES, 5, one)
            c.n = before + NODE_TILES
            dve.wait_ge(stat_done, c.n)
            even, odd = 1, 4
            c.mark(dve.tensor_tensor(mean[:], stat[:, :, even], stat[:, :, odd], ALU.add))
            c.mark(dve.tensor_tensor(small[1][:], stat[:, :, even + 1], stat[:, :, odd + 1], ALU.add))
            c.link(dve.tensor_tensor(small[0][:], stat[:, :, even], stat[:, :, odd], ALU.subtract))
            c.link(dve.tensor_tensor(small[0][:], small[0][:], small[0][:], ALU.mult))
            dve.scalar_tensor_tensor(out=small[1][:], in0=small[0][:], scalar=FEAT / 4, in1=small[1][:],
                                     op0=ALU.mult, op1=ALU.add).then_inc(s.var_ready, 1)
            dve.wait_ge(s.std_ready, 1)
            c.link(dve.reciprocal(rstd[:], small[2][:]))
            dve.scalar_tensor_tensor(out=shift[:], in0=mean[:], scalar=-0.5, in1=rstd[:],
                                     op0=ALU.mult, op1=ALU.mult).then_inc(s.norm_ready, 1)

        def norm_rows(act, s, keep=None):
            act.wait_ge(s.var_ready, 1)
            act.activation(small[2][:], small[1][:], ACT.Sqrt, bias=eps_col[:], scale=1.0 / FEAT).then_inc(s.std_ready, 1)
            act.wait_ge(s.norm_ready, 1)

            def one(t, slot, rnd):
                tile_x = x[:, bass.ds(t, 1), :].rearrange("p a f -> p (a f)")
                kw = dict(bias=shift[:, bass.ds(t, 1)], scale=rstd[:, bass.ds(t, 1)])
                if keep is not None:
                    act.activation(keep[:, bass.ds(t, 1), :].rearrange("p a f -> p (a f)"), tile_x, ACT.Relu, **kw)
                if not (isinstance(t, int) and t < 2):
                    hold(act, "act", s.turned, t - 1)
                act.activation(h_ring[:, slot, :], tile_x, ACT.Relu, **kw).then_inc(s.rows_ready, 1)
            one(0, 0, 0)
            one(1, 1, 0)
            tile_loop(act, NODE_TILES - 2, 2, one, first=2)

        def project(pe, s, groups, bias=None):
            def turn(t, slot, rnd):
                pe.wait_ge(s.rows_ready, t + 1)
                pe.wait_ge(s.turn_free, t + 1)
                for k in range(CHUNKS):
                    ins = pe.transpose(bank[slot][:, k * P:(k + 1) * P], h_ring[:, slot, k * P:(k + 1) * P], ident[:])
                ins.then_inc(s.turned, 1)

            def multiply(t, slot, rnd):
                pe.wait_ge(s.cols_ready, t + 1)
                pe.wait_ge(s.out_free, t + 1)
                for b, lo, hi in groups:
                    for k in range(CHUNKS):
                        ins = pe.matmul(bank[2 + slot * len(groups) + b][:, 0:hi - lo], ht_ring[:, slot, k, :],
                                        wbuf[:, k, lo:hi], start=(k == 0), stop=(k == CHUNKS - 1 and bias is None))
                    if bias is not None:
                        ins = pe.matmul(bank[2 + slot * len(groups) + b][:, 0:hi - lo], ones[0:1, :],
                                        bias[0:1, lo:hi], start=False, stop=True)
                ins.then_inc(s.projected, 1)

            def both(t, slot, rnd):
                turn(t, slot, rnd)
                multiply(t - 1, 1 - slot, rnd)
            turn(0, 0, 0)
            tile_loop(pe, NODE_TILES - 1, 2, both, first=1)
            multiply(NODE_TILES - 1, (NODE_TILES - 1) % 2, 0)

        def read_out(dve, s, copy_cols, finish):
            dve.sem_inc(s.turn_free, 2)
            dve.sem_inc(s.out_free, 2)

            def cols(t, slot, rnd):
                dve.wait_ge(s.turned, t + 1)
                if not (isinstance(t, int) and t < 2):
                    dve.wait_ge(s.projected, t - 1)
                copy_cols(slot).then_inc(s.cols_ready, 1)
                dve.wait_ge(s.cols_ready, t + 1)
                dve.sem_inc(s.turn_free, 1)

            def both(t, slot, rnd):
                cols(t, slot, rnd)
                dve.wait_ge(s.projected, t)
                finish(t - 1, 1 - slot, rnd - 1 + slot)
            cols(0, 0, 0)
            both(1, 1, 0)
            tile_loop(dve, NODE_TILES - 2, 2, both, first=2)
            dve.wait_ge(s.projected, NODE_TILES)
            finish(NODE_TILES - 1, (NODE_TILES - 1) % 2, (NODE_TILES - 1) // 2)

        def plain_cols(dve):
            return lambda slot: dve.tensor_copy(flat(ht_ring[:, slot, :, :]), bank[slot][:, 0:FEAT])

        run_max = work[0][0:IPB, :].rearrange("p (g e) -> p g e", e=P)
        seg_max = work[1][0:IPB, :].rearrange("p (g e) -> p g e", e=P)
        lasts_max = work[2][0:IPB, :].rearrange("p (g e) -> p g e", e=P)
        ends = work[3][0:IPB, 0:16]
        carries = work[3][0:IPB, 16:32]
        states = work[3][0:1, 32:32 + HEADS * (ITEMS + 1)].rearrange("p (h w) -> p h w", h=HEADS)

        class Segments:
            def __init__(self, name):
                self.rows = sem(f"seg_rows_{name}")
                self.ends = sem(f"seg_ends_{name}")
                self.turned = sem(f"seg_turned_{name}")
                self.states = sem(f"seg_states_{name}")
                self.carried = sem(f"seg_carried_{name}")
                self.found = sem(f"seg_found_{name}")
                self.cols = sem(f"seg_cols_{name}")

        def segment_max_pe(pe, s, values, heads, ready):
            pe.wait_ge(ready, 1)
            for hd in range(heads):
                for b in range(BLOCKS):
                    ins = pe.transpose(bank[hd][0:IPB, b * P:(b + 1) * P], values[:, b * IPB:(b + 1) * IPB, hd], ident[:])
                ins.then_inc(s.rows, 1)
            for way in range(2):
                pe.wait_ge(s.ends, way + 1)
                for hd in range(heads):
                    for b in range(BLOCKS):
                        g = hd * BLOCKS + b
                        ins = pe.transpose(bank[4 + hd][0:1, b * IPB:(b + 1) * IPB], ends[:, g:g + 1], ident[0:IPB, 0:IPB])
                ins.then_inc(s.turned, 1)
                pe.wait_ge(s.states, way + 1)
                for hd in range(heads):
                    for b in range(BLOCKS):
                        g = hd * BLOCKS + b
                        at = b * IPB + way
                        ins = pe.transpose(bank[4][0:IPB, g:g + 1], states[:, hd, at:at + IPB], ident[0:1, 0:1])
                ins.then_inc(s.carried, 1)
            pe.wait_ge(s.found, 1)
            for hd in range(heads):
                for b in range(BLOCKS):
                    ins = pe.transpose(bank[hd][:, b * IPB:(b + 1) * IPB], seg_max[:, hd * BLOCKS + b, :],
                                       ident[0:IPB, 0:IPB])
                ins.then_inc(s.cols, 1)

        def segment_max_dve(dve, c, s, result, heads):
            groups = [(hd, b) for hd in range(heads) for b in range(BLOCKS)]
            n = len(groups)

            def forward(initial):
                for g, (hd, b) in enumerate(groups):
                    c.mark(dve.tensor_tensor_scan(run_max[:, g, :], starts[:, b, :], bank[hd][0:IPB, b * P:(b + 1) * P],
                                                  initial(g), ALU.add, ALU.max))
                dve.wait_ge(c.sem, c.n)

            def backward(initial):
                for g, (hd, b) in enumerate(groups):
                    c.mark(dve.tensor_tensor_scan(seg_max[:, g, ::-1], keeps[:, b, ::-1], lasts_max[:, g, ::-1],
                                                  initial(g), ALU.mult, ALU.add))
                dve.wait_ge(c.sem, c.n)

            dve.wait_ge(s.rows, heads)
            forward(lambda g: -BIG)
            dve.tensor_copy(ends[:, 0:n], run_max[:, 0:n, P - 1]).then_inc(s.ends, 1)
            c.link(dve.memset(states[:, 0:heads, 0:1], -BIG))
            dve.wait_ge(s.turned, 1)
            for hd in range(heads):
                c.mark(dve.tensor_tensor_scan(states[:, hd, 1:ITEMS + 1], starts_row[:], bank[4 + hd][0:1, 0:ITEMS],
                                              -BIG, ALU.add, ALU.max))
            dve.wait_ge(c.sem, c.n)
            dve.sem_inc(s.states, 1)
            dve.wait_ge(s.carried, 1)
            c.link(dve.tensor_copy(carries[:, 0:n], bank[4][0:IPB, 0:n]))
            forward(lambda g: carries[:, g:g + 1])
            for hd in range(heads):
                c.mark(dve.tensor_tensor(lasts_max[:, hd * BLOCKS:(hd + 1) * BLOCKS, :], lasts[:],
                                         run_max[:, hd * BLOCKS:(hd + 1) * BLOCKS, :], ALU.mult))
            dve.wait_ge(c.sem, c.n)
            backward(lambda g: 0.0)
            dve.tensor_copy(ends[:, 0:n], seg_max[:, 0:n, 0]).then_inc(s.ends, 1)
            c.link(dve.memset(states[:, 0:heads, ITEMS:ITEMS + 1], 0.0))
            dve.wait_ge(s.turned, 2)
            for hd in range(heads):
                c.mark(dve.tensor_tensor_scan(states[:, hd, 0:ITEMS][:, ::-1], keeps_row[:, ::-1],
                                              bank[4 + hd][0:1, 0:ITEMS][:, ::-1], 0.0, ALU.mult, ALU.add))
            dve.wait_ge(c.sem, c.n)
            dve.sem_inc(s.states, 1)
            dve.wait_ge(s.carried, 2)
            c.link(dve.tensor_copy(carries[:, 0:n], bank[4][0:IPB, 0:n]))
            backward(lambda g: carries[:, g:g + 1])
            dve.sem_inc(s.found, 1)
            for hd in range(heads):
                dve.wait_ge(s.cols, hd + 1)
                c.mark(dve.tensor_copy(result[:, :, hd], bank[hd][:, 0:ITEMS]))
            dve.wait_ge(c.sem, c.n)

        s0 = Norm(0)
        l0_loads = sem("l0_loads")
        attn = sb("attn", [P, 6])
        gate = sb("gate", [P, NODE_TILES])
        z = sb("z", [P, NODE_TILES, 2])
        node_vals = sb("node_vals", [P, 4, NODE_TILES])
        node_rest = sb("node_rest", [P, 2, 4 * NODE_TILES])
        node_parts = sb("node_parts", [P, 3, 4 * NODE_TILES], BF16)

        with nc.Block() as block:
            @block.sync
            def _(sp):
                sp.dma_start(wbuf[:, :, 0:2], io["l0_w"]).then_inc(l0_loads, 16)
                sp.dma_start(attn[:], io["l0_attn"].broadcast_to([P, 6])).then_inc(l0_loads, 16)
                sp.dma_start(gate[:], io["gate"]).then_inc(l0_loads, 16)
                sp.wait_ge(l0_loads, 48)

            @block.scalar
            def _(act):
                norm_rows(act, s0, keep=h)

            @block.tensor
            def _(pe):
                pe.wait_ge(l0_loads, 48)
                project(pe, s0, [(0, 0, 2)])

            @block.vector
            def _(dve):
                c = Chain(dve, "stage2_dve")
                norm_statistics(dve, c, s0)

                def keep_z(t, slot, rnd):
                    dve.tensor_copy(z[:, bass.ds(t, 1), :].rearrange("p a k -> p (a k)"), bank[2 + slot][:, 0:2]
                                    ).then_inc(s0.out_free, 1)
                read_out(dve, s0, plain_cols(dve), keep_z)
                dve.wait_ge(s0.out_free, 2 + NODE_TILES)
                dve.wait_ge(l0_loads, 48)
                for k in range(2):
                    c.mark(dve.tensor_copy(node_vals[:, 1 + k, :], z[:, :, k]))
                for row, at in ((0, 0), (3, 2)):
                    c.link(dve.tensor_scalar(node_vals[:, row, :], z[:, :, 0], attn[:, at:at + 1], None, ALU.mult))
                    c.link(dve.scalar_tensor_tensor(out=node_vals[:, row, :], in0=z[:, :, 1], scalar=attn[:, at + 1:at + 2],
                                                    in1=node_vals[:, row, :], op0=ALU.mult, op1=ALU.add))
                whole = flat(node_vals[:])
                c.link(dve.tensor_copy(node_parts[:, 0, :], whole))
                c.link(dve.tensor_tensor(node_rest[:, 0, :], whole, node_parts[:, 0, :], ALU.subtract))
                c.link(dve.tensor_copy(node_parts[:, 1, :], node_rest[:, 0, :]))
                c.link(dve.tensor_tensor(node_rest[:, 1, :], node_rest[:, 0, :], node_parts[:, 1, :], ALU.subtract))
                c.link(dve.tensor_copy(node_parts[:, 2, :], node_rest[:, 1, :]))

        CHUNK = 4
        CHUNK_EDGES = CHUNK * P
        EDGE_CHUNKS = ITEMS // CHUNK
        VALS = 4 * NODE_TILES
        rows_ring = sb("rows_ring", [P, 2, 2, CHUNK_EDGES], BF16)
        place_ring = sb("place_ring", [P, 2, 2, CHUNK_EDGES], BF16)
        tile_mask = flat(acc[:])[:, 0:400].rearrange("p (s u k n) -> p s u k n", s=2, u=CHUNK, k=2)
        picked = flat(acc[:])[:, 400:1200].rearrange("p (s u v n) -> p s u v n", s=2, u=CHUNK, v=4)
        edge_vals = maxima
        rows_in = [sem(f"rows_in{u}") for u in range(2)]
        rows_free = sem("rows_free")
        place_ready = sem("place_ready")
        vals_ready = sem("vals_ready")
        vals_free = sem("vals_free")
        masks_done = sem("masks_done")
        picks_done = sem("picks_done")
        reduced = sem("reduced")

        SPLIT = 512
        SPLITS = ATTR_COLS // SPLIT
        split_memory = flat(acc[:])[:, 1536:]
        attr_in = split_memory[:, 0:2 * SPLIT].rearrange("p (s c) -> p s c", s=2)
        attr_rest = split_memory[:, 1024:1024 + 4 * SPLIT].rearrange("p (s k c) -> p s k c", s=2, k=2)
        attr_parts = split_memory[:, 3072:3072 + 3 * SPLIT].bitcast(BF16).rearrange("p (s k c) -> p s k c", s=2, k=3)
        attr_loaded = [sem(f"attr_loaded{u}") for u in range(2)]
        part_ready = sem("part_ready")
        rest_made = sem("rest_made")
        parts_out = [sem(f"parts_out{u}") for u in range(2)]

        with nc.Block() as block:
            @block.scalar
            def _(act):
                def load_attrs(t, slot):
                    act.dma_start(attr_in[:, slot, :], io["attr_t"][:, bass.ds(t * SPLIT, SPLIT)]).then_inc(attr_loaded[slot], 16)

                def split(t, slot, rnd, more=True):
                    act.wait_ge(attr_loaded[slot], rnd * 16 + 16)
                    if not (isinstance(t, int) and t < 2):
                        act.wait_ge(parts_out[slot], rnd * 48)
                    act.copy(attr_parts[:, slot, 0, :], attr_in[:, slot, :]).then_inc(part_ready, 1)
                    for k in range(2):
                        act.wait_ge(rest_made, t * 2 + (k + 1))
                        act.copy(attr_parts[:, slot, k + 1, :], attr_rest[:, slot, k, :]).then_inc(part_ready, 1)
                    act.wait_ge(part_ready, t * 3 + 3)
                    for k, (lo, hi) in enumerate(((0, 3), (3, 6), (6, PAIRS))):
                        act.dma_start(attr_parts_d[lo:hi, :, bass.ds(t * SPLIT, SPLIT)].rearrange("b p c -> p b c"),
                                      attr_parts[:, slot, k:k + 1, :].broadcast_to([P, hi - lo, SPLIT])).then_inc(parts_out[slot], 16)
                    if more:
                        load_attrs(t + 2, slot)
                load_attrs(0, 0)
                load_attrs(1, 1)
                split(0, 0, 0)
                split(1, 1, 0)
                tile_loop(act, SPLITS - 5, 2, split, first=2)
                for t in range(SPLITS - 3, SPLITS):
                    split(t, t % 2, t // 2, more=t + 2 < SPLITS)
                for u in range(2):
                    act.wait_ge(parts_out[u], (SPLITS + 1 - u) // 2 * 48)

            @block.gpsimd
            def _(pool):
                def rest(t, slot, rnd):
                    for k in range(2):
                        pool.wait_ge(part_ready, t * 3 + (k + 1))
                        pool.tensor_tensor(attr_rest[:, slot, k, :], (attr_in[:, slot, :], attr_rest[:, slot, 0, :])[k],
                                           attr_parts[:, slot, k, :], ALU.subtract).then_inc(rest_made, 1)
                tile_loop(pool, SPLITS, 2, rest)

            @block.sync
            def _(sp):
                def load(t, slot, rnd):
                    sp.wait_ge(rows_free, t + 1)
                    for k, d in enumerate((src_rows_d, dst_rows_d)):
                        sp.dma_start(rows_ring[:, slot, k, :],
                                     d[bass.ds(t * CHUNK_EDGES, CHUNK_EDGES)].unsqueeze(0).broadcast_to([P, CHUNK_EDGES])
                                     ).then_inc(rows_in[slot], 16)
                tile_loop(sp, EDGE_CHUNKS, 2, load)

            @block.tensor
            def _(pe):
                def pick(t, slot, rnd):
                    pe.wait_ge(place_ready, t + 1)
                    pe.wait_ge(vals_free, t + 1)
                    for u in range(CHUNK):
                        for k, lo, hi in ((0, 0, 3 * NODE_TILES), (1, 3 * NODE_TILES, VALS)):
                            for part in range(3):
                                ins = pe.matmul(bank[slot][:, u * VALS + lo:u * VALS + hi],
                                                place_ring[:, slot, k, u * P:(u + 1) * P],
                                                node_parts[:, part, lo:hi], start=(part == 0), stop=(part == 2))
                    ins.then_inc(vals_ready, 1)
                tile_loop(pe, EDGE_CHUNKS, 2, pick)

            @block.vector
            def _(dve):
                dve.sem_inc(rows_free, 2)
                dve.sem_inc(vals_free, 2)

                def masks(t, slot, rnd):
                    dve.wait_ge(rows_in[slot], rnd * 32 + 32)
                    if not (isinstance(t, int) and t < 2):
                        dve.wait_ge(vals_ready, t - 1)
                    dve.tensor_scalar(place_ring[:, slot, :, :].rearrange("p k e -> p (k e)"),
                                      rows_ring[:, slot, :, :].rearrange("p k e -> p (k e)"),
                                      p_index[:], None, ALU.is_equal).then_inc(place_ready, 1)
                    for k, tiles_of in enumerate((hi_col, tile_col)):
                        dve.tensor_tensor(tile_mask[:, slot, :, k, :],
                                          tiles_of[:, bass.ds(t * CHUNK, CHUNK)].unsqueeze(2).broadcast_to([P, CHUNK, NODE_TILES]),
                                          iota_t[:].unsqueeze(1).broadcast_to([P, CHUNK, NODE_TILES]), ALU.is_equal
                                          ).then_inc(masks_done, 1)
                    dve.wait_ge(place_ready, t + 1)
                    dve.sem_inc(rows_free, 1)

                def gather(t, slot, rnd):
                    dve.wait_ge(vals_ready, t + 1)
                    dve.wait_ge(masks_done, t * 2 + 2)
                    got = bank[slot][:, 0:CHUNK * VALS].rearrange("p (u v n) -> p u v n", u=CHUNK, v=4)
                    dve.tensor_tensor(picked[:, slot, :, 0:3, :], got[:, :, 0:3, :],
                                      tile_mask[:, slot, :, 0:1, :].broadcast_to([P, CHUNK, 3, NODE_TILES]), ALU.mult
                                      ).then_inc(picks_done, 1)
                    dve.tensor_tensor(picked[:, slot, :, 3, :], got[:, :, 3, :], tile_mask[:, slot, :, 1, :], ALU.mult
                                      ).then_inc(picks_done, 1)
                    dve.wait_ge(picks_done, t * 2 + 2)
                    dve.sem_inc(vals_free, 1)
                    dve.tensor_reduce(edge_vals[:, bass.ds(t * CHUNK, CHUNK), :], picked[:, slot, :, :, :], X_AXIS, ALU.add
                                      ).then_inc(reduced, 1)

                def both(t, slot, rnd):
                    masks(t, slot, rnd)
                    if not (isinstance(t, int) and t < 3):
                        dve.wait_ge(reduced, t - 2)
                    gather(t - 1, 1 - slot, rnd)
                masks(0, 0, 0)
                both(1, 1, 0)
                both(2, 0, 1)
                tile_loop(dve, EDGE_CHUNKS - 3, 2, both, first=3)
                gather(EDGE_CHUNKS - 1, (EDGE_CHUNKS - 1) % 2, 0)

        seg0 = Segments("l0")
        sum_parts = flat(item_vals[:])[:, 0:ITEMS * 6].bitcast(BF16).rearrange("p (w k v) -> p w k v", k=3, v=4)
        sum_rests = [flat(acc[:])[:, k * ITEMS * 4:(k + 1) * ITEMS * 4].rearrange("p (w v) -> p w v", v=4) for k in range(2)]
        masked0 = sem("masked0")
        less0 = sem("less0")
        exp0 = sem("exp0")
        scores = logits[:, :, 0:1]
        top = logits[:, :, 1:2]

        with nc.Block() as block:
            @block.tensor
            def _(pe):
                segment_max_pe(pe, seg0, scores, 1, masked0)

            @block.scalar
            def _(act):
                act.wait_ge(less0, 1)
                act.activation(sums_rhs[:, :, 0], logits[:, :, 2], ACT.Exp).then_inc(exp0, 1)

            @block.vector
            def _(dve):
                c = Chain(dve, "stage4_dve")
                el, z0, z1, er = (edge_vals[:, :, k] for k in range(4))
                score = logits[:, :, 0]
                c.link(dve.tensor_tensor(score, el, er, ALU.add))
                c.link(dve.scalar_tensor_tensor(out=score, in0=score, scalar=NEG_GAT, in1=score, op0=ALU.mult, op1=ALU.max))
                c.link(dve.tensor_tensor(score, score, off_col[:], ALU.add))
                dve.sem_inc(masked0, 1)
                segment_max_dve(dve, c, seg0, top, 1)
                dve.tensor_tensor(logits[:, :, 2], score, logits[:, :, 1], ALU.subtract).then_inc(less0, 1)
                c.mark(dve.memset(sums_rhs[:, :, 3], 1.0))
                dve.wait_ge(exp0, 1)
                c.mark(dve.tensor_tensor(sums_rhs[:, :, 1], sums_rhs[:, :, 0], z0, ALU.mult))
                c.link(dve.tensor_tensor(sums_rhs[:, :, 2], sums_rhs[:, :, 0], z1, ALU.mult))
                c.link(dve.tensor_copy(sum_parts[:, :, 0, :], sums_rhs[:, :, 0:4]))
                c.link(dve.tensor_tensor(sum_rests[0], sums_rhs[:, :, 0:4], sum_parts[:, :, 0, :], ALU.subtract))
                c.link(dve.tensor_copy(sum_parts[:, :, 1, :], sum_rests[0]))
                c.link(dve.tensor_tensor(sum_rests[1], sum_rests[0], sum_parts[:, :, 1, :], ALU.subtract))
                c.link(dve.tensor_copy(sum_parts[:, :, 2, :], sum_rests[1]))

        onehot = sb("onehot", [P, 8, P])
        GROUP = 8
        onehot_b = flat(onehot[:]).bitcast(BF16).rearrange("p (u n) -> p u n", n=P)
        sums_by_part = spare[:, 0:ITEMS * 12].rearrange("p (w k v) -> p w k v", k=3, v=4)
        item_sums = sum_rests[0]
        onehot_ready = sem("onehot_ready")
        sums_ready0 = sem("sums_ready0")
        sums_free0 = sem("sums_free0")

        with nc.Block() as block:
            @block.vector
            def _(dve):
                c = Chain(dve, "stage5_dve")

                def make(t, slot, rnd):
                    if not (isinstance(t, int) and t < 2):
                        dve.wait_ge(sums_ready0, t - 1)
                    dve.tensor_tensor(onehot_b[:, slot * GROUP:(slot + 1) * GROUP, :],
                                      iota_b[:].unsqueeze(1).broadcast_to([P, GROUP, P]),
                                      dst_col[:, bass.ds(t * GROUP, GROUP)].unsqueeze(2).broadcast_to([P, GROUP, P]),
                                      ALU.is_equal).then_inc(onehot_ready, 1)
                make(0, 0, 0)
                make(1, 1, 0)
                tile_loop(dve, ITEMS // GROUP - 2, 2, make, first=2)
                dve.wait_ge(sums_free0, 2 + ITEMS // GROUP)
                c.link(dve.tensor_tensor(item_sums, sums_by_part[:, :, 2, :], sums_by_part[:, :, 1, :], ALU.add))
                c.link(dve.tensor_tensor(item_sums, item_sums, sums_by_part[:, :, 0, :], ALU.add))

            @block.tensor
            def _(pe):
                def add_up(t, slot, rnd):
                    pe.wait_ge(onehot_ready, t + 1)
                    pe.wait_ge(sums_free0, t + 1)
                    for u in range(GROUP):
                        ins = pe.matmul(bank[slot][:, u * 12:u * 12 + 12], onehot_b[:, slot * GROUP + u, :],
                                        sum_parts[:, bass.ds(t * GROUP + u, 1), :, :].rearrange("p a k v -> p (a k v)"),
                                        start=True, stop=True)
                    ins.then_inc(sums_ready0, 1)
                tile_loop(pe, ITEMS // GROUP, 2, add_up)

            @block.scalar
            def _(act):
                act.sem_inc(sums_free0, 2)

                def keep(t, slot, rnd):
                    hold(act, "act", sums_ready0, t + 1)
                    act.copy(sums_by_part[:, bass.ds(t * GROUP, GROUP), :, :].rearrange("p a k v -> p (a k v)"),
                             bank[slot][:, 0:GROUP * 12]).then_inc(sums_free0, 1)
                tile_loop(act, ITEMS // GROUP, 2, keep)

        s1 = Norm(1)
        l1_loads = sem("l1_loads")
        turned_sums = sem("turned_sums")
        sums_rows = sem("sums_rows")
        node_sums = sem("node_sums")
        squares = sem("squares")
        roots = sem("roots")
        gates_in = sem("gates_in")
        gates = sem("gates")
        norm1 = sb("norm1", [P, 4, CHUNKS])
        bn_scale = sb("bn_scale", [P, CHUNKS])
        bn_shift = sb("bn_shift", [P, CHUNKS])
        bn_root = sb("bn_root", [P, CHUNKS])
        bn_in = sb("bn_in", [P, CHUNKS])
        item_rows = work[1][0:IPB, :].rearrange("p (v b n) -> p v b n", v=4, b=BLOCKS)
        by_node = bank[4][:, 0:4 * NODE_TILES].rearrange("p (v t) -> p v t", v=4)
        degree1 = sb("degree1", [P, NODE_TILES])
        degree_root = sb("degree_root", [P, NODE_TILES])
        gate_arg = sb("gate_arg", [P, NODE_TILES])
        gate_out = sb("gate_out", [P, NODE_TILES])
        gated = sem("gated")
        gcn_stored = sem("gcn_stored")

        with nc.Block() as block:
            @block.sync
            def _(sp):
                sp.dma_start(wbuf[:, :, 0:FEAT], io["l1_w"]).then_inc(l1_loads, 16)
                sp.dma_start(norm1[:], io["l1_norm"]).then_inc(l1_loads, 16)

                def store(t, slot, rnd):
                    sp.wait_ge(s1.out_free, t + 3)
                    sp.dma_start(gcn_table[bass.ds(t * P, P), :],
                                 h[:, bass.ds(t, 1), :].rearrange("p a f -> p (a f)")).then_inc(gcn_stored, 16)
                tile_loop(sp, NODE_TILES, 5, store)
                sp.wait_ge(gcn_stored, 16 * NODE_TILES)

            @block.tensor
            def _(pe):
                for v in range(4):
                    for b in range(BLOCKS):
                        ins = pe.transpose(bank[v][0:IPB, b * P:(b + 1) * P], item_sums[:, b * IPB:(b + 1) * IPB, v], ident[:])
                    ins.then_inc(turned_sums, 1)
                for v in range(4):
                    pe.wait_ge(sums_rows, v + 1)
                    for b in range(BLOCKS):
                        ins = pe.matmul(by_node[:, v, :], item_rows[:, v, b, :], tile_onehot[:, b, :],
                                        start=(b == 0), stop=(b == BLOCKS - 1))
                ins.then_inc(node_sums, 1)
                pe.wait_ge(l1_loads, 32)
                project(pe, s1, [(0, 0, FEAT)])

            @block.scalar
            def _(act):
                act.wait_ge(squares, 1)
                act.activation(degree_root[:], degree1[:], ACT.Sqrt)
                act.activation(bn_root[:], bn_in[:], ACT.Sqrt).then_inc(roots, 1)
                act.wait_ge(gates_in, 1)
                act.activation(gate_out[:], gate_arg[:], ACT.Sigmoid).then_inc(gates, 1)
                norm_rows(act, s1)

            @block.vector
            def _(dve):
                c = Chain(dve, "stage6_dve")
                for v in range(4):
                    dve.wait_ge(turned_sums, v + 1)
                    dve.tensor_copy(item_rows[:, v, :, :].rearrange("p b n -> p (b n)"), bank[v][0:IPB, :]).then_inc(sums_rows, 1)
                dve.wait_ge(l1_loads, 32)
                c.mark(dve.tensor_scalar(bn_in[:], norm1[:, 3, :], BN_EPS, None, ALU.add))
                dve.wait_ge(node_sums, 1)
                c.mark(dve.tensor_scalar(small[0][:], by_node[:, 0, :], 0.0, None, ALU.is_equal))
                c.link(dve.tensor_scalar(degree1[:], by_node[:, 3, :], 1.0, None, ALU.add))
                dve.sem_inc(squares, 1)
                c.link(dve.tensor_tensor(small[0][:], small[0][:], by_node[:, 0, :], ALU.add))
                c.link(dve.reciprocal(small[0][:], small[0][:]))
                for k in range(2):
                    c.link(dve.tensor_tensor(small[1 + k][:], by_node[:, 1 + k, :], small[0][:], ALU.mult))
                    c.link(dve.tensor_scalar(small[1 + k][:], small[1 + k][:], attn[:, 4 + k:5 + k], 0.0, ALU.add, ALU.max))
                c.link(dve.tensor_tensor(gate_arg[:], gate[:], small[1][:], ALU.mult))
                c.link(dve.tensor_tensor(gate_arg[:], gate_arg[:], small[2][:], ALU.add))
                dve.sem_inc(gates_in, 1)
                dve.wait_ge(roots, 1)
                c.mark(dve.reciprocal(dinv[:], degree_root[:]))
                c.link(dve.reciprocal(bn_scale[:], bn_root[:]))
                c.link(dve.tensor_tensor(bn_scale[:], bn_scale[:], norm1[:, 0, :], ALU.mult))
                c.link(dve.tensor_tensor(bn_shift[:], bn_scale[:], norm1[:, 2, :], ALU.mult))
                c.link(dve.tensor_tensor(bn_shift[:], norm1[:, 1, :], bn_shift[:], ALU.subtract))
                dve.wait_ge(gates, 1)

                def add_gated(t, slot, rnd):
                    tile_x = x[:, bass.ds(t, 1), :].rearrange("p a f -> p (a f)")
                    dve.scalar_tensor_tensor(out=tile_x, in0=h[:, bass.ds(t, 1), :].rearrange("p a f -> p (a f)"),
                                             scalar=gate_out[:, bass.ds(t, 1)], in1=tile_x,
                                             op0=ALU.mult, op1=ALU.add).then_inc(gated, 1)
                tile_loop(dve, NODE_TILES, 5, add_gated)
                dve.wait_ge(gated, NODE_TILES)
                norm_statistics(dve, c, s1)

                def batch_norm(slot):
                    for k in range(CHUNKS):
                        ins = dve.tensor_scalar(ht_ring[:, slot, k, :], bank[slot][:, k * P:(k + 1) * P],
                                                bn_scale[:, k:k + 1], bn_shift[:, k:k + 1], ALU.mult, ALU.add)
                    return ins

                def scale(t, slot, rnd):
                    dve.tensor_scalar(h[:, bass.ds(t, 1), :].rearrange("p a f -> p (a f)"), bank[2 + slot][:, 0:FEAT],
                                      dinv[:, bass.ds(t, 1)], None, ALU.mult).then_inc(s1.out_free, 1)
                read_out(dve, s1, batch_norm, scale)

        RING = 8

        early_sems = clear_sems()

        class Gather:

            def __init__(self, name):
                self.index_ready = sem(f"index_ready_{name}")
                self.rows_in = [sem(f"g_rows_in_{name}{u}") for u in range(RING)]
                self.rows_used = sem(f"g_rows_used_{name}")

        def gather_rows(pool, g, table, cols, more_waits=None):
            def one_round(t, slot, rnd):
                pool.tensor_copy(idx_ring[:, slot, :], src_idx[:, bass.ds(t * RING, RING)]).then_inc(g.index_ready, 1)
                hold(pool, "pool", g.index_ready, t + 1)
                for u in range(RING):
                    hold(pool, "pool", g.rows_used, t * RING + (u + 1))
                    pool.indirect_dma_start(g_ring[:, u, 0:cols], None, table,
                                            bass.IndirectOffsetOnAxis(ap=idx_ring[:, slot, u:u + 1], axis=0)
                                            ).then_inc(g.rows_in[u], 16)
            tile_loop(pool, ITEMS // RING, 2, one_round)

        g1 = Gather("l1")
        ACC_BANKS = 4
        attrs_landed = [sem(f"attrs_landed{u}") for u in range(2)]
        onehot1 = sem("onehot1")
        acc_done1 = sem("acc_done1")

        def onehots(dve, t, u, used, ready, base):
            if not (isinstance(t, int) and t < 8):
                dve.wait_ge(used, t + (base - 7))
            dve.tensor_scalar(onehot[:, u, :], iota_b[:], dst_col[:, bass.ds(t, 1)], None, ALU.is_equal
                              ).then_inc(ready, 1)

        def item_tiles(eng, t0, n, table=None, top=NODE_TILES - 1):
            _, tiles = nc.values_load_multi_w_load_instructions((table or item_tile)[0:1, bass.ds(t0, n)], engines=(eng.engine,),
                                                                min_val=0, max_val=top,
                                                                skip_runtime_bounds_check_because="they count tiles passed")
            return tiles

        AHEAD = 4

        def accumulate(dve, cols, used, ready, done, extra=None, base=0):
            dve.memset(acc[:], 0.0).then_inc(done, 1)
            for t in range(AHEAD):
                onehots(dve, t, t, used, ready, base)
                if extra is not None:
                    extra(t, t, 0)

            def step(t, u, rnd, tile, ahead=True):
                if extra is not None and ahead:
                    extra(t + AHEAD, (u + AHEAD) % 8, rnd + (u + AHEAD) // 8)
                if ahead:
                    onehots(dve, t + AHEAD, (u + AHEAD) % 8, used, ready, base)
                sums = bank[u % ACC_BANKS][:, 0:cols]
                into = acc[:, bass.ds(tile, 1), 0:cols].rearrange("p a f -> p (a f)")
                dve.wait_ge(used, t + (base + 1))
                dve.wait_ge(done, t + 1)
                dve.tensor_tensor(into, into, sums, ALU.add).then_inc(done, 1)

            tiles = item_tiles(dve, 0, 8)
            for u in range(8):
                step(u, u, 0, tiles[u])
            with dve.Fori(1, ITEMS // 8 - 1) as i:
                tiles = item_tiles(dve, i * 8, 8)
                for u in range(8):
                    step(i * 8 + u, u, i, tiles[u])
            t0 = ITEMS - 8
            tiles = item_tiles(dve, t0, 8)
            for u in range(8):
                step(t0 + u, u, t0 // 8, tiles[u], ahead=t0 + u + AHEAD < ITEMS)

        with nc.Block() as block:
            @block.gpsimd
            def _(pool):
                gather_rows(pool, g1, gcn_table, FEAT)

            @block.sync
            def _(sp):
                def load(t, slot, rnd):
                    sp.wait_ge(g1.rows_used, t * CHUNK + CHUNK)
                    sp.dma_start(g_ring[:, slot * CHUNK:(slot + 1) * CHUNK, FEAT:GCN_COLS],
                                 edge_attr_d[bass.ds(t * CHUNK_EDGES, CHUNK_EDGES), :].rearrange("(u e) f -> e u f", e=P)
                                 ).then_inc(attrs_landed[slot], 16)
                tile_loop(sp, EDGE_CHUNKS, 2, load)

            @block.tensor
            def _(pe):
                pe.sem_inc(g1.rows_used, RING)

                def sums(t, u, rnd):
                    if u % CHUNK == 0:
                        pe.wait_ge(attrs_landed[u // CHUNK], rnd * 16 + 16)
                    pe.wait_ge(onehot1, t + 1)
                    pe.wait_ge(g1.rows_in[u], rnd * 16 + 16)
                    if not (isinstance(t, int) and t < ACC_BANKS):
                        pe.wait_ge(acc_done1, t - (ACC_BANKS - 2))
                    pe.matmul(bank[u % ACC_BANKS][:, 0:GCN_COLS], onehot[:, u, :], g_ring[:, u, :], start=True, stop=True
                              ).then_inc(g1.rows_used, 1)
                for u in range(RING):
                    sums(u, u, 0)
                tile_loop(pe, ITEMS - RING, RING, sums, first=RING)

            @block.vector
            def _(dve):
                accumulate(dve, GCN_COLS, g1.rows_used, onehot1, acc_done1, base=RING)

        free_sems(early_sems)

        s2 = Norm(2)
        l2_loads = sem("l2_loads")
        self_added = sem("self_added")
        scaled_in = sem("scaled_in")
        x2_done = sem("x2_done")
        heads_of = sb("heads_of", [P, CHUNKS, 2 * HEADS])
        attn2 = sb("attn2", [P, 2, CHUNKS])
        heads_ready = sem("heads_ready")
        folded = sem("folded")
        fold_read = sem("fold_read")
        row_b = sb("row_b", [P, FEAT])
        rows_out = [sem(f"rows_out{u}") for u in range(2)]
        logit_table = dram("logit_table", [NODE_TILES * P, 2 * HEADS])
        loop_attr = sb("loop_attr", [P, NODE_TILES, EDGE_DIM])
        wt = [work[2][:, 0:CHUNKS * FEAT].rearrange("p (c k) -> p c k", c=CHUNKS),
              work[3][:, 0:CHUNKS * FEAT].rearrange("p (c k) -> p c k", c=CHUNKS)]

        with nc.Block() as block:
            @block.sync
            def _(sp):
                for dst, name in ((wbuf[:, :, 0:FEAT], "l2_w"), (wt[0], "l2_wt"), (attn2[:], "l2_attn")):
                    sp.dma_start(dst, io[name]).then_inc(l2_loads, 16)
                sp.dma_start(row_b[:], io["l1_bias"].broadcast_to([P, FEAT])).then_inc(l2_loads, 16)

                def store(t, slot, rnd):
                    sp.wait_ge(s2.out_free, t + 3)
                    sp.dma_start(l2_table[bass.ds(t * P, P), :], row_ring[:, slot, :]).then_inc(rows_out[slot], 16)
                    sp.dma_start(logit_table[bass.ds(t * P, P), :], row_ring[:, slot, FEAT:L2_COLS]).then_inc(rows_out[slot], 16)
                tile_loop(sp, NODE_TILES, 2, store)
                sp.wait_ge(rows_out[0], 32 * ((NODE_TILES + 1) // 2))
                sp.wait_ge(rows_out[1], 32 * (NODE_TILES // 2))

            @block.gpsimd
            def _(pool):
                def add_self(t, slot, rnd):
                    rows = acc[:, bass.ds(t, 1), 0:FEAT].rearrange("p a f -> p (a f)")
                    pool.tensor_tensor(rows, rows, h[:, bass.ds(t, 1), :].rearrange("p a f -> p (a f)"), ALU.add
                                       ).then_inc(self_added, 1)
                tile_loop(pool, NODE_TILES, 5, add_self)

            @block.scalar
            def _(act):
                norm_rows(act, s2)

            @block.tensor
            def _(pe):
                pe.wait_ge(heads_ready, 1)
                pe.wait_ge(l2_loads, 64)
                for k in range(CHUNKS):
                    for f in range(CHUNKS):
                        ins = pe.matmul(bank[6][:, k * 8:k * 8 + 2 * HEADS], wt[0][:, f, k * P:(k + 1) * P],
                                        heads_of[:, f, :], start=(f == 0), stop=(f == CHUNKS - 1))
                ins.then_inc(folded, 1)
                pe.wait_ge(fold_read, 1)
                project(pe, s2, [(0, 0, L2_COLS)])

            @block.vector
            def _(dve):
                c = Chain(dve, "stage8_dve")
                c.link(dve.memset(heads_of[:], 0.0))
                dve.wait_ge(l2_loads, 64)
                half = P // 2
                for side in range(2):
                    for f in range(CHUNKS):
                        for n in range(2):
                            c.mark(dve.tensor_copy(heads_of[n * half:(n + 1) * half, f, side * HEADS + 2 * f + n:side * HEADS + 2 * f + n + 1],
                                                   attn2[n * half:(n + 1) * half, side, f:f + 1]))
                dve.wait_ge(c.sem, c.n)
                dve.sem_inc(heads_ready, 1)
                dve.wait_ge(folded, 1)
                dve.tensor_copy(wbuf[:, :, FEAT:L2_COLS], bank[6][:, 0:16].rearrange("p (k n) -> p k n", k=CHUNKS)).then_inc(fold_read, 1)
                c.link(dve.tensor_scalar(small[0][:], degree1[:], -1.0, 1.0, ALU.add, ALU.max))
                c.link(dve.reciprocal(small[0][:], small[0][:]))
                c.link(dve.tensor_tensor(loop_attr[:], acc[:, :, FEAT:GCN_COLS],
                                         small[0][:].unsqueeze(2).broadcast_to([P, NODE_TILES, EDGE_DIM]), ALU.mult))

                def scale(t):
                    rows = acc[:, bass.ds(t, 1), 0:FEAT].rearrange("p a f -> p (a f)")
                    dve.wait_ge(self_added, t + 1)
                    dve.scalar_tensor_tensor(out=rows, in0=rows, scalar=dinv[:, bass.ds(t, 1)], in1=row_b[:],
                                             op0=ALU.mult, op1=ALU.add).then_inc(scaled_in, 1)

                def add(t):
                    rows = acc[:, bass.ds(t, 1), 0:FEAT].rearrange("p a f -> p (a f)")
                    tile_x = x[:, bass.ds(t, 1), :].rearrange("p a f -> p (a f)")
                    dve.wait_ge(scaled_in, t + 1)
                    dve.scalar_tensor_tensor(out=tile_x, in0=rows, scalar=0.0, in1=tile_x,
                                             op0=ALU.max, op1=ALU.add).then_inc(x2_done, 1)

                def both(t, slot, rnd):
                    scale(t)
                    add(t - 1)
                scale(0)
                tile_loop(dve, NODE_TILES - 1, 4, both, first=1)
                add(NODE_TILES - 1)
                dve.wait_ge(x2_done, NODE_TILES)
                norm_statistics(dve, c, s2)

                def keep(t, slot, rnd):
                    if not (isinstance(t, int) and t < 2):
                        dve.wait_ge(rows_out[slot], rnd * 32)
                    dve.tensor_copy(row_ring[:, slot, :], bank[2 + slot][:, 0:L2_COLS]).then_inc(s2.out_free, 1)
                read_out(dve, s2, plain_cols(dve), keep)

        idx2_in = sem("idx2_in")
        idx2 = sb("idx2", [P, 2, NODE_TILES], I32)
        side_logits = sb("side_logits", [P, NODE_TILES, 2 * HEADS])
        side_in = sem("side_in")
        GROUPS2 = 5
        rows2_in = [sem(f"rows2_in{k}") for k in range(GROUPS2)]
        alpha = sb("alpha", [P, NODE_TILES, HEADS])
        less2 = sem("less2")
        exp2 = sem("exp2")
        mixed = sem("mixed")
        mean_head = sb("mean_head", [P, 2, HEAD_DIM])

        with nc.Block() as block:
            @block.sync
            def _(sp):
                sp.dma_start(idx2[:, 0, :], io["l2_src"]).then_inc(idx2_in, 16)
                sp.dma_start(idx2[:, 1, :], io["l2_dst"]).then_inc(idx2_in, 16)

            @block.gpsimd
            def _(pool):
                pool.wait_ge(idx2_in, 32)
                for t in range(NODE_TILES):
                    pool.indirect_dma_start(side_logits[:, t, :], None, logit_table,
                                            bass.IndirectOffsetOnAxis(ap=idx2[:, 0, t:t + 1], axis=0)).then_inc(side_in, 16)
                for t in range(NODE_TILES):
                    pool.indirect_dma_start(acc[:, t, 0:L2_COLS], None, l2_table,
                                            bass.IndirectOffsetOnAxis(ap=idx2[:, 1, t:t + 1], axis=0)
                                            ).then_inc(rows2_in[t // 5], 16)

            @block.scalar
            def _(act):
                act.wait_ge(less2, 1)
                act.activation(alpha[:], alpha[:], ACT.Exp).then_inc(exp2, 1)

            @block.vector
            def _(dve):
                c = Chain(dve, "stage9_dve")
                dve.wait_ge(side_in, 16 * NODE_TILES)
                for k in range(GROUPS2):
                    dve.wait_ge(rows2_in[k], 16 * 5)
                c.link(dve.tensor_tensor(alpha[:], side_logits[:, :, 0:HEADS], acc[:, :, FEAT + HEADS:L2_COLS], ALU.add))
                c.link(dve.scalar_tensor_tensor(out=alpha[:], in0=alpha[:], scalar=NEG_L2, in1=alpha[:], op0=ALU.mult, op1=ALU.max))
                c.link(dve.tensor_reduce(small[0][:], alpha[:], X_AXIS, ALU.max))
                dve.tensor_tensor(alpha[:], alpha[:], small[0][:].unsqueeze(2).broadcast_to([P, NODE_TILES, HEADS]), ALU.subtract
                                  ).then_inc(less2, 1)
                dve.wait_ge(exp2, 1)
                c.link(dve.tensor_reduce(small[1][:], alpha[:], X_AXIS, ALU.add))
                c.link(dve.reciprocal(small[1][:], small[1][:]))
                c.link(dve.tensor_tensor(alpha[:], alpha[:], small[1][:].unsqueeze(2).broadcast_to([P, NODE_TILES, HEADS]), ALU.mult))

                def mix(t, slot, rnd):
                    rows = acc[:, bass.ds(t, 1), 0:FEAT].rearrange("p a (h d) -> p (a h) d", h=HEADS)
                    dve.tensor_tensor(rows, rows, alpha[:, bass.ds(t, 1), :].rearrange("p a h -> p (a h)").unsqueeze(2).broadcast_to([P, HEADS, HEAD_DIM]),
                                      ALU.mult).then_inc(mixed, 1)
                    hold(dve, "dve", mixed, t * 3 + 1)
                    dve.tensor_reduce(mean_head[:, slot, :], acc[:, bass.ds(t, 1), 0:FEAT].rearrange("p a (h d) -> p (a d) h", h=HEADS),
                                      X_AXIS, ALU.add).then_inc(mixed, 1)
                    dve.wait_ge(mixed, t * 3 + 2)
                    tile_x = x[:, bass.ds(t, 1), :].rearrange("p a (h d) -> p (a h) d", h=HEADS)
                    dve.tensor_tensor(tile_x, tile_x, mean_head[:, slot, :].unsqueeze(1).broadcast_to([P, HEADS, HEAD_DIM]),
                                      ALU.add).then_inc(mixed, 1)
                    dve.wait_ge(mixed, t * 3 + 3)
                tile_loop(dve, NODE_TILES, 2, mix)

        s3 = Norm(3)
        l3_loads = sem("l3_loads")
        we_ext = sb("we_ext", [EDGE_DIM, L3_COLS])
        attt = sb("attt", [P, CHUNKS])
        bt = sb("bt", [P, 2, CHUNKS])
        bias3 = sb("bias3", [1, 2 * L3_COLS])
        heads3_ready = sem("heads3_ready")
        folded3 = sem("folded3")
        fold3_read = sem("fold3_read")
        xl_linear = sb("xl_linear", [P, NODE_TILES, HEADS])
        rest_ring = item_vals[:, 0, 0:4 * L3_COLS].rearrange("p (s k f) -> p s k f", s=2, k=2)
        rest_ready = sem("rest_ready")
        split_steps = sem("split_steps")
        split_done = sem("split_done")
        l3_stored = sem("l3_stored")

        wt3 = [flat(acc[:])[:, k * CHUNKS * FEAT:(k + 1) * CHUNKS * FEAT].rearrange("p (c k) -> p c k", c=CHUNKS)
               for k in range(2)]
        wet = flat(acc[:])[:, 2048:2048 + CHUNKS * EDGE_DIM].rearrange("p (c k) -> p c k", c=CHUNKS)

        with nc.Block() as block:
            @block.sync
            def _(sp):
                for dst, name in ((wbuf[:, :, 0:FEAT], "l3_wl"), (wbuf[:, :, L3_COLS:L3_COLS + FEAT], "l3_wr"),
                                  (wt3[0], "l3_wlt"), (wt3[1], "l3_wrt"), (wet, "l3_wet"), (attt[:], "l3_attt"),
                                  (bt[:], "l3_bt"), (we_ext[:, 0:FEAT], "l3_we")):
                    sp.dma_start(dst, io[name]).then_inc(l3_loads, 16)
                sp.dma_start(bias3[:, 0:FEAT], io["l3_bias"][:, 0:FEAT]).then_inc(l3_loads, 16)
                sp.dma_start(bias3[:, L3_COLS:L3_COLS + FEAT], io["l3_bias"][:, FEAT:2 * FEAT]).then_inc(l3_loads, 16)
                sp.dma_start(row_b[:], io["l3_att"].broadcast_to([P, FEAT])).then_inc(l3_loads, 16)

                def store(t, slot, rnd):
                    sp.wait_ge(s3.out_free, t + 3)
                    sp.dma_start(l3_table[bass.ds(t * P, P), 0:FEAT],
                                 h[:, bass.ds(t, 1), :].rearrange("p a f -> p (a f)")).then_inc(l3_stored, 16)
                    sp.dma_start(l3_table[bass.ds(t * P, P), FEAT:L3_COLS],
                                 xl_linear[:, bass.ds(t, 1), :].rearrange("p a f -> p (a f)")).then_inc(l3_stored, 16)
                tile_loop(sp, NODE_TILES, 5, store)
                sp.wait_ge(l3_stored, 32 * NODE_TILES)

            @block.scalar
            def _(act):
                norm_rows(act, s3)

            @block.tensor
            def _(pe):
                pe.wait_ge(heads3_ready, 1)
                pe.wait_ge(l3_loads, 16 * 11)
                att_of = heads_of[:, :, 0:HEADS]
                for n in range(2):
                    for k in range(CHUNKS):
                        for f in range(CHUNKS):
                            at = (n * CHUNKS + k) * HEADS
                            pe.matmul(bank[6][:, at:at + HEADS], wt3[n][:, f, k * P:(k + 1) * P], att_of[:, f, :],
                                      start=(f == 0), stop=(f == CHUNKS - 1))
                    for f in range(CHUNKS):
                        pe.matmul(bank[7][0:1, n * HEADS:(n + 1) * HEADS], bt[:, n, f:f + 1], att_of[:, f, :],
                                  start=(f == 0), stop=(f == CHUNKS - 1))
                for f in range(CHUNKS):
                    ins = pe.matmul(bank[7][0:EDGE_DIM, 16:16 + HEADS], wet[:, f, :], att_of[:, f, :],
                                    start=(f == 0), stop=(f == CHUNKS - 1))
                ins.then_inc(folded3, 1)
                pe.wait_ge(fold3_read, 1)
                project(pe, s3, [(0, 0, L3_COLS), (1, L3_COLS, 2 * L3_COLS)], bias=bias3)

            @block.gpsimd
            def _(pool):
                def split(t, slot, rnd):
                    pool.wait_ge(rest_ready, t + 1)
                    part = [xr_parts[:, bass.ds(t, 1), k, :].rearrange("p a f -> p (a f)") for k in range(3)]
                    pool.tensor_copy(part[1], rest_ring[:, slot, 0, :]).then_inc(split_steps, 1)
                    hold(pool, "pool", split_steps, t * 2 + 1)
                    pool.tensor_tensor(rest_ring[:, slot, 1, :], rest_ring[:, slot, 0, :], part[1], ALU.subtract
                                       ).then_inc(split_steps, 1)
                    pool.wait_ge(split_steps, t * 2 + 2)
                    pool.tensor_copy(part[2], rest_ring[:, slot, 1, :]).then_inc(split_done, 1)
                tile_loop(pool, NODE_TILES, 2, split)

            @block.vector
            def _(dve):
                c = Chain(dve, "stage10_dve")
                c.link(dve.memset(heads_of[:], 0.0))
                dve.wait_ge(l3_loads, 16 * 11)
                half = P // 2
                for f in range(CHUNKS):
                    for n in range(2):
                        c.mark(dve.tensor_copy(heads_of[n * half:(n + 1) * half, f, 2 * f + n:2 * f + n + 1],
                                               attt[n * half:(n + 1) * half, f:f + 1]))
                dve.wait_ge(c.sem, c.n)
                dve.sem_inc(heads3_ready, 1)
                c.mark(dve.tensor_scalar(row_b[:], row_b[:], 1.0 - NEG_GAT, None, ALU.mult))
                dve.wait_ge(folded3, 1)
                for n in range(2):
                    at = n * CHUNKS * HEADS
                    c.mark(dve.tensor_scalar(wbuf[:, :, n * L3_COLS + FEAT:(n + 1) * L3_COLS],
                                             bank[6][:, at:at + CHUNKS * HEADS].rearrange("p (k n) -> p k n", k=CHUNKS),
                                             NEG_GAT, None, ALU.mult))
                    c.mark(dve.tensor_scalar(bias3[:, n * L3_COLS + FEAT:(n + 1) * L3_COLS],
                                             bank[7][0:1, n * HEADS:(n + 1) * HEADS], NEG_GAT, None, ALU.mult))
                c.link(dve.tensor_scalar(we_ext[:, FEAT:L3_COLS], bank[7][0:EDGE_DIM, 16:16 + HEADS], NEG_GAT, None, ALU.mult))
                dve.sem_inc(fold3_read, 1)
                norm_statistics(dve, c, s3)
                parts_made = c.sem
                before = c.n

                def keep(t, slot, rnd):
                    left, right = bank[2 + slot * 2], bank[3 + slot * 2]
                    first = xr_parts[:, bass.ds(t, 1), 0, :].rearrange("p a f -> p (a f)")
                    dve.tensor_copy(first, right[:, 0:L3_COLS]).then_inc(parts_made, 1)
                    dve.tensor_copy(h[:, bass.ds(t, 1), :].rearrange("p a f -> p (a f)"), left[:, 0:FEAT]).then_inc(parts_made, 1)
                    if not (isinstance(t, int) and t < 2):
                        dve.wait_ge(split_done, t - 1)
                    dve.wait_ge(parts_made, t * 2 + (before + 1))
                    dve.tensor_tensor(rest_ring[:, slot, 0, :], right[:, 0:L3_COLS], first, ALU.subtract).then_inc(rest_ready, 1)
                    dve.wait_ge(parts_made, t * 2 + (before + 2))
                    dve.wait_ge(rest_ready, t + 1)
                    dve.tensor_copy(xl_linear[:, bass.ds(t, 1), :].rearrange("p a f -> p (a f)"), left[:, FEAT:L3_COLS]
                                    ).then_inc(s3.out_free, 1)
                read_out(dve, s3, plain_cols(dve), keep)

        ident_b = sb("ident_b", [P, P], BF16)
        attr_row = sb("attr_row", [P, 2, EDGE_DIM])
        attr_turned = sb("attr_turned", [EDGE_DIM, 2, P])
        own = acc[:, :, 0:L3_COLS]
        own_logits = sb("own_logits", [P, NODE_TILES, HEADS])
        ident_ready = sem("ident_ready")
        attr_ready = sem("attr_ready")
        attr_flipped = sem("attr_flipped")
        attr_stored = sem("attr_stored")
        own_products = sem("own_products")
        own_added = sem("own_added")
        own_relued = sem("own_relued")
        we_parts = sb("we_parts", [P, L3_COLS], BF16)
        we_part = item_vals[0:EDGE_DIM, 1, 0:3 * L3_COLS // 2].bitcast(BF16).rearrange("p (k f) -> p k f", k=3)
        we_rest = item_vals[0:EDGE_DIM, 1, 512:512 + 2 * L3_COLS].rearrange("p (k f) -> p k f", k=2)
        we_split = sem("we_split")
        we_placed = sem("we_placed")

        def add_terms(pe, into, places, tile, attrs, weights):
            for k in range(3):
                pe.matmul(into, places, xr_parts[:, bass.ds(tile, 1), k, :].rearrange("p a f -> p (a f)"),
                          start=(k == 0), stop=False)
            return pe.matmul(into, attrs, weights, start=False, stop=True)

        with nc.Block() as block:
            @block.sync
            def _(sp):
                sp.wait_ge(we_split, 1)
                for b in range(PAIRS):
                    sp.dma_start(we_parts[b * EDGE_DIM:(b + 1) * EDGE_DIM, :], we_part[:, b % 3, :]).then_inc(we_placed, 16)
                sp.wait_ge(we_placed, 16 * PAIRS)

            @block.tensor
            def _(pe):
                def flip(t, slot):
                    pe.wait_ge(attr_ready, t + 1)
                    pe.transpose(bank[2 + slot][0:EDGE_DIM, 0:P], attr_row[:, slot, :], ident[:]).then_inc(attr_flipped, 1)

                def product(t, slot):
                    pe.wait_ge(attr_stored, t + 1)
                    if not (isinstance(t, int) and t < 2):
                        pe.wait_ge(own_added, t - 1)
                    add_terms(pe, bank[slot][:, 0:L3_COLS], ident_b[:], t, attr_turned[:, slot, :],
                              we_ext[:]).then_inc(own_products, 1)

                def both(t, slot, rnd):
                    flip(t, slot)
                    product(t - 1, 1 - slot)
                pe.wait_ge(ident_ready, 1)
                flip(0, 0)
                both(1, 1, 0)
                both(2, 0, 1)
                tile_loop(pe, NODE_TILES - 3, 2, both, first=3)
                product(NODE_TILES - 1, (NODE_TILES - 1) % 2)

            @block.scalar
            def _(act):
                def relu(t, slot, rnd):
                    hold(act, "act", own_added, t + 1)
                    rows = own[:, bass.ds(t, 1), 0:FEAT].rearrange("p a f -> p (a f)")
                    act.activation(rows, rows, ACT.Relu).then_inc(own_relued, 1)
                tile_loop(act, NODE_TILES, 5, relu)

            @block.vector
            def _(dve):
                c = Chain(dve, "stage11_dve")
                dve.tensor_copy(ident_b[:], ident[:]).then_inc(ident_ready, 1)
                c.link(dve.tensor_copy(we_part[:, 0, :], we_ext[:]))
                c.link(dve.tensor_tensor(we_rest[:, 0, :], we_ext[:], we_part[:, 0, :], ALU.subtract))
                c.link(dve.tensor_copy(we_part[:, 1, :], we_rest[:, 0, :]))
                c.link(dve.tensor_tensor(we_rest[:, 1, :], we_rest[:, 0, :], we_part[:, 1, :], ALU.subtract))
                c.link(dve.tensor_copy(we_part[:, 2, :], we_rest[:, 1, :]))
                dve.sem_inc(we_split, 1)

                def stage_attr(t, slot):
                    if not (isinstance(t, int) and t < 2):
                        dve.wait_ge(attr_flipped, t - 1)
                    dve.tensor_copy(attr_row[:, slot, :], loop_attr[:, bass.ds(t, 1), :].rearrange("p a k -> p (a k)")
                                    ).then_inc(attr_ready, 1)

                def store_attr(t, slot):
                    if not (isinstance(t, int) and t < 2):
                        dve.wait_ge(own_products, t - 1)
                    dve.wait_ge(attr_flipped, t + 1)
                    dve.tensor_copy(attr_turned[:, slot, :], bank[2 + slot][0:EDGE_DIM, 0:P]).then_inc(attr_stored, 1)

                def add(t, slot):
                    dve.wait_ge(own_products, t + 1)
                    dve.tensor_tensor(own[:, bass.ds(t, 1), 0:FEAT].rearrange("p a f -> p (a f)"), bank[slot][:, 0:FEAT],
                                      h[:, bass.ds(t, 1), :].rearrange("p a f -> p (a f)"), ALU.add)
                    dve.tensor_tensor(own[:, bass.ds(t, 1), FEAT:L3_COLS].rearrange("p a h -> p (a h)"), bank[slot][:, FEAT:L3_COLS],
                                      xl_linear[:, bass.ds(t, 1), :].rearrange("p a h -> p (a h)"), ALU.add).then_inc(own_added, 1)

                def both(t, slot, rnd):
                    stage_attr(t, slot)
                    store_attr(t, slot)
                    add(t - 1, 1 - slot)
                stage_attr(0, 0)
                store_attr(0, 0)
                both(1, 1, 0)
                tile_loop(dve, NODE_TILES - 2, 2, both, first=2)
                add(NODE_TILES - 1, (NODE_TILES - 1) % 2)
                dve.wait_ge(own_relued, NODE_TILES)
                wide = own[:, :, 0:FEAT]
                c.link(dve.tensor_tensor(wide, wide, row_b[:].unsqueeze(1).broadcast_to([P, NODE_TILES, FEAT]), ALU.mult))
                c.link(dve.tensor_reduce(own_logits[:], wide.rearrange("p t (h d) -> p t h d", h=HEADS), X_AXIS, ALU.add))
                c.link(dve.tensor_tensor(own_logits[:], own_logits[:], own[:, :, FEAT:L3_COLS], ALU.add))

        g3 = Gather("l3a")
        sum_ring = flat(sums_rhs[:])[:, 0:RING * L3_COLS].rearrange("p (u f) -> p u f", u=RING)
        relu_ring = flat(sums_rhs[:])[:, RING * L3_COLS:RING * L3_COLS + 4 * FEAT].rearrange("p (u f) -> p u f", u=4)
        attrs_turned = item_vals[:, 1, 0:RING * P // 2].bitcast(BF16).rearrange("p (u e) -> p u e", u=RING)
        pair_rows = attr_parts_d.rearrange("b p c -> (b p c)").rearrange("(k g e) -> k g e", g=EDGE_TILES, e=P)
        edge_tile = item_vals[0:1, 1, 1024:1024 + ITEMS].bitcast(I32)
        edge_tile_in = sem("edge_tile_in")
        nonlinear = sb("nonlinear", [P, RING, HEADS])
        rows3_in = [sem(f"rows3_in{u}") for u in range(2)]
        attrs3_in = [sem(f"attrs3_in{u}") for u in range(RING)]
        places3 = sem("places3")
        terms3 = sem("terms3")
        relued3 = sem("relued3")
        dotted3 = sem("dotted3")
        logits3 = sem("logits3")
        LAG = 2

        def item_rounds(eng, step, prepare=None):
            def one(t0, rnd):
                extra = (prepare(t0),) if prepare else ()
                for u in range(RING):
                    step(t0 + u, u, rnd, *extra)
            one(0, 0)
            with eng.Fori(1, ITEMS // RING - 1) as i:
                one(i * RING, i)
            one(ITEMS - RING, ITEMS // RING - 1)

        def at_least(t, n):
            return not isinstance(t, int) or t >= n

        def known_after(t, n):
            return not isinstance(t, int) or t + n < ITEMS

        with nc.Block() as block:
            @block.gpsimd
            def _(pool):
                gather_rows(pool, g3, l3_table, L3_COLS)

            @block.sync
            def _(sp):
                sp.dma_start(edge_tile, edge_tile_d.unsqueeze(0)).then_inc(edge_tile_in, 16)
                sp.wait_ge(edge_tile_in, 16)

                def load(t, u, rnd, tiles):
                    slot = u // CHUNK
                    if u % CHUNK == 0:
                        if at_least(t, RING):
                            sp.wait_ge(places3, rnd * 2 + (slot - 1))
                        sp.dma_start(rows_ring[:, slot, 0, :],
                                     dst_rows_d[bass.ds(t * P, CHUNK_EDGES)].unsqueeze(0).broadcast_to([P, CHUNK_EDGES])
                                     ).then_inc(rows3_in[slot], 16)
                    if at_least(t, RING):
                        sp.wait_ge(terms3, t - (RING - 1))
                    sp.dma_start(attrs_turned[:, u, :], pair_rows[:, bass.ds(tiles[u], 1), :].rearrange("k a e -> k (a e)")
                                 ).then_inc(attrs3_in[u], 16)
                item_rounds(sp, load, lambda t0: item_tiles(sp, t0, RING, edge_tile, EDGE_TILES - 1))

            @block.tensor
            def _(pe):
                def item(t, u, rnd, tiles):
                    slot = u // CHUNK
                    if u % CHUNK == 0:
                        pe.wait_ge(places3, rnd * 2 + (slot + 1))
                    pe.wait_ge(attrs3_in[u], rnd * 16 + 16)
                    if at_least(t, ACC_BANKS):
                        pe.wait_ge(g3.rows_used, t + (RING + 1 - ACC_BANKS))
                    add_terms(pe, bank[u % ACC_BANKS][:, 0:L3_COLS], place_ring[:, slot, 0, u % CHUNK * P:(u % CHUNK + 1) * P],
                              tiles[u], attrs_turned[:, u, :], we_parts[:]).then_inc(terms3, 1)
                item_rounds(pe, item, lambda t0: item_tiles(pe, t0, RING))

            @block.scalar
            def _(act):
                def item(t, u, rnd):
                    act.wait_ge(g3.rows_used, t + (RING + 1))
                    if at_least(t, 4):
                        act.wait_ge(dotted3, t - 3)
                    act.activation(relu_ring[:, u % 4, :], sum_ring[:, u, 0:FEAT], ACT.Relu).then_inc(relued3, 1)
                item_rounds(act, item)

            @block.vector
            def _(dve):
                dve.sem_inc(g3.rows_used, RING)

                def places(chunk, slot, rnd):
                    dve.wait_ge(rows3_in[slot], rnd * 16 + 16)
                    if at_least(chunk, 2):
                        dve.wait_ge(terms3, chunk * CHUNK - CHUNK)
                    dve.tensor_scalar(place_ring[:, slot, 0, :], rows_ring[:, slot, 0, :], p_index[:], None, ALU.is_equal
                                      ).then_inc(places3, 1)

                def dot(t, u):
                    dve.wait_ge(relued3, t + 1)
                    for hd in range(HEADS):
                        d = slice(hd * HEAD_DIM, (hd + 1) * HEAD_DIM)
                        ins = dve.tensor_tensor_reduce(out=relu_ring[:, u % 4, d], in0=relu_ring[:, u % 4, d], in1=row_b[:, d],
                                                       scale=1.0, scalar=0.0, op0=ALU.mult, op1=ALU.add,
                                                       accum_out=nonlinear[:, u, hd:hd + 1])
                    ins.then_inc(dotted3, 1)

                def finish(t0, slot):
                    dve.wait_ge(dotted3, t0 + CHUNK)
                    us = slice(slot * CHUNK, (slot + 1) * CHUNK)
                    dve.tensor_tensor(logits[:, bass.ds(t0, CHUNK), :], nonlinear[:, us, :], sum_ring[:, us, FEAT:L3_COLS], ALU.add
                                      ).then_inc(logits3, 1)

                def item(t, u, rnd):
                    slot = u // CHUNK
                    if u % CHUNK == 0 and known_after(t, CHUNK):
                        places(rnd * 2 + (slot + 1), 1 - slot, rnd + slot)
                    dve.wait_ge(g3.rows_in[u], rnd * 16 + 16)
                    dve.wait_ge(terms3, t + 1)
                    if at_least(t, RING):
                        dve.wait_ge(relued3, t - (RING - 1))
                        if u % CHUNK == 0:
                            dve.wait_ge(logits3, rnd * 2 + (slot - 1))
                    dve.tensor_tensor(sum_ring[:, u, :], g_ring[:, u, 0:L3_COLS], bank[u % ACC_BANKS][:, 0:L3_COLS], ALU.add
                                      ).then_inc(g3.rows_used, 1)
                    if at_least(t, LAG):
                        dot(t - LAG, (u - LAG) % RING)
                        if u % CHUNK == CHUNK - 1 and at_least(t, CHUNK):
                            finish(t - (2 * CHUNK - 1), 1 - slot)
                places(0, 0, 0)
                item_rounds(dve, item)
                for t in range(ITEMS - LAG, ITEMS):
                    dot(t, t % RING)
                finish(ITEMS - CHUNK, 1)

        seg3 = Segments("l3")
        masked3 = sem("masked3")
        less3 = sem("less3")
        exp3 = sem("exp3")

        with nc.Block() as block:
            @block.tensor
            def _(pe):
                segment_max_pe(pe, seg3, logits, HEADS, masked3)

            @block.scalar
            def _(act):
                act.wait_ge(less3, 1)
                act.activation(sums_rhs[:, :, 0:HEADS], logits, ACT.Exp).then_inc(exp3, 1)
                act.wait_ge(exp3, 1)

            @block.vector
            def _(dve):
                c = Chain(dve, "stage13_dve")
                by_head = [P, ITEMS, HEADS]
                c.link(dve.tensor_tensor(logits, logits, off_col[:].unsqueeze(2).broadcast_to(by_head), ALU.add))
                dve.sem_inc(masked3, 1)
                segment_max_dve(dve, c, seg3, maxima, HEADS)
                dve.tensor_tensor(logits, logits, maxima, ALU.subtract).then_inc(less3, 1)
                c.mark(dve.tensor_tensor(sums_rhs[:, :, HEADS:2 * HEADS], maxima, last_col[:].unsqueeze(2).broadcast_to(by_head), ALU.mult))

        g4 = Gather("l3b")
        weighted = flat(item_vals[:])[:, 0:RING * OUT_COLS].rearrange("p (u f) -> p u f", u=RING)
        onehot4 = sem("onehot4")
        summed4 = sem("summed4")
        acc_done4 = sem("acc_done4")
        beside4 = sem("beside4")

        with nc.Block() as block:
            @block.gpsimd
            def _(pool):
                gather_rows(pool, g4, l3_table, L3_COLS)

            @block.scalar
            def _(act):
                def beside(t, slot, rnd):
                    if at_least(t, 2):
                        hold(act, "act", summed4, t * CHUNK - CHUNK)
                    act.copy(weighted[:, slot * CHUNK:(slot + 1) * CHUNK, FEAT:OUT_COLS],
                             sums_rhs[:, bass.ds(t * CHUNK, CHUNK), :]).then_inc(beside4, 1)
                beside(0, 0, 0)
                beside(1, 1, 0)
                tile_loop(act, EDGE_CHUNKS - 2, 2, beside, first=2)

            @block.tensor
            def _(pe):
                def sums(t, u, rnd):
                    if u % CHUNK == 0:
                        pe.wait_ge(beside4, rnd * 2 + (u // CHUNK + 1))
                    pe.wait_ge(onehot4, t + 1)
                    pe.wait_ge(g4.rows_used, t + (RING + 1))
                    if at_least(t, ACC_BANKS):
                        pe.wait_ge(acc_done4, t - (ACC_BANKS - 2))
                    pe.matmul(bank[u % ACC_BANKS][:, 0:OUT_COLS], onehot[:, u, :], weighted[:, u, :], start=True, stop=True
                              ).then_inc(summed4, 1)
                item_rounds(pe, sums)

            @block.vector
            def _(dve):
                dve.sem_inc(g4.rows_used, RING)

                def weigh(t, u, rnd):
                    dve.wait_ge(g4.rows_in[u], rnd * 16 + 16)
                    if at_least(t, RING):
                        dve.wait_ge(summed4, t - (RING - 1))
                    dve.tensor_tensor(weighted[:, u, 0:FEAT].rearrange("p (h d) -> p h d", h=HEADS),
                                      g_ring[:, u, 0:FEAT].rearrange("p (h d) -> p h d", h=HEADS),
                                      sums_rhs[:, bass.ds(t, 1), 0:HEADS].rearrange("p a h -> p (a h)").unsqueeze(2).broadcast_to([P, HEADS, HEAD_DIM]),
                                      ALU.mult).then_inc(g4.rows_used, 1)
                accumulate(dve, OUT_COLS, summed4, onehot4, acc_done4, extra=weigh)

        final_loads = sem("final_loads")
        shares_in = sem("shares_in")
        shares = sem("shares")
        bias_in = sem("bias_in")
        own_weighed = sem("own_weighed")
        sum_weighed = sem("sum_weighed")
        total = sem("total")
        biased = sem("biased")
        sigmoids = sem("sigmoids")
        silu = sem("silu")
        base = sem("base")
        normed = sem("normed")
        result = sem("result")
        written = sem("written")
        top_all, den, share_0, share_1 = [
            flat(item_vals[:])[:, 2560 + i * 128:2560 + i * 128 + NODE_TILES * HEADS].rearrange("p (t h) -> p t h", h=HEADS)
            for i in range(4)]
        share = [share_0, share_1]
        sig_ring = rings[:, 0:2 * FEAT].rearrange("p (s f) -> p s f", s=2)
        norm_ring = rings[:, 512:512 + 2 * FEAT].rearrange("p (s f) -> p s f", s=2)

        def rows_of(table, t, cols=FEAT):
            return table[:, bass.ds(t, 1), 0:cols].rearrange("p a f -> p (a f)")

        def heads_view(ap):
            return ap.rearrange("p (h d) -> p h d", h=HEADS)

        def head_scale(n, t):
            return share[n][:, bass.ds(t, 1), :].rearrange("p a h -> p (a h)").unsqueeze(2).broadcast_to([P, HEADS, HEAD_DIM])

        with nc.Block() as block:
            @block.sync
            def _(sp):
                sp.dma_start(row_b[:], io["l3_bias"][:, 2 * FEAT:3 * FEAT].broadcast_to([P, FEAT])).then_inc(final_loads, 16)

                def write(t, slot, rnd):
                    sp.wait_ge(result, t + 1)
                    sp.dma_start(out[bass.ds(t * P, P), :], rows_of(x, t)).then_inc(written, 16)
                tile_loop(sp, NODE_TILES - 1, 4, write)
                sp.wait_ge(result, NODE_TILES)
                sp.dma_start(out[(NODE_TILES - 1) * P:NODES, :], x[0:LAST_ROWS, NODE_TILES - 1, :]).then_inc(written, 16)
                sp.wait_ge(written, 16 * NODE_TILES)

            @block.gpsimd
            def _(pool):
                pool.wait_ge(shares, 1)

                def weigh(t, slot, rnd):
                    pool.tensor_tensor(heads_view(rows_of(h, t)), heads_view(rows_of(h, t)), head_scale(1, t), ALU.mult
                                       ).then_inc(own_weighed, 1)
                tile_loop(pool, NODE_TILES, 5, weigh)

            @block.scalar
            def _(act):
                act.wait_ge(shares_in, 1)
                act.activation(share[0], share[0], ACT.Exp)
                act.activation(share[1], share[1], ACT.Exp).then_inc(shares_in, 1)

                def norm(t, slot):
                    if at_least(t, 2):
                        hold(act, "act", base, t - 1)
                    act.activation(norm_ring[:, slot, :], rows_of(x, t), ACT.Relu, bias=shift[:, bass.ds(t, 1)],
                                   scale=rstd[:, bass.ds(t, 1)]).then_inc(normed, 1)

                def one(t, slot, rnd):
                    norm(t, slot)
                    if at_least(t, 2):
                        act.wait_ge(silu, t - 1)
                    hold(act, "act", biased, t + 1)
                    act.activation(sig_ring[:, slot, :], rows_of(acc, t), ACT.Sigmoid).then_inc(sigmoids, 1)
                one(0, 0, 0)
                one(1, 1, 0)
                tile_loop(act, NODE_TILES - 2, 2, one, first=2)

            @block.vector
            def _(dve):
                c = Chain(dve, "stage15_dve")
                edges_den = acc[:, :, FEAT:FEAT + HEADS]
                edges_top = acc[:, :, FEAT + HEADS:OUT_COLS]
                c.link(dve.tensor_scalar(den, edges_den, 0.0, -BIG, ALU.is_equal, ALU.mult))
                c.link(dve.tensor_tensor(den, den, edges_top, ALU.add))
                c.link(dve.tensor_tensor(top_all, den, own_logits[:], ALU.max))
                c.mark(dve.tensor_tensor(share[0], den, top_all, ALU.subtract))
                c.link(dve.tensor_tensor(share[1], own_logits[:], top_all, ALU.subtract))
                dve.sem_inc(shares_in, 1)
                dve.wait_ge(shares_in, 2)
                c.link(dve.tensor_tensor(den, edges_den, share[0], ALU.mult))
                c.link(dve.scalar_tensor_tensor(out=den, in0=den, scalar=1e-16, in1=share[1], op0=ALU.add, op1=ALU.add))
                c.link(dve.reciprocal(den, den))
                for n in range(2):
                    c.mark(dve.tensor_tensor(share[n], share[n], den, ALU.mult))
                dve.wait_ge(c.sem, c.n)
                dve.sem_inc(shares, 1)
                dve.wait_ge(final_loads, 16)

                def value(t):
                    rows = rows_of(acc, t)
                    dve.tensor_tensor(heads_view(rows), heads_view(rows), head_scale(0, t), ALU.mult).then_inc(sum_weighed, 1)
                    dve.wait_ge(own_weighed, t + 1)
                    dve.tensor_tensor(rows_of(h, t), rows_of(h, t), row_b[:], ALU.add).then_inc(total, 1)
                    dve.wait_ge(sum_weighed, t + 1)
                    dve.wait_ge(total, t + 1)
                    dve.tensor_tensor(rows, rows, rows_of(h, t), ALU.add).then_inc(biased, 1)

                def residual(t, slot):
                    dve.wait_ge(normed, t + 1)
                    dve.tensor_tensor(rows_of(x, t), rows_of(x, t), norm_ring[:, slot, :], ALU.add).then_inc(base, 1)
                    dve.wait_ge(sigmoids, t + 1)
                    dve.tensor_tensor(sig_ring[:, slot, :], sig_ring[:, slot, :], rows_of(acc, t), ALU.mult).then_inc(silu, 1)
                    dve.wait_ge(base, t + 1)
                    dve.wait_ge(silu, t + 1)
                    dve.tensor_tensor(rows_of(x, t), rows_of(x, t), sig_ring[:, slot, :], ALU.add).then_inc(result, 1)

                def both(t, slot, rnd):
                    value(t)
                    residual(t - 1, 1 - slot)
                value(0)
                tile_loop(dve, NODE_TILES - 1, 2, both, first=1)
                residual(NODE_TILES - 1, (NODE_TILES - 1) % 2)


def layouts(a):
    import numpy as np
    pad = EDGE_TILES * P - EDGES
    node_pad = NODE_TILES * P
    src = np.concatenate([a["src"], np.zeros(pad, a["src"].dtype)])
    beyond = np.full(pad + 1, node_pad, a["dst"].dtype)
    before = np.full(1, -1, a["dst"].dtype)
    dst = np.concatenate([before, a["dst"], beyond])
    dst_ext = np.stack([dst[g * P:g * P + P + 2] for g in range(EDGE_TILES)])
    attr = np.concatenate([a["edge_attr_16"], np.zeros((pad, EDGE_DIM), a["edge_attr_16"].dtype)])
    gate = np.concatenate([a["node_vec1"][:, 0], np.zeros(node_pad - NODES, a["node_vec1"].dtype)])

    def features_on_partitions(w):
        return np.ascontiguousarray(w.reshape(CHUNKS, P, -1).transpose(1, 0, 2))

    return {
        "x": a["x"],
        "dst_all": dst[1:-1].reshape(P, EDGE_TILES),
        "dst_ext": dst_ext,
        "src_tiles": src.reshape(EDGE_TILES, P),
        "edge_attr": attr.reshape(EDGE_TILES, P * EDGE_DIM),
        "attr_t": np.ascontiguousarray(attr.T).reshape(P, ATTR_COLS),
        "gate": np.ascontiguousarray(gate.reshape(NODE_TILES, P).T),
        "l2_src": np.ascontiguousarray(a["src"][:node_pad].reshape(NODE_TILES, P).T),
        "l2_dst": np.ascontiguousarray(a["dst"][:node_pad].reshape(NODE_TILES, P).T),
        "l0_w": features_on_partitions(a["L0_gnn_W"]),
        "l0_attn": np.concatenate([a["L0_gnn_attn_l"], a["L0_gnn_attn_r"], a["L0_gnn_bias"]]).reshape(1, 6),
        "l1_w": features_on_partitions(a["L1_gnn_weight"]),
        "l1_bias": a["L1_gnn_bias"].reshape(1, FEAT),
        "l1_norm": np.ascontiguousarray(np.stack([features_on_partitions(a["L1_gnn_" + k])[:, :, 0] for k in (
            "gamma", "beta", "running_mean", "running_var")], axis=1)),
        "l2_w": features_on_partitions(a["L2_gnn_weight"]),
        "l2_wt": features_on_partitions(a["L2_gnn_weight"].T),
        "l2_attn": np.ascontiguousarray(np.stack([a["L2_gnn_attn_l"].reshape(CHUNKS, P).T,
                                                  a["L2_gnn_attn_r"].reshape(CHUNKS, P).T], axis=1)),
        "l3_wl": features_on_partitions(a["L3_gnn_W_l"].T),
        "l3_wlt": features_on_partitions(a["L3_gnn_W_l"]),
        "l3_wr": features_on_partitions(a["L3_gnn_W_r"].T),
        "l3_wrt": features_on_partitions(a["L3_gnn_W_r"]),
        "l3_we": np.ascontiguousarray(a["L3_gnn_W_e"].T),
        "l3_wet": features_on_partitions(a["L3_gnn_W_e"]),
        "l3_bias": np.stack([a["L3_gnn_b_l"], a["L3_gnn_b_r"], a["L3_gnn_bias"]]).reshape(1, 3 * FEAT),
        "l3_bt": np.ascontiguousarray(np.stack([a["L3_gnn_b_l"].reshape(CHUNKS, P).T,
                                                a["L3_gnn_b_r"].reshape(CHUNKS, P).T], axis=1)),
        "l3_att": a["L3_gnn_att"].reshape(1, FEAT),
        "l3_attt": np.ascontiguousarray(a["L3_gnn_att"].reshape(CHUNKS, P).T),
    }


def kernel(**inputs):
    import numpy as np
    import concourse.bacc as bacc
    from concourse.bass_utils import run_bass_kernel_spmd
    arrays = layouts({k: np.asarray(v) for k, v in inputs.items()})
    nc = bacc.Bacc("TRN2", target_bir_lowering=False, num_devices=1)
    io = {k: nc.dram_tensor(f"in_{k}", v.shape, mybir.dt.from_np(v.dtype), kind="ExternalInput").ap()
          for k, v in arrays.items()}
    out = nc.dram_tensor("out", (NODES, FEAT), F32, kind="ExternalOutput").ap()
    build(nc, io, out)
    result = run_bass_kernel_spmd(nc, [{f"in_{k}": v for k, v in arrays.items()}], core_ids=[0])
    return result.results[0]["out"]
```

```python
from contextlib import ExitStack

import concourse.bass as bass
from concourse import mybir

F32 = mybir.dt.float32
BF16 = mybir.dt.bfloat16
I32 = mybir.dt.int32
ALU = mybir.AluOpType
ACT = mybir.ActivationFunctionType
X_AXIS = mybir.AxisListType.X

P = 128
NODES = 3125
EDGES = 53125
FEAT = 256
CHUNKS = FEAT // P
HEADS = 4
HEAD_DIM = FEAT // HEADS
EDGE_DIM = 16
NODE_TILES = -(-NODES // P)
LAST_ROWS = NODES - (NODE_TILES - 1) * P
EDGE_TILES = -(-EDGES // P)
ITEMS = EDGE_TILES + NODE_TILES - 1
BLOCKS = 4
IPB = ITEMS // BLOCKS
BIG = 1.0e30
LN_EPS = 1e-5
BN_EPS = 1e-5
GCN_COLS = FEAT + EDGE_DIM
L2_COLS = FEAT + 2 * HEADS
L3_COLS = FEAT + HEADS
OUT_COLS = FEAT + 2 * HEADS
NEG_GAT, NEG_L2 = 0.2, 0.01
PAIRS = P // EDGE_DIM
ATTR_COLS = EDGE_TILES * EDGE_DIM

assert IPB * BLOCKS == ITEMS and IPB <= P


def flat(ap):
    return ap.rearrange("p a b -> p (a b)")


def tile_loop(eng, count, unroll, body, first=0):
    main = count // unroll
    with eng.Fori(0, main) as i:
        for u in range(unroll):
            body(i * unroll + (first + u), (first + u) % unroll, i + (first + u) // unroll)
    for t in range(first + main * unroll, first + count):
        body(t, t % unroll, t // unroll)


def build(nc, io, out):
    ctx = ExitStack()

    def sb(name, shape, dt=F32):
        return ctx.enter_context(nc.sbuf_tensor(name, shape, dt))

    stage_sems = []

    def sem(name, kept=False):
        s = nc.alloc_semaphore(name=name)
        if not kept:
            stage_sems.append(s)
        return s

    def clear_sems():
        cleared = list(stage_sems)
        stage_sems.clear()
        for s in cleared:
            nc.sync.sem_clear(s)
        return cleared

    def free_sems(cleared):
        for s in cleared:
            nc.release_semaphore(s)

    def dram(name, shape, dt=F32):
        return nc.dram_tensor(name, shape, dt, kind="Internal").ap()

    class Chain:

        def __init__(self, eng, name):
            self.eng, self.sem, self.n = eng, sem(name), 0

        def mark(self, ins):
            self.n += 1
            ins.then_inc(self.sem, 1)

        def link(self, ins):
            self.mark(ins)
            self.eng.wait_ge(self.sem, self.n)

    idle = {e: sem(f"idle_{e}", kept=True) for e in ("act", "pool", "pe", "dve")}

    def hold(eng, who, s, value):
        eng.wait_ge(s, value)
        eng.sem_inc(idle[who], 1)

    with ctx:
        bank = [ctx.enter_context(nc.psum_tensor(f"bank{i}", [P, 512], F32)) for i in range(8)]
        x = sb("x", [P, NODE_TILES, FEAT])
        h = sb("h", [P, NODE_TILES, FEAT])
        acc = sb("acc", [P, NODE_TILES, GCN_COLS])
        xr_parts = sb("xr_parts", [P, NODE_TILES, 3, L3_COLS], BF16)
        ident = sb("ident", [P, P])
        ones = sb("ones", [P, P])
        p_index = sb("p_index", [P, 1])
        iota_b = sb("iota_b", [P, P], BF16)
        iota_t = sb("iota_t", [P, NODE_TILES])
        dst_col = sb("dst_col", [P, ITEMS])
        on_col = sb("on_col", [P, ITEMS])
        last_col = sb("last_col", [P, ITEMS])
        hi_col = sb("hi_col", [P, ITEMS])
        tile_col = sb("tile_col", [P, ITEMS])
        src_idx = sb("src_idx", [P, ITEMS], I32)
        item_tile = sb("item_tile", [1, ITEMS], I32)
        off_col = sb("off_col", [P, ITEMS])
        starts = sb("starts", [IPB, BLOCKS, P])
        keeps = sb("keeps", [IPB, BLOCKS, P])
        lasts = sb("lasts", [IPB, BLOCKS, P])
        starts_row = sb("starts_row", [1, ITEMS])
        keeps_row = sb("keeps_row", [1, ITEMS])
        tile_onehot = sb("tile_onehot", [IPB, BLOCKS, NODE_TILES])
        item_vals = sb("item_vals", [P, 2, ITEMS * HEADS])
        logits = item_vals[:, 0, :].rearrange("p (w h) -> p w h", h=HEADS)
        maxima = item_vals[:, 1, :].rearrange("p (w h) -> p w h", h=HEADS)
        sums_rhs = sb("sums_rhs", [P, ITEMS, 2 * HEADS])
        idx_ring = sb("idx_ring", [P, 2, 8], I32)
        stat = sb("stat", [P, NODE_TILES, 6])
        mean = sb("mean", [P, NODE_TILES])
        rstd = sb("rstd", [P, NODE_TILES])
        shift = sb("shift", [P, NODE_TILES])
        small = [sb(f"small{i}", [P, NODE_TILES]) for i in range(4)]
        eps_col = sb("eps_col", [P, 1])
        dinv = sb("dinv", [P, NODE_TILES])
        g_ring = sb("g_ring", [P, 8, GCN_COLS])
        rings = flat(g_ring[:])
        h_ring = rings[:, 0:2 * FEAT].rearrange("p (s f) -> p s f", s=2)
        ht_ring = rings[:, 512:1024].rearrange("p (s k n) -> p s k n", s=2, k=CHUNKS)
        wbuf = sb("wbuf", [P, CHUNKS, 2 * L3_COLS])
        row_ring = rings[:, 1024:1024 + 2 * L2_COLS].rearrange("p (s f) -> p s f", s=2)
        spare = xr_parts[:].rearrange("p t k f -> p (t k f)")[:, 0:4 * 4096].bitcast(F32)
        work = [spare[:, i * 2048:(i + 1) * 2048] for i in range(4)] + [flat(h[:])[:, 0:2048]]

        item_tile_d = dram("item_tile_d", [ITEMS])
        edge_tile_d = dram("edge_tile_d", [ITEMS], I32)
        dst_rows_d = dram("dst_rows_d", [ITEMS * P], BF16)
        src_rows_d = dram("src_rows_d", [ITEMS * P], BF16)
        edge_attr_d = dram("edge_attr_d", [ITEMS * P, EDGE_DIM])
        attr_parts_d = dram("attr_parts_d", [PAIRS, P, ATTR_COLS], BF16)
        gcn_table = dram("gcn_table", [NODE_TILES * P, FEAT])
        l2_table = dram("l2_table", [NODE_TILES * P, L2_COLS])
        l3_table = dram("l3_table", [NODE_TILES * P, L3_COLS])

        loads = sem("loads", kept=True)
        dst_loaded = sem("dst_loaded")
        consts_i = sem("consts_i")
        pool_chain_s = sem("pool_chain")
        counts_ready = sem("counts_ready")
        sums_ready = sem("sums_ready")
        tile_ready = sem("tile_ready")
        tile_stored = sem("tile_stored")
        group_ready = sem("group_ready")
        lists_in = [sem(f"lists_in{b}", kept=True) for b in range(BLOCKS)]
        attrs_in = [sem(f"attrs_in{b}", kept=True) for b in range(BLOCKS)]
        attrs_out = [sem(f"attrs_out{b}", kept=True) for b in range(BLOCKS)]
        rows_ready = sem("rows_ready")
        rows_stored = sem("rows_stored")
        cols_ready = sem("cols_ready")
        cols_used = sem("cols_used")
        tile_back = sem("tile_back")
        edge_tile_stored = sem("edge_tile_stored")
        conv_done = sem("conv_done")

        dst_all_i = work[0][:, 0:EDGE_TILES].bitcast(I32)
        dst_all = work[0][:, 512:512 + EDGE_TILES]
        counted = work[0][:, 1024:1024 + EDGE_TILES]
        iota_i = sb("iota_i", [P, P], I32)
        items_i = sb("items_i", [IPB, BLOCKS], I32)
        items_f = sb("items_f", [IPB, BLOCKS])
        pidx_i = sb("pidx_i", [P, 1], I32)
        below = sb("below", [P, NODE_TILES])
        below_i = sb("below_i", [P, NODE_TILES], I32)
        passed = work[1][0:IPB, 0:BLOCKS * NODE_TILES].rearrange("p (b t) -> p b t", b=BLOCKS)
        tile_of = sb("tile_of", [IPB, BLOCKS])
        base_of = sb("base_of", [IPB, BLOCKS])
        group_i = sb("group_i", [IPB, BLOCKS], I32)
        lists = flat(h[:])[0:IPB, 2048:6400]
        dst_ext_i = lists[:, 0:520].bitcast(I32).rearrange("p (b e) -> p b e", b=BLOCKS)
        dst_ext = lists[:, 520:1040].rearrange("p (b e) -> p b e", b=BLOCKS)
        src_i = lists[:, 1040:1552].bitcast(I32).rearrange("p (b e) -> p b e", b=BLOCKS)
        lo_i = work[1][0:IPB, 512:1024].bitcast(I32).rearrange("p (b e) -> p b e", b=BLOCKS)
        hi_i = work[1][0:IPB, 1024:1536].bitcast(I32).rearrange("p (b e) -> p b e", b=BLOCKS)
        src_f = work[2][0:IPB, 0:512].rearrange("p (b e) -> p b e", b=BLOCKS)
        hi_f = work[2][0:IPB, 512:1024].rearrange("p (b e) -> p b e", b=BLOCKS)
        loc = work[2][0:IPB, 1024:1536].rearrange("p (b e) -> p b e", b=BLOCKS)
        on = work[2][0:IPB, 1536:2048].rearrange("p (b e) -> p b e", b=BLOCKS)
        tmp = work[1][0:IPB, 1536:2048].rearrange("p (b e) -> p b e", b=BLOCKS)
        lo_b = lists[:, 1600:1856].bitcast(BF16).rearrange("p (b e) -> p b e", b=BLOCKS)
        loc_b = lists[:, 1856:2112].bitcast(BF16).rearrange("p (b e) -> p b e", b=BLOCKS)
        attr_stage = [work[3][0:IPB, :], work[4][0:IPB, :]]
        item_least = sb("item_least", [IPB, 2, BLOCKS])

        with nc.Block() as block:
            @block.sync
            def _(sp):
                sp.dma_start(dst_all_i, io["dst_all"]).then_inc(dst_loaded, 16)
                for t in range(5):
                    n = NODE_TILES // 5
                    if t < 4:
                        sp.dma_start(x[:, t * n:(t + 1) * n, :],
                                     io["x"][t * n * P:(t + 1) * n * P, :].rearrange("(t p) f -> p t f", p=P)
                                     ).then_inc(loads, 16)
                sp.dma_start(x[:, 20:24, :],
                             io["x"][20 * P:24 * P, :].rearrange("(t p) f -> p t f", p=P)).then_inc(loads, 16)
                sp.wait_ge(conv_done, 1)
                sp.dma_start(x[0:LAST_ROWS, NODE_TILES - 1, :], io["x"][(NODE_TILES - 1) * P:NODES, :]
                             ).then_inc(loads, 16)
                sp.wait_ge(tile_ready, 1)
                with nc.allow_non_contiguous_dma(reason="440 numbers, once"):
                    sp.dma_start(item_tile_d.rearrange("(b p) -> p b", b=BLOCKS), tile_of[:]).then_inc(tile_stored, 16)
                sp.wait_ge(tile_stored, 16)
                sp.dma_start(tile_col[:], item_tile_d.unsqueeze(0).broadcast_to([P, ITEMS])).then_inc(tile_back, 16)
                sp.wait_ge(group_ready, 1)
                with nc.allow_non_contiguous_dma(reason="440 numbers, once"):
                    sp.dma_start(edge_tile_d.rearrange("(b p) -> p b", b=BLOCKS), group_i[:]).then_inc(edge_tile_stored, 16)
                sp.wait_ge(edge_tile_stored, 16)
                for b in range(BLOCKS):
                    sp.wait_ge(attrs_in[b], 16)
                    sp.dma_start(edge_attr_d[b * IPB * P:(b + 1) * IPB * P, :].rearrange("(p e) f -> p (e f)", e=P),
                                 attr_stage[b % 2]).then_inc(attrs_out[b], 16)
                sp.wait_ge(rows_ready, 2)
                for d, s in ((dst_rows_d, loc_b), (src_rows_d, lo_b)):
                    sp.dma_start(d.rearrange("(b p e) -> p b e", b=BLOCKS, e=P), s).then_inc(rows_stored, 16)
                sp.wait_ge(rows_stored, 32)
                for b in range(BLOCKS):
                    sp.wait_ge(attrs_out[b], 16)
                sp.wait_ge(loads, 16 * 6)

            @block.gpsimd
            def _(pool):
                pool.iota(iota_i[:], [[1, P]], base=0, channel_multiplier=0).then_inc(consts_i, 1)
                pool.iota(pidx_i[:], [[0, 1]], base=0, channel_multiplier=1).then_inc(consts_i, 1)
                pool.iota(items_i[:], [[IPB, BLOCKS]], base=0, channel_multiplier=1).then_inc(consts_i, 1)
                pool.memset(ident[:], 0.0).then_inc(pool_chain_s, 1)
                pool.wait_ge(pool_chain_s, 1)
                pool.affine_select(out=ident[:], in_=ident[:], compare_op=ALU.not_equal, fill=1.0, base=0,
                                   pattern=[[-1, P]], channel_multiplier=1).then_inc(consts_i, 1)
                pool.wait_ge(group_ready, 1)
                for b in range(BLOCKS):
                    rows = bass.IndirectOffsetOnAxis(ap=group_i[:, b:b + 1], axis=0)
                    pool.indirect_dma_start(dst_ext_i[:, b, :], None, io["dst_ext"], rows).then_inc(lists_in[b], 16)
                    pool.indirect_dma_start(src_i[:, b, :], None, io["src_tiles"], rows).then_inc(lists_in[b], 16)
                for b in range(BLOCKS):
                    rows = bass.IndirectOffsetOnAxis(ap=group_i[:, b:b + 1], axis=0)
                    if b >= 2:
                        pool.wait_ge(attrs_out[b - 2], 16)
                    pool.indirect_dma_start(attr_stage[b % 2], None, io["edge_attr"], rows).then_inc(attrs_in[b], 16)

            @block.vector
            def _(dve):
                c = Chain(dve, "stage1_dve")
                c.mark(dve.memset(ones[:], 1.0))
                c.mark(dve.memset(eps_col[:], LN_EPS))
                dve.memset(x[:, NODE_TILES - 1, :], 0.0).then_inc(conv_done, 1)
                dve.wait_ge(consts_i, 4)
                c.mark(dve.tensor_copy(iota_b[:], iota_i[:]))
                c.mark(dve.tensor_copy(iota_t[:], iota_i[:, 0:NODE_TILES]))
                c.mark(dve.tensor_copy(p_index[:], pidx_i[:]))
                c.mark(dve.tensor_copy(items_f[:], items_i[:]))
                dve.wait_ge(dst_loaded, 16)
                c.link(dve.tensor_copy(dst_all, dst_all_i))
                for t in range(1, NODE_TILES):
                    c.link(dve.tensor_scalar(counted, dst_all, float(t * P), 0.0, ALU.is_lt, ALU.add,
                                             accum_out=below[:, t - 1:t]))
                dve.sem_inc(counts_ready, 1)
                dve.wait_ge(sums_ready, 1)
                last = NODE_TILES - 1
                c.link(dve.tensor_scalar(below_i[:, 0:last], bank[0][:, 0:last], float(P - 1), None, ALU.add))
                c.link(dve.tensor_scalar(below_i[:, 0:last], below_i[:, 0:last], 7, None, ALU.arith_shift_right))
                c.link(dve.tensor_copy(below[:, 0:last], below_i[:, 0:last]))
                c.link(dve.tensor_scalar(below[:, 0:last], below[:, 0:last], -1.0, 0.0, ALU.add, ALU.max))
                c.link(dve.tensor_tensor(below[:, 0:last], below[:, 0:last], iota_t[:, 0:last], ALU.add))
                c.link(dve.tensor_tensor(passed[:, :, 0:last], items_f[:].unsqueeze(2).broadcast_to([IPB, BLOCKS, last]),
                                         below[0:IPB, 0:last].unsqueeze(1).broadcast_to([IPB, BLOCKS, last]), ALU.is_gt))
                c.link(dve.tensor_reduce(tile_of[:], passed[:, :, 0:last], X_AXIS, ALU.add))
                dve.sem_inc(tile_ready, 1)
                c.link(dve.tensor_tensor(group_i[:], items_f[:], tile_of[:], ALU.subtract))
                dve.sem_inc(group_ready, 1)
                c.mark(dve.tensor_tensor(tile_onehot[:], tile_of[:].unsqueeze(2).broadcast_to([IPB, BLOCKS, NODE_TILES]),
                                         iota_t[0:IPB, :].unsqueeze(1).broadcast_to([IPB, BLOCKS, NODE_TILES]), ALU.is_equal))
                c.link(dve.tensor_scalar(base_of[:], tile_of[:], float(P), None, ALU.mult))
                for b in range(BLOCKS):
                    dve.wait_ge(lists_in[b], 32)
                c.link(dve.tensor_copy(dst_ext, dst_ext_i))
                cur = dst_ext[:, :, 1:P + 1]
                c.mark(dve.tensor_copy(src_f, src_i))
                c.mark(dve.tensor_scalar(lo_i, src_i, P - 1, None, ALU.bitwise_and))
                c.mark(dve.tensor_scalar(hi_i, src_i, 7, None, ALU.arith_shift_right))
                c.link(dve.tensor_tensor(loc, cur, base_of[:].unsqueeze(2).broadcast_to([IPB, BLOCKS, P]), ALU.subtract))
                dve.tensor_copy(lo_b, lo_i).then_inc(rows_ready, 1)
                c.mark(dve.tensor_copy(hi_f, hi_i))
                c.link(dve.tensor_scalar(tmp, loc, 0.0, None, ALU.is_ge))
                c.link(dve.scalar_tensor_tensor(out=on, in0=loc, scalar=float(P), in1=tmp, op0=ALU.is_lt, op1=ALU.mult))
                c.link(dve.scalar_tensor_tensor(out=loc, in0=loc, scalar=1.0, in1=on, op0=ALU.add, op1=ALU.mult))
                c.link(dve.tensor_scalar(loc, loc, -1.0, None, ALU.add))
                dve.tensor_copy(loc_b, loc).then_inc(rows_ready, 1)
                c.link(dve.tensor_tensor(tmp, cur, dst_ext[:, :, 0:P], ALU.not_equal))
                c.link(dve.scalar_tensor_tensor(out=starts[:], in0=tmp, scalar=-BIG, in1=on, op0=ALU.mult, op1=ALU.mult))
                c.link(dve.tensor_tensor(tmp, cur, dst_ext[:, :, 2:P + 2], ALU.not_equal))
                c.link(dve.tensor_tensor(lasts[:], tmp, on, ALU.mult))
                c.link(dve.tensor_scalar(keeps[:], lasts[:], -1.0, 1.0, ALU.mult, ALU.add))
                c.mark(dve.tensor_reduce(item_least[:, 0, :], starts[:], X_AXIS, ALU.min))
                c.link(dve.tensor_reduce(item_least[:, 1, :], keeps[:], X_AXIS, ALU.min))
                dve.sem_inc(cols_ready, 1)
                for n, table in enumerate((dst_col, on_col, last_col, src_idx, hi_col)):
                    dve.wait_ge(cols_used, n + 1)
                    c.mark(dve.tensor_copy(table[:], bank[1 + n][:, 0:ITEMS]))
                dve.wait_ge(cols_used, 6)
                c.mark(dve.tensor_copy(starts_row[:], bank[6][0:1, 0:ITEMS]))
                c.mark(dve.tensor_copy(keeps_row[:], bank[7][0:1, 0:ITEMS]))
                dve.wait_ge(c.sem, c.n)
                c.mark(dve.tensor_scalar(off_col[:], on_col[:], BIG, -BIG, ALU.mult, ALU.add))
                dve.wait_ge(tile_back, 16)
                c.link(dve.tensor_copy(item_tile[:], tile_col[0:1, :]))

            @block.tensor
            def _(pe):
                pe.wait_ge(counts_ready, 1)
                pe.matmul(bank[0][:, 0:NODE_TILES - 1], ones[:], below[:, 0:NODE_TILES - 1], start=True, stop=True
                          ).then_inc(sums_ready, 1)
                pe.wait_ge(cols_ready, 1)
                for n, rows in enumerate((loc, on, lasts[:], src_f, hi_f)):
                    for b in range(BLOCKS):
                        ins = pe.transpose(bank[1 + n][:, b * IPB:(b + 1) * IPB], rows[:, b, :], ident[0:IPB, 0:IPB])
                    ins.then_inc(cols_used, 1)
                for n in range(2):
                    for b in range(BLOCKS):
                        ins = pe.transpose(bank[6 + n][0:1, b * IPB:(b + 1) * IPB], item_least[:, n, b:b + 1],
                                           ident[0:IPB, 0:IPB])
                ins.then_inc(cols_used, 1)

        class Norm:

            def __init__(self, layer):
                self.var_ready = sem(f"var_ready{layer}")
                self.std_ready = sem(f"std_ready{layer}")
                self.norm_ready = sem(f"norm_ready{layer}")
                self.rows_ready = sem(f"rows_ready{layer}")
                self.turned = sem(f"turned{layer}")
                self.turn_free = sem(f"turn_free{layer}")
                self.cols_ready = sem(f"cols_ready{layer}")
                self.projected = sem(f"projected{layer}")
                self.out_free = sem(f"out_free{layer}")

        def norm_statistics(dve, c, s):
            stat_done = c.sem
            before = c.n

            def one(t, slot, rnd):
                dve.bn_stats(stat[:, bass.ds(t, 1), :].rearrange("p a k -> p (a k)"),
                             x[:, bass.ds(t, 1), :].rearrange("p a f -> p (a f)")).then_inc(stat_done, 1)
            tile_loop(dve, NODE_TILES, 5, one)
            c.n = before + NODE_TILES
            dve.wait_ge(stat_done, c.n)
            even, odd = 1, 4
            c.mark(dve.tensor_tensor(mean[:], stat[:, :, even], stat[:, :, odd], ALU.add))
            c.mark(dve.tensor_tensor(small[1][:], stat[:, :, even + 1], stat[:, :, odd + 1], ALU.add))
            c.link(dve.tensor_tensor(small[0][:], stat[:, :, even], stat[:, :, odd], ALU.subtract))
            c.link(dve.tensor_tensor(small[0][:], small[0][:], small[0][:], ALU.mult))
            dve.scalar_tensor_tensor(out=small[1][:], in0=small[0][:], scalar=FEAT / 4, in1=small[1][:],
                                     op0=ALU.mult, op1=ALU.add).then_inc(s.var_ready, 1)
            dve.wait_ge(s.std_ready, 1)
            c.link(dve.reciprocal(rstd[:], small[2][:]))
            dve.scalar_tensor_tensor(out=shift[:], in0=mean[:], scalar=-0.5, in1=rstd[:],
                                     op0=ALU.mult, op1=ALU.mult).then_inc(s.norm_ready, 1)

        def norm_rows(act, s, keep=None):
            act.wait_ge(s.var_ready, 1)
            act.activation(small[2][:], small[1][:], ACT.Sqrt, bias=eps_col[:], scale=1.0 / FEAT).then_inc(s.std_ready, 1)
            act.wait_ge(s.norm_ready, 1)

            def one(t, slot, rnd):
                tile_x = x[:, bass.ds(t, 1), :].rearrange("p a f -> p (a f)")
                kw = dict(bias=shift[:, bass.ds(t, 1)], scale=rstd[:, bass.ds(t, 1)])
                if keep is not None:
                    act.activation(keep[:, bass.ds(t, 1), :].rearrange("p a f -> p (a f)"), tile_x, ACT.Relu, **kw)
                if not (isinstance(t, int) and t < 2):
                    hold(act, "act", s.turned, t - 1)
                act.activation(h_ring[:, slot, :], tile_x, ACT.Relu, **kw).then_inc(s.rows_ready, 1)
            one(0, 0, 0)
            one(1, 1, 0)
            tile_loop(act, NODE_TILES - 2, 2, one, first=2)

        def project(pe, s, groups, bias=None):
            def turn(t, slot, rnd):
                pe.wait_ge(s.rows_ready, t + 1)
                pe.wait_ge(s.turn_free, t + 1)
                for k in range(CHUNKS):
                    ins = pe.transpose(bank[slot][:, k * P:(k + 1) * P], h_ring[:, slot, k * P:(k + 1) * P], ident[:])
                ins.then_inc(s.turned, 1)

            def multiply(t, slot, rnd):
                pe.wait_ge(s.cols_ready, t + 1)
                pe.wait_ge(s.out_free, t + 1)
                for b, lo, hi in groups:
                    for k in range(CHUNKS):
                        ins = pe.matmul(bank[2 + slot * len(groups) + b][:, 0:hi - lo], ht_ring[:, slot, k, :],
                                        wbuf[:, k, lo:hi], start=(k == 0), stop=(k == CHUNKS - 1 and bias is None))
                    if bias is not None:
                        ins = pe.matmul(bank[2 + slot * len(groups) + b][:, 0:hi - lo], ones[0:1, :],
                                        bias[0:1, lo:hi], start=False, stop=True)
                ins.then_inc(s.projected, 1)

            def both(t, slot, rnd):
                turn(t, slot, rnd)
                multiply(t - 1, 1 - slot, rnd)
            turn(0, 0, 0)
            tile_loop(pe, NODE_TILES - 1, 2, both, first=1)
            multiply(NODE_TILES - 1, (NODE_TILES - 1) % 2, 0)

        def read_out(dve, s, copy_cols, finish):
            dve.sem_inc(s.turn_free, 2)
            dve.sem_inc(s.out_free, 2)

            def cols(t, slot, rnd):
                dve.wait_ge(s.turned, t + 1)
                if not (isinstance(t, int) and t < 2):
                    dve.wait_ge(s.projected, t - 1)
                copy_cols(slot).then_inc(s.cols_ready, 1)
                dve.wait_ge(s.cols_ready, t + 1)
                dve.sem_inc(s.turn_free, 1)

            def both(t, slot, rnd):
                cols(t, slot, rnd)
                dve.wait_ge(s.projected, t)
                finish(t - 1, 1 - slot, rnd - 1 + slot)
            cols(0, 0, 0)
            both(1, 1, 0)
            tile_loop(dve, NODE_TILES - 2, 2, both, first=2)
            dve.wait_ge(s.projected, NODE_TILES)
            finish(NODE_TILES - 1, (NODE_TILES - 1) % 2, (NODE_TILES - 1) // 2)

        def plain_cols(dve):
            return lambda slot: dve.tensor_copy(flat(ht_ring[:, slot, :, :]), bank[slot][:, 0:FEAT])

        run_max = flat(acc[:])[0:IPB, 0:2048].rearrange("p (g e) -> p g e", e=P)
        seg_max = flat(acc[:])[0:IPB, 2048:4096].rearrange("p (g e) -> p g e", e=P)
        lasts_max = flat(acc[:])[0:IPB, 4096:6144].rearrange("p (g e) -> p g e", e=P)
        ends = flat(acc[:])[0:IPB, 6144:6160]
        carries = flat(acc[:])[0:IPB, 6160:6176]
        states = rings[0:1, 0:HEADS * (ITEMS + 1)].rearrange("p (h w) -> p h w", h=HEADS)

        class Segments:
            def __init__(self, name):
                self.rows = sem(f"seg_rows_{name}")
                self.ends = sem(f"seg_ends_{name}")
                self.turned = sem(f"seg_turned_{name}")
                self.states = sem(f"seg_states_{name}")
                self.carried = sem(f"seg_carried_{name}")
                self.found = sem(f"seg_found_{name}")
                self.cols = sem(f"seg_cols_{name}")

        def segment_max_pe(pe, s, values, heads, ready):
            pe.wait_ge(ready, 1)
            for hd in range(heads):
                for b in range(BLOCKS):
                    ins = pe.transpose(bank[hd][0:IPB, b * P:(b + 1) * P], values[:, b * IPB:(b + 1) * IPB, hd], ident[:])
                ins.then_inc(s.rows, 1)
            for way in range(2):
                pe.wait_ge(s.ends, way + 1)
                for hd in range(heads):
                    for b in range(BLOCKS):
                        g = hd * BLOCKS + b
                        ins = pe.transpose(bank[4 + hd][0:1, b * IPB:(b + 1) * IPB], ends[:, g:g + 1], ident[0:IPB, 0:IPB])
                ins.then_inc(s.turned, 1)
                pe.wait_ge(s.states, way + 1)
                for hd in range(heads):
                    for b in range(BLOCKS):
                        g = hd * BLOCKS + b
                        at = b * IPB + way
                        ins = pe.transpose(bank[4][0:IPB, g:g + 1], states[:, hd, at:at + IPB], ident[0:1, 0:1])
                ins.then_inc(s.carried, 1)
            pe.wait_ge(s.found, 1)
            for hd in range(heads):
                for b in range(BLOCKS):
                    ins = pe.transpose(bank[hd][:, b * IPB:(b + 1) * IPB], seg_max[:, hd * BLOCKS + b, :],
                                       ident[0:IPB, 0:IPB])
                ins.then_inc(s.cols, 1)

        def segment_max_dve(dve, c, s, result, heads):
            groups = [(hd, b) for hd in range(heads) for b in range(BLOCKS)]
            n = len(groups)

            def forward(initial):
                for g, (hd, b) in enumerate(groups):
                    c.mark(dve.tensor_tensor_scan(run_max[:, g, :], starts[:, b, :], bank[hd][0:IPB, b * P:(b + 1) * P],
                                                  initial(g), ALU.add, ALU.max))
                dve.wait_ge(c.sem, c.n)

            def backward(initial):
                for g, (hd, b) in enumerate(groups):
                    c.mark(dve.tensor_tensor_scan(seg_max[:, g, ::-1], keeps[:, b, ::-1], lasts_max[:, g, ::-1],
                                                  initial(g), ALU.mult, ALU.add))
                dve.wait_ge(c.sem, c.n)

            dve.wait_ge(s.rows, heads)
            forward(lambda g: -BIG)
            dve.tensor_copy(ends[:, 0:n], run_max[:, 0:n, P - 1]).then_inc(s.ends, 1)
            c.link(dve.memset(states[:, 0:heads, 0:1], -BIG))
            dve.wait_ge(s.turned, 1)
            for hd in range(heads):
                c.mark(dve.tensor_tensor_scan(states[:, hd, 1:ITEMS + 1], starts_row[:], bank[4 + hd][0:1, 0:ITEMS],
                                              -BIG, ALU.add, ALU.max))
            dve.wait_ge(c.sem, c.n)
            dve.sem_inc(s.states, 1)
            dve.wait_ge(s.carried, 1)
            c.link(dve.tensor_copy(carries[:, 0:n], bank[4][0:IPB, 0:n]))
            forward(lambda g: carries[:, g:g + 1])
            for hd in range(heads):
                c.mark(dve.tensor_tensor(lasts_max[:, hd * BLOCKS:(hd + 1) * BLOCKS, :], lasts[:],
                                         run_max[:, hd * BLOCKS:(hd + 1) * BLOCKS, :], ALU.mult))
            dve.wait_ge(c.sem, c.n)
            backward(lambda g: 0.0)
            dve.tensor_copy(ends[:, 0:n], seg_max[:, 0:n, 0]).then_inc(s.ends, 1)
            c.link(dve.memset(states[:, 0:heads, ITEMS:ITEMS + 1], 0.0))
            dve.wait_ge(s.turned, 2)
            for hd in range(heads):
                c.mark(dve.tensor_tensor_scan(states[:, hd, 0:ITEMS][:, ::-1], keeps_row[:, ::-1],
                                              bank[4 + hd][0:1, 0:ITEMS][:, ::-1], 0.0, ALU.mult, ALU.add))
            dve.wait_ge(c.sem, c.n)
            dve.sem_inc(s.states, 1)
            dve.wait_ge(s.carried, 2)
            c.link(dve.tensor_copy(carries[:, 0:n], bank[4][0:IPB, 0:n]))
            backward(lambda g: carries[:, g:g + 1])
            dve.sem_inc(s.found, 1)
            for hd in range(heads):
                dve.wait_ge(s.cols, hd + 1)
                c.mark(dve.tensor_copy(result[:, :, hd], bank[hd][:, 0:ITEMS]))
            dve.wait_ge(c.sem, c.n)

        s0 = Norm(0)
        l0_loads = sem("l0_loads")
        attn = sb("attn", [P, 6])
        gate = sb("gate", [P, NODE_TILES])
        z = sb("z", [P, NODE_TILES, 2])
        node_vals = sb("node_vals", [P, 4, NODE_TILES])
        node_rest = sb("node_rest", [P, 2, 4 * NODE_TILES])
        node_parts = sb("node_parts", [P, 3, 4 * NODE_TILES], BF16)

        with nc.Block() as block:
            @block.sync
            def _(sp):
                sp.dma_start(wbuf[:, :, 0:2], io["l0_w"]).then_inc(l0_loads, 16)
                sp.dma_start(attn[:], io["l0_attn"].broadcast_to([P, 6])).then_inc(l0_loads, 16)
                sp.dma_start(gate[:], io["gate"]).then_inc(l0_loads, 16)
                sp.wait_ge(l0_loads, 48)

            @block.scalar
            def _(act):
                norm_rows(act, s0, keep=h)

            @block.tensor
            def _(pe):
                pe.wait_ge(l0_loads, 48)
                project(pe, s0, [(0, 0, 2)])

            @block.vector
            def _(dve):
                c = Chain(dve, "stage2_dve")
                norm_statistics(dve, c, s0)

                def keep_z(t, slot, rnd):
                    dve.tensor_copy(z[:, bass.ds(t, 1), :].rearrange("p a k -> p (a k)"), bank[2 + slot][:, 0:2]
                                    ).then_inc(s0.out_free, 1)
                read_out(dve, s0, plain_cols(dve), keep_z)
                dve.wait_ge(s0.out_free, 2 + NODE_TILES)
                dve.wait_ge(l0_loads, 48)
                for k in range(2):
                    c.mark(dve.tensor_copy(node_vals[:, 1 + k, :], z[:, :, k]))
                for row, at in ((0, 0), (3, 2)):
                    c.link(dve.tensor_scalar(node_vals[:, row, :], z[:, :, 0], attn[:, at:at + 1], None, ALU.mult))
                    c.link(dve.scalar_tensor_tensor(out=node_vals[:, row, :], in0=z[:, :, 1], scalar=attn[:, at + 1:at + 2],
                                                    in1=node_vals[:, row, :], op0=ALU.mult, op1=ALU.add))
                whole = flat(node_vals[:])
                c.link(dve.tensor_copy(node_parts[:, 0, :], whole))
                c.link(dve.tensor_tensor(node_rest[:, 0, :], whole, node_parts[:, 0, :], ALU.subtract))
                c.link(dve.tensor_copy(node_parts[:, 1, :], node_rest[:, 0, :]))
                c.link(dve.tensor_tensor(node_rest[:, 1, :], node_rest[:, 0, :], node_parts[:, 1, :], ALU.subtract))
                c.link(dve.tensor_copy(node_parts[:, 2, :], node_rest[:, 1, :]))

        CHUNK = 4
        CHUNK_EDGES = CHUNK * P
        EDGE_CHUNKS = ITEMS // CHUNK
        VALS = 3 * NODE_TILES
        ROW_SLOTS = 4
        edge_rows = flat(acc[:])[:, 3072:3072 + ROW_SLOTS * CHUNK_EDGES].bitcast(BF16).rearrange(
            "p (s k e) -> p s k e", s=ROW_SLOTS, k=2)
        place_ring = sb("place_ring", [P, 2, 2, CHUNK_EDGES], BF16)
        picked = flat(acc[:])[:, 200:800].rearrange("p (s u v n) -> p s u v n", s=2, u=CHUNK, v=3)
        er_parts = flat(acc[:])[:, 800:800 + 3 * ITEMS // 2].bitcast(BF16).rearrange("p (w k) -> p w k", k=3)
        er_rest = spare[:, 0:2 * ITEMS].rearrange("p (k w) -> p k w", k=2)
        er_picked = spare[:, 2048:2048 + 3 * ITEMS].rearrange("p (w k) -> p w k", k=3)
        er_edges = spare[:, 3584:3584 + ITEMS]
        er_turned = spare[0:NODE_TILES, 1024:1024 + P]
        tiles_turned = spare[0:NODE_TILES, 1280:1280 + ITEMS]
        er_items = bank[7][:, 0:ITEMS]
        edge_vals = maxima
        er_turned_ready = sem("er_turned_ready")
        er_rows_ready = sem("er_rows_ready")
        er_items_ready = sem("er_items_ready")
        er_split = sem("er_split")
        rows_in = [sem(f"rows_in{u}") for u in range(ROW_SLOTS)]
        place_ready = sem("place_ready")
        vals_ready = sem("vals_ready")
        masks_done = sem("masks_done")
        picks_done = sem("picks_done")
        reduced = sem("reduced")

        SPLIT = 512
        SPLITS = ATTR_COLS // SPLIT
        split_memory = spare[:, 4096:]
        attr_in = split_memory[:, 0:2 * SPLIT].rearrange("p (s c) -> p s c", s=2)
        attr_rest = split_memory[:, 1024:1024 + 4 * SPLIT].rearrange("p (s k c) -> p s k c", s=2, k=2)
        attr_parts = flat(acc[:])[:, 1536:1536 + 3 * SPLIT].bitcast(BF16).rearrange("p (s k c) -> p s k c", s=2, k=3)
        attr_loaded = [sem(f"attr_loaded{u}") for u in range(2)]
        part_ready = sem("part_ready")
        MASKS = EDGE_CHUNKS // SPLITS
        off_tile = flat(g_ring[:])[:, 0:400].rearrange("p (s k u n) -> p s k u n", s=2, k=2, u=CHUNK)
        tile_mask = flat(g_ring[:])[:, 400:400 + MASKS * CHUNK * NODE_TILES].rearrange("p (s u n) -> p s u n", s=MASKS, u=CHUNK)
        distances = sem("distances")
        rest_made = sem("rest_made")
        parts_out = [sem(f"parts_out{u}") for u in range(2)]

        with nc.Block() as block:
            @block.scalar
            def _(act):
                def load_attrs(t, slot):
                    act.dma_start(attr_in[:, slot, :], io["attr_t"][:, bass.ds(t * SPLIT, SPLIT)]).then_inc(attr_loaded[slot], 16)

                def split(t, slot, rnd, more=True):
                    act.wait_ge(attr_loaded[slot], rnd * 16 + 16)
                    if not (isinstance(t, int) and t < 2):
                        act.wait_ge(parts_out[slot], rnd * 48)
                    act.copy(attr_parts[:, slot, 0, :], attr_in[:, slot, :]).then_inc(part_ready, 1)
                    for k in range(2):
                        act.wait_ge(rest_made, t * 2 + (k + 1))
                        act.copy(attr_parts[:, slot, k + 1, :], attr_rest[:, slot, k, :]).then_inc(part_ready, 1)
                    act.wait_ge(part_ready, t * 3 + 3)
                    for k, (lo, hi) in enumerate(((0, 3), (3, 6), (6, PAIRS))):
                        act.dma_start(attr_parts_d[lo:hi, :, bass.ds(t * SPLIT, SPLIT)].rearrange("b p c -> p b c"),
                                      attr_parts[:, slot, k:k + 1, :].broadcast_to([P, hi - lo, SPLIT])).then_inc(parts_out[slot], 16)
                    if more:
                        load_attrs(t + 2, slot)

                def mask(t, slot):
                    if not (isinstance(t, int) and t < MASKS):
                        act.wait_ge(picks_done, t - (MASKS - 1))
                    act.wait_ge(distances, t * 2 + 2)
                    act.activation(tile_mask[:, slot, :, :], off_tile[:, slot % 2, 1, :, :], ACT.Relu, scale=-1.0, bias=ones[:, 0:1]
                                   ).then_inc(masks_done, 1)

                def masks_and_split(t, slot, rnd, more=True):
                    for m in range(MASKS):
                        mask(t * MASKS + m, m)
                    split(t, slot, rnd, more)
                load_attrs(0, 0)
                load_attrs(1, 1)
                masks_and_split(0, 0, 0)
                masks_and_split(1, 1, 0)
                tile_loop(act, SPLITS - 5, 2, masks_and_split, first=2)
                for t in range(SPLITS - 3, SPLITS):
                    masks_and_split(t, t % 2, t // 2, more=t + 2 < SPLITS)
                for t in range(MASKS * SPLITS, EDGE_CHUNKS):
                    mask(t, t % MASKS)
                for u in range(2):
                    act.wait_ge(parts_out[u], (SPLITS + 1 - u) // 2 * 48)

            @block.gpsimd
            def _(pool):
                def rest(t, slot, rnd):
                    for k in range(2):
                        pool.wait_ge(part_ready, t * 3 + (k + 1))
                        pool.tensor_tensor(attr_rest[:, slot, k, :], (attr_in[:, slot, :], attr_rest[:, slot, 0, :])[k],
                                           attr_parts[:, slot, k, :], ALU.subtract).then_inc(rest_made, 1)
                def distance(t, slot):
                    if not (isinstance(t, int) and t < 2):
                        hold(pool, "pool", masks_done, t - 1)
                    pool.tensor_tensor(off_tile[:, slot, 0, :, :],
                                       hi_col[:, bass.ds(t * CHUNK, CHUNK)].unsqueeze(2).broadcast_to([P, CHUNK, NODE_TILES]),
                                       iota_t[:].unsqueeze(1).broadcast_to([P, CHUNK, NODE_TILES]), ALU.subtract
                                       ).then_inc(distances, 1)
                    pool.wait_ge(distances, t * 2 + 1)
                    pool.tensor_tensor(off_tile[:, slot, 1, :, :], off_tile[:, slot, 0, :, :], off_tile[:, slot, 0, :, :], ALU.mult
                                       ).then_inc(distances, 1)

                def distances_and_rest(t, slot, rnd):
                    for m in range(MASKS):
                        distance(t * MASKS + m, m % 2)
                    rest(t, slot, rnd)
                distances_and_rest(0, 0, 0)
                distances_and_rest(1, 1, 0)
                tile_loop(pool, SPLITS - 2, 2, distances_and_rest, first=2)
                for t in range(MASKS * SPLITS, EDGE_CHUNKS):
                    distance(t, t % 2)

            @block.sync
            def _(sp):
                def load(t, slot, rnd):
                    if not (isinstance(t, int) and t < ROW_SLOTS):
                        sp.wait_ge(place_ready, t - (ROW_SLOTS - 1))
                    for k, d in enumerate((src_rows_d, dst_rows_d)):
                        sp.dma_start(edge_rows[:, slot, k, :],
                                     d[bass.ds(t * CHUNK_EDGES, CHUNK_EDGES)].unsqueeze(0).broadcast_to([P, CHUNK_EDGES])
                                     ).then_inc(rows_in[slot], 16)
                for t in range(ROW_SLOTS):
                    load(t, t, 0)
                tile_loop(sp, EDGE_CHUNKS - ROW_SLOTS, ROW_SLOTS, load, first=ROW_SLOTS)

            @block.tensor
            def _(pe):
                pe.transpose(bank[6][0:NODE_TILES, 0:P], node_vals[:, 3, :], ident[:])
                for b in range(BLOCKS):
                    ins = pe.transpose(bank[4][0:NODE_TILES, b * IPB:(b + 1) * IPB], tile_onehot[:, b, :], ident[0:IPB, 0:IPB])
                ins.then_inc(er_turned_ready, 1)
                pe.wait_ge(er_rows_ready, 1)
                pe.matmul(er_items, er_turned, tiles_turned, start=True, stop=True).then_inc(er_items_ready, 1)
                pe.wait_ge(er_split, 1)

                def pick(t, slot, rnd):
                    pe.wait_ge(place_ready, t + 1)
                    if not (isinstance(t, int) and t < 2):
                        pe.wait_ge(picks_done, t - 1)
                    for u in range(CHUNK):
                        e = slice(u * P, (u + 1) * P)
                        for part in range(3):
                            pe.matmul(bank[slot][:, u * VALS:(u + 1) * VALS], place_ring[:, slot, 0, e],
                                      node_parts[:, part, 0:VALS], start=(part == 0), stop=(part == 2))
                        ins = pe.matmul(bank[slot][:, CHUNK * VALS + u * 3:CHUNK * VALS + u * 3 + 3], place_ring[:, slot, 1, e],
                                        er_parts[:, bass.ds(t * CHUNK + u, 1), :].rearrange("p a k -> p (a k)"), start=True, stop=True)
                    ins.then_inc(vals_ready, 1)
                pick(0, 0, 0)
                pick(1, 1, 0)
                tile_loop(pe, EDGE_CHUNKS - 2, 2, pick, first=2)

            @block.vector
            def _(dve):
                c = Chain(dve, "stage3_dve")
                dve.wait_ge(er_turned_ready, 1)
                c.mark(dve.tensor_copy(er_turned, bank[6][0:NODE_TILES, 0:P]))
                c.link(dve.tensor_copy(tiles_turned, bank[4][0:NODE_TILES, 0:ITEMS]))
                dve.sem_inc(er_rows_ready, 1)
                dve.wait_ge(er_items_ready, 1)
                c.link(dve.tensor_copy(er_parts[:, :, 0], er_items))
                c.link(dve.tensor_tensor(er_rest[:, 0, :], er_items, er_parts[:, :, 0], ALU.subtract))
                c.link(dve.tensor_copy(er_parts[:, :, 1], er_rest[:, 0, :]))
                c.link(dve.tensor_tensor(er_rest[:, 1, :], er_rest[:, 0, :], er_parts[:, :, 1], ALU.subtract))
                c.link(dve.tensor_copy(er_parts[:, :, 2], er_rest[:, 1, :]))
                dve.sem_inc(er_split, 1)

                def places(t, slot, row_slot, rnd):
                    dve.wait_ge(rows_in[row_slot], rnd * 32 + 32)
                    if not (isinstance(t, int) and t < 2):
                        dve.wait_ge(vals_ready, t - 1)
                    dve.tensor_scalar(place_ring[:, slot, :, :].rearrange("p k e -> p (k e)"),
                                      edge_rows[:, row_slot, :, :].rearrange("p k e -> p (k e)"),
                                      p_index[:], None, ALU.is_equal).then_inc(place_ready, 1)

                def pick(t, mask_slot):
                    slot = mask_slot % 2
                    dve.wait_ge(vals_ready, t + 1)
                    dve.wait_ge(masks_done, t + 1)
                    if not (isinstance(t, int) and t < 2):
                        dve.wait_ge(reduced, t - 1)
                    dve.tensor_tensor(picked[:, slot, :, :, :], bank[slot][:, 0:CHUNK * VALS].rearrange("p (u v n) -> p u v n", u=CHUNK, v=3),
                                      tile_mask[:, mask_slot, :, :].unsqueeze(2).broadcast_to([P, CHUNK, 3, NODE_TILES]), ALU.mult)
                    dve.tensor_copy(er_picked[:, bass.ds(t * CHUNK, CHUNK), :].rearrange("p u k -> p (u k)"),
                                    bank[slot][:, CHUNK * VALS:CHUNK * VALS + CHUNK * 3]).then_inc(picks_done, 1)

                def add(t, slot):
                    hold(dve, "dve", picks_done, t + 1)
                    dve.tensor_reduce(edge_vals[:, bass.ds(t * CHUNK, CHUNK), 0:3], picked[:, slot, :, :, :], X_AXIS, ALU.add
                                      ).then_inc(reduced, 1)

                def three(t, u, rnd):
                    places(t, u % 2, u % ROW_SLOTS, rnd * (MASKS // ROW_SLOTS) + u // ROW_SLOTS)
                    pick(t - 1, (u - 1) % MASKS)
                    add(t - 2, u % 2)
                places(0, 0, 0, 0)
                places(1, 1, 1, 0)
                pick(0, 0)
                three(2, 2, 0)
                three(3, 3, 0)
                tile_loop(dve, EDGE_CHUNKS - 4, MASKS, three, first=4)
                pick(EDGE_CHUNKS - 1, (EDGE_CHUNKS - 1) % MASKS)
                for t in (EDGE_CHUNKS - 2, EDGE_CHUNKS - 1):
                    add(t, t % 2)

        seg0 = Segments("l0")
        sum_parts = flat(item_vals[:])[:, 0:ITEMS * 6].bitcast(BF16).rearrange("p (w k v) -> p w k v", k=3, v=4)
        sum_rests = [flat(acc[:])[:, k * ITEMS * 4:(k + 1) * ITEMS * 4].rearrange("p (w v) -> p w v", v=4) for k in range(2)]
        masked0 = sem("masked0")
        less0 = sem("less0")
        exp0 = sem("exp0")
        scores = logits[:, :, 0:1]
        top = logits[:, :, 1:2]

        with nc.Block() as block:
            @block.tensor
            def _(pe):
                segment_max_pe(pe, seg0, scores, 1, masked0)

            @block.scalar
            def _(act):
                act.wait_ge(less0, 1)
                act.activation(sums_rhs[:, :, 0], logits[:, :, 2], ACT.Exp).then_inc(exp0, 1)

            @block.vector
            def _(dve):
                c = Chain(dve, "stage4_dve")
                el, z0, z1 = (edge_vals[:, :, k] for k in range(3))
                c.link(dve.tensor_tensor(er_edges, er_picked[:, :, 0], er_picked[:, :, 1], ALU.add))
                c.link(dve.tensor_tensor(er_edges, er_edges, er_picked[:, :, 2], ALU.add))
                score = logits[:, :, 0]
                c.link(dve.tensor_tensor(score, er_edges, el, ALU.add))
                c.link(dve.scalar_tensor_tensor(out=score, in0=score, scalar=NEG_GAT, in1=score, op0=ALU.mult, op1=ALU.max))
                c.link(dve.tensor_tensor(score, score, off_col[:], ALU.add))
                dve.sem_inc(masked0, 1)
                segment_max_dve(dve, c, seg0, top, 1)
                dve.tensor_tensor(logits[:, :, 2], score, logits[:, :, 1], ALU.subtract).then_inc(less0, 1)
                c.mark(dve.memset(sums_rhs[:, :, 3], 1.0))
                dve.wait_ge(exp0, 1)
                c.mark(dve.tensor_tensor(sums_rhs[:, :, 1], sums_rhs[:, :, 0], z0, ALU.mult))
                c.link(dve.tensor_tensor(sums_rhs[:, :, 2], sums_rhs[:, :, 0], z1, ALU.mult))
                c.link(dve.tensor_copy(sum_parts[:, :, 0, :], sums_rhs[:, :, 0:4]))
                c.link(dve.tensor_tensor(sum_rests[0], sums_rhs[:, :, 0:4], sum_parts[:, :, 0, :], ALU.subtract))
                c.link(dve.tensor_copy(sum_parts[:, :, 1, :], sum_rests[0]))
                c.link(dve.tensor_tensor(sum_rests[1], sum_rests[0], sum_parts[:, :, 1, :], ALU.subtract))
                c.link(dve.tensor_copy(sum_parts[:, :, 2, :], sum_rests[1]))

        onehot = sb("onehot", [P, 8, P])
        GROUP = 8
        onehot_b = flat(onehot[:]).bitcast(BF16).rearrange("p (u n) -> p u n", n=P)
        sums_by_part = spare[:, 0:ITEMS * 12].rearrange("p (w k v) -> p w k v", k=3, v=4)
        item_sums = sum_rests[0]
        onehot_ready = sem("onehot_ready")
        sums_ready0 = sem("sums_ready0")
        sums_free0 = sem("sums_free0")

        with nc.Block() as block:
            @block.vector
            def _(dve):
                c = Chain(dve, "stage5_dve")

                def make(t, slot, rnd):
                    if not (isinstance(t, int) and t < 2):
                        dve.wait_ge(sums_ready0, t - 1)
                    dve.tensor_tensor(onehot_b[:, slot * GROUP:(slot + 1) * GROUP, :],
                                      iota_b[:].unsqueeze(1).broadcast_to([P, GROUP, P]),
                                      dst_col[:, bass.ds(t * GROUP, GROUP)].unsqueeze(2).broadcast_to([P, GROUP, P]),
                                      ALU.is_equal).then_inc(onehot_ready, 1)
                make(0, 0, 0)
                make(1, 1, 0)
                tile_loop(dve, ITEMS // GROUP - 2, 2, make, first=2)
                dve.wait_ge(sums_free0, 2 + ITEMS // GROUP)
                c.link(dve.tensor_tensor(item_sums, sums_by_part[:, :, 2, :], sums_by_part[:, :, 1, :], ALU.add))
                c.link(dve.tensor_tensor(item_sums, item_sums, sums_by_part[:, :, 0, :], ALU.add))

            @block.tensor
            def _(pe):
                def add_up(t, slot, rnd):
                    pe.wait_ge(onehot_ready, t + 1)
                    pe.wait_ge(sums_free0, t + 1)
                    for u in range(GROUP):
                        ins = pe.matmul(bank[slot][:, u * 12:u * 12 + 12], onehot_b[:, slot * GROUP + u, :],
                                        sum_parts[:, bass.ds(t * GROUP + u, 1), :, :].rearrange("p a k v -> p (a k v)"),
                                        start=True, stop=True)
                    ins.then_inc(sums_ready0, 1)
                tile_loop(pe, ITEMS // GROUP, 2, add_up)

            @block.scalar
            def _(act):
                act.sem_inc(sums_free0, 2)

                def keep(t, slot, rnd):
                    hold(act, "act", sums_ready0, t + 1)
                    act.copy(sums_by_part[:, bass.ds(t * GROUP, GROUP), :, :].rearrange("p a k v -> p (a k v)"),
                             bank[slot][:, 0:GROUP * 12]).then_inc(sums_free0, 1)
                tile_loop(act, ITEMS // GROUP, 2, keep)

        s1 = Norm(1)
        l1_loads = sem("l1_loads")
        turned_sums = sem("turned_sums")
        sums_rows = sem("sums_rows")
        node_sums = sem("node_sums")
        squares = sem("squares")
        roots = sem("roots")
        gates_in = sem("gates_in")
        gates = sem("gates")
        norm1 = sb("norm1", [P, 4, CHUNKS])
        bn_scale = sb("bn_scale", [P, CHUNKS])
        bn_shift = sb("bn_shift", [P, CHUNKS])
        bn_root = sb("bn_root", [P, CHUNKS])
        bn_in = sb("bn_in", [P, CHUNKS])
        item_rows = work[1][0:IPB, :].rearrange("p (v b n) -> p v b n", v=4, b=BLOCKS)
        by_node = bank[4][:, 0:4 * NODE_TILES].rearrange("p (v t) -> p v t", v=4)
        degree1 = sb("degree1", [P, NODE_TILES])
        degree_root = sb("degree_root", [P, NODE_TILES])
        gate_arg = sb("gate_arg", [P, NODE_TILES])
        gate_out = sb("gate_out", [P, NODE_TILES])
        gated = sem("gated")
        gcn_stored = sem("gcn_stored")

        with nc.Block() as block:
            @block.sync
            def _(sp):
                sp.dma_start(wbuf[:, :, 0:FEAT], io["l1_w"]).then_inc(l1_loads, 16)
                sp.dma_start(norm1[:], io["l1_norm"]).then_inc(l1_loads, 16)

                def store(t, slot, rnd):
                    sp.wait_ge(s1.out_free, t + 3)
                    sp.dma_start(gcn_table[bass.ds(t * P, P), :],
                                 h[:, bass.ds(t, 1), :].rearrange("p a f -> p (a f)")).then_inc(gcn_stored, 16)
                tile_loop(sp, NODE_TILES, 5, store)
                sp.wait_ge(gcn_stored, 16 * NODE_TILES)

            @block.tensor
            def _(pe):
                for v in range(4):
                    for b in range(BLOCKS):
                        ins = pe.transpose(bank[v][0:IPB, b * P:(b + 1) * P], item_sums[:, b * IPB:(b + 1) * IPB, v], ident[:])
                    ins.then_inc(turned_sums, 1)
                for v in range(4):
                    pe.wait_ge(sums_rows, v + 1)
                    for b in range(BLOCKS):
                        ins = pe.matmul(by_node[:, v, :], item_rows[:, v, b, :], tile_onehot[:, b, :],
                                        start=(b == 0), stop=(b == BLOCKS - 1))
                ins.then_inc(node_sums, 1)
                pe.wait_ge(l1_loads, 32)
                project(pe, s1, [(0, 0, FEAT)])

            @block.scalar
            def _(act):
                act.wait_ge(squares, 1)
                act.activation(degree_root[:], degree1[:], ACT.Sqrt)
                act.activation(bn_root[:], bn_in[:], ACT.Sqrt).then_inc(roots, 1)
                act.wait_ge(gates_in, 1)
                act.activation(gate_out[:], gate_arg[:], ACT.Sigmoid).then_inc(gates, 1)
                norm_rows(act, s1)

            @block.vector
            def _(dve):
                c = Chain(dve, "stage6_dve")
                for v in range(4):
                    dve.wait_ge(turned_sums, v + 1)
                    dve.tensor_copy(item_rows[:, v, :, :].rearrange("p b n -> p (b n)"), bank[v][0:IPB, :]).then_inc(sums_rows, 1)
                dve.wait_ge(l1_loads, 32)
                c.mark(dve.tensor_scalar(bn_in[:], norm1[:, 3, :], BN_EPS, None, ALU.add))
                dve.wait_ge(node_sums, 1)
                c.mark(dve.tensor_scalar(small[0][:], by_node[:, 0, :], 0.0, None, ALU.is_equal))
                c.link(dve.tensor_scalar(degree1[:], by_node[:, 3, :], 1.0, None, ALU.add))
                dve.sem_inc(squares, 1)
                c.link(dve.tensor_tensor(small[0][:], small[0][:], by_node[:, 0, :], ALU.add))
                c.link(dve.reciprocal(small[0][:], small[0][:]))
                for k in range(2):
                    c.link(dve.tensor_tensor(small[1 + k][:], by_node[:, 1 + k, :], small[0][:], ALU.mult))
                    c.link(dve.tensor_scalar(small[1 + k][:], small[1 + k][:], attn[:, 4 + k:5 + k], 0.0, ALU.add, ALU.max))
                c.link(dve.tensor_tensor(gate_arg[:], gate[:], small[1][:], ALU.mult))
                c.link(dve.tensor_tensor(gate_arg[:], gate_arg[:], small[2][:], ALU.add))
                dve.sem_inc(gates_in, 1)
                dve.wait_ge(roots, 1)
                c.mark(dve.reciprocal(dinv[:], degree_root[:]))
                c.link(dve.reciprocal(bn_scale[:], bn_root[:]))
                c.link(dve.tensor_tensor(bn_scale[:], bn_scale[:], norm1[:, 0, :], ALU.mult))
                c.link(dve.tensor_tensor(bn_shift[:], bn_scale[:], norm1[:, 2, :], ALU.mult))
                c.link(dve.tensor_tensor(bn_shift[:], norm1[:, 1, :], bn_shift[:], ALU.subtract))
                dve.wait_ge(gates, 1)

                def add_gated(t, slot, rnd):
                    tile_x = x[:, bass.ds(t, 1), :].rearrange("p a f -> p (a f)")
                    dve.scalar_tensor_tensor(out=tile_x, in0=h[:, bass.ds(t, 1), :].rearrange("p a f -> p (a f)"),
                                             scalar=gate_out[:, bass.ds(t, 1)], in1=tile_x,
                                             op0=ALU.mult, op1=ALU.add).then_inc(gated, 1)
                tile_loop(dve, NODE_TILES, 5, add_gated)
                dve.wait_ge(gated, NODE_TILES)
                norm_statistics(dve, c, s1)

                def batch_norm(slot):
                    for k in range(CHUNKS):
                        ins = dve.tensor_scalar(ht_ring[:, slot, k, :], bank[slot][:, k * P:(k + 1) * P],
                                                bn_scale[:, k:k + 1], bn_shift[:, k:k + 1], ALU.mult, ALU.add)
                    return ins

                def scale(t, slot, rnd):
                    dve.tensor_scalar(h[:, bass.ds(t, 1), :].rearrange("p a f -> p (a f)"), bank[2 + slot][:, 0:FEAT],
                                      dinv[:, bass.ds(t, 1)], None, ALU.mult).then_inc(s1.out_free, 1)
                read_out(dve, s1, batch_norm, scale)

        RING = 8

        early_sems = clear_sems()

        class Gather:

            def __init__(self, name):
                self.index_ready = sem(f"index_ready_{name}")
                self.rows_in = [sem(f"g_rows_in_{name}{u}", kept=True) for u in range(RING)]
                self.rows_used = sem(f"g_rows_used_{name}")

        def gather_rows(pool, g, table, cols, more_waits=None):
            def one_round(t, slot, rnd):
                pool.tensor_copy(idx_ring[:, slot, :], src_idx[:, bass.ds(t * RING, RING)]).then_inc(g.index_ready, 1)
                hold(pool, "pool", g.index_ready, t + 1)
                for u in range(RING):
                    hold(pool, "pool", g.rows_used, t * RING + (u + 1))
                    pool.indirect_dma_start(g_ring[:, u, 0:cols], None, table,
                                            bass.IndirectOffsetOnAxis(ap=idx_ring[:, slot, u:u + 1], axis=0)
                                            ).then_inc(g.rows_in[u], 16)
            tile_loop(pool, ITEMS // RING, 2, one_round)

        g1 = Gather("l1")
        ACC_BANKS = 4
        attrs_landed = [sem(f"attrs_landed{u}") for u in range(2)]
        onehot1 = sem("onehot1")
        acc_done1 = sem("acc_done1")

        def onehots(dve, t, u, used, ready, base):
            if not (isinstance(t, int) and t < 8):
                dve.wait_ge(used, t + (base - 7))
            dve.tensor_scalar(onehot[:, u, :], iota_b[:], dst_col[:, bass.ds(t, 1)], None, ALU.is_equal
                              ).then_inc(ready, 1)

        def item_tiles(eng, t0, n, table=None, top=NODE_TILES - 1):
            _, tiles = nc.values_load_multi_w_load_instructions((table or item_tile)[0:1, bass.ds(t0, n)], engines=(eng.engine,),
                                                                min_val=0, max_val=top,
                                                                skip_runtime_bounds_check_because="they count tiles passed")
            return tiles

        AHEAD = 4

        ROUNDS = ITEMS // RING

        def all_rounds(eng, one):
            one(0, None, None)
            with eng.Fori(1, ROUNDS - 1) as i:
                one(i, None, None)
            one(ROUNDS - 1, None, None)

        def accumulate(dve, cols, used, ready, done, extra=None, base=0, rounds=all_rounds, beside=None):
            dve.memset(acc[:], 0.0).then_inc(done, 1)
            for t in range(AHEAD):
                onehots(dve, t, t, used, ready, base)
                if extra is not None:
                    extra(t, t, 0)

            def one(rnd, begun, ended):
                t0 = rnd * RING
                tiles = item_tiles(dve, t0, RING)
                for u in range(RING):
                    t = t0 + u
                    if not (isinstance(t, int) and t + AHEAD >= ITEMS):
                        if extra is not None:
                            extra(t + AHEAD, (u + AHEAD) % RING, rnd + (u + AHEAD) // RING)
                        onehots(dve, t + AHEAD, (u + AHEAD) % RING, used, ready, base)
                    into = acc[:, bass.ds(tiles[u], 1), 0:cols].rearrange("p a f -> p (a f)")
                    dve.wait_ge(used, t + (base + 1))
                    dve.wait_ge(done, t + 1)
                    dve.tensor_tensor(into, into, bank[u % ACC_BANKS][:, 0:cols], ALU.add).then_inc(done, 1)
                    if beside is not None:
                        beside(u, begun, ended)
            rounds(dve, one)

        with nc.Block() as block:
            @block.gpsimd
            def _(pool):
                gather_rows(pool, g1, gcn_table, FEAT)

            @block.sync
            def _(sp):
                def load(t, slot, rnd):
                    sp.wait_ge(g1.rows_used, t * CHUNK + CHUNK)
                    sp.dma_start(g_ring[:, slot * CHUNK:(slot + 1) * CHUNK, FEAT:GCN_COLS],
                                 edge_attr_d[bass.ds(t * CHUNK_EDGES, CHUNK_EDGES), :].rearrange("(u e) f -> e u f", e=P)
                                 ).then_inc(attrs_landed[slot], 16)
                tile_loop(sp, EDGE_CHUNKS, 2, load)

            @block.tensor
            def _(pe):
                pe.sem_inc(g1.rows_used, RING)

                def sums(t, u, rnd):
                    if u % CHUNK == 0:
                        pe.wait_ge(attrs_landed[u // CHUNK], rnd * 16 + 16)
                    pe.wait_ge(onehot1, t + 1)
                    pe.wait_ge(g1.rows_in[u], rnd * 16 + 16)
                    if not (isinstance(t, int) and t < ACC_BANKS):
                        pe.wait_ge(acc_done1, t - (ACC_BANKS - 2))
                    pe.matmul(bank[u % ACC_BANKS][:, 0:GCN_COLS], onehot[:, u, :], g_ring[:, u, :], start=True, stop=True
                              ).then_inc(g1.rows_used, 1)
                for u in range(RING):
                    sums(u, u, 0)
                tile_loop(pe, ITEMS - RING, RING, sums, first=RING)

            @block.vector
            def _(dve):
                accumulate(dve, GCN_COLS, g1.rows_used, onehot1, acc_done1, base=RING)

        free_sems(early_sems)

        s2 = Norm(2)
        l2_loads = sem("l2_loads")
        self_added = sem("self_added")
        scaled_in = sem("scaled_in")
        x2_done = sem("x2_done")
        heads_of = sb("heads_of", [P, CHUNKS, 2 * HEADS])
        attn2 = sb("attn2", [P, 2, CHUNKS])
        heads_ready = sem("heads_ready")
        folded = sem("folded")
        fold_read = sem("fold_read")
        row_b = sb("row_b", [P, FEAT])
        rows_out = [sem(f"rows_out{u}") for u in range(2)]
        logit_table = dram("logit_table", [NODE_TILES * P, 2 * HEADS])
        loop_attr = sb("loop_attr", [P, NODE_TILES, EDGE_DIM])
        wt = [work[2][:, 0:CHUNKS * FEAT].rearrange("p (c k) -> p c k", c=CHUNKS),
              work[3][:, 0:CHUNKS * FEAT].rearrange("p (c k) -> p c k", c=CHUNKS)]

        with nc.Block() as block:
            @block.sync
            def _(sp):
                for dst, name in ((wbuf[:, :, 0:FEAT], "l2_w"), (wt[0], "l2_wt"), (attn2[:], "l2_attn")):
                    sp.dma_start(dst, io[name]).then_inc(l2_loads, 16)
                sp.dma_start(row_b[:], io["l1_bias"].broadcast_to([P, FEAT])).then_inc(l2_loads, 16)

                def store(t, slot, rnd):
                    sp.wait_ge(s2.out_free, t + 3)
                    sp.dma_start(l2_table[bass.ds(t * P, P), :], row_ring[:, slot, :]).then_inc(rows_out[slot], 16)
                    sp.dma_start(logit_table[bass.ds(t * P, P), :], row_ring[:, slot, FEAT:L2_COLS]).then_inc(rows_out[slot], 16)
                tile_loop(sp, NODE_TILES, 2, store)
                sp.wait_ge(rows_out[0], 32 * ((NODE_TILES + 1) // 2))
                sp.wait_ge(rows_out[1], 32 * (NODE_TILES // 2))

            @block.gpsimd
            def _(pool):
                def add_self(t, slot, rnd):
                    rows = acc[:, bass.ds(t, 1), 0:FEAT].rearrange("p a f -> p (a f)")
                    pool.tensor_tensor(rows, rows, h[:, bass.ds(t, 1), :].rearrange("p a f -> p (a f)"), ALU.add
                                       ).then_inc(self_added, 1)
                tile_loop(pool, NODE_TILES, 5, add_self)

            @block.scalar
            def _(act):
                norm_rows(act, s2)

            @block.tensor
            def _(pe):
                pe.wait_ge(heads_ready, 1)
                pe.wait_ge(l2_loads, 64)
                for k in range(CHUNKS):
                    for f in range(CHUNKS):
                        ins = pe.matmul(bank[6][:, k * 8:k * 8 + 2 * HEADS], wt[0][:, f, k * P:(k + 1) * P],
                                        heads_of[:, f, :], start=(f == 0), stop=(f == CHUNKS - 1))
                ins.then_inc(folded, 1)
                pe.wait_ge(fold_read, 1)
                project(pe, s2, [(0, 0, L2_COLS)])

            @block.vector
            def _(dve):
                c = Chain(dve, "stage8_dve")
                c.link(dve.memset(heads_of[:], 0.0))
                dve.wait_ge(l2_loads, 64)
                half = P // 2
                for side in range(2):
                    for f in range(CHUNKS):
                        for n in range(2):
                            c.mark(dve.tensor_copy(heads_of[n * half:(n + 1) * half, f, side * HEADS + 2 * f + n:side * HEADS + 2 * f + n + 1],
                                                   attn2[n * half:(n + 1) * half, side, f:f + 1]))
                dve.wait_ge(c.sem, c.n)
                dve.sem_inc(heads_ready, 1)
                dve.wait_ge(folded, 1)
                dve.tensor_copy(wbuf[:, :, FEAT:L2_COLS], bank[6][:, 0:16].rearrange("p (k n) -> p k n", k=CHUNKS)).then_inc(fold_read, 1)
                c.link(dve.tensor_scalar(small[0][:], degree1[:], -1.0, 1.0, ALU.add, ALU.max))
                c.link(dve.reciprocal(small[0][:], small[0][:]))
                c.link(dve.tensor_tensor(loop_attr[:], acc[:, :, FEAT:GCN_COLS],
                                         small[0][:].unsqueeze(2).broadcast_to([P, NODE_TILES, EDGE_DIM]), ALU.mult))

                def scale(t):
                    rows = acc[:, bass.ds(t, 1), 0:FEAT].rearrange("p a f -> p (a f)")
                    dve.wait_ge(self_added, t + 1)
                    dve.scalar_tensor_tensor(out=rows, in0=rows, scalar=dinv[:, bass.ds(t, 1)], in1=row_b[:],
                                             op0=ALU.mult, op1=ALU.add).then_inc(scaled_in, 1)

                def add(t):
                    rows = acc[:, bass.ds(t, 1), 0:FEAT].rearrange("p a f -> p (a f)")
                    tile_x = x[:, bass.ds(t, 1), :].rearrange("p a f -> p (a f)")
                    dve.wait_ge(scaled_in, t + 1)
                    dve.scalar_tensor_tensor(out=tile_x, in0=rows, scalar=0.0, in1=tile_x,
                                             op0=ALU.max, op1=ALU.add).then_inc(x2_done, 1)

                def both(t, slot, rnd):
                    scale(t)
                    add(t - 1)
                scale(0)
                tile_loop(dve, NODE_TILES - 1, 4, both, first=1)
                add(NODE_TILES - 1)
                dve.wait_ge(x2_done, NODE_TILES)
                norm_statistics(dve, c, s2)

                def keep(t, slot, rnd):
                    if not (isinstance(t, int) and t < 2):
                        dve.wait_ge(rows_out[slot], rnd * 32)
                    dve.tensor_copy(row_ring[:, slot, :], bank[2 + slot][:, 0:L2_COLS]).then_inc(s2.out_free, 1)
                read_out(dve, s2, plain_cols(dve), keep)

        idx2_in = sem("idx2_in")
        idx2 = sb("idx2", [P, 2, NODE_TILES], I32)
        side_logits = sb("side_logits", [P, NODE_TILES, 2 * HEADS])
        GROUPS2 = 5
        G2 = NODE_TILES // GROUPS2
        sides_in = [sem(f"sides_in{k}", kept=True) for k in range(GROUPS2)]
        rows2_in = [sem(f"rows2_in{k}", kept=True) for k in range(GROUPS2)]
        alpha = sb("alpha", [P, NODE_TILES, HEADS])
        less2 = sem("less2")
        exp2 = sem("exp2")
        mean_head = flat(g_ring[:])[:, 0:G2 * HEAD_DIM].rearrange("p (t d) -> p t d", t=G2)

        with nc.Block() as block:
            @block.sync
            def _(sp):
                sp.dma_start(idx2[:, 0, :], io["l2_src"]).then_inc(idx2_in, 16)
                sp.dma_start(idx2[:, 1, :], io["l2_dst"]).then_inc(idx2_in, 16)

            @block.gpsimd
            def _(pool):
                pool.wait_ge(idx2_in, 32)
                for k in range(GROUPS2):
                    for t in range(k * G2, (k + 1) * G2):
                        pool.indirect_dma_start(side_logits[:, t, :], None, logit_table,
                                                bass.IndirectOffsetOnAxis(ap=idx2[:, 0, t:t + 1], axis=0)).then_inc(sides_in[k], 16)
                    for t in range(k * G2, (k + 1) * G2):
                        pool.indirect_dma_start(acc[:, t, 0:L2_COLS], None, l2_table,
                                                bass.IndirectOffsetOnAxis(ap=idx2[:, 1, t:t + 1], axis=0)).then_inc(rows2_in[k], 16)

            @block.scalar
            def _(act):
                for k in range(GROUPS2):
                    ts = slice(k * G2, (k + 1) * G2)
                    act.wait_ge(less2, k + 1)
                    act.activation(alpha[:, ts, :], alpha[:, ts, :], ACT.Exp).then_inc(exp2, 1)

            @block.vector
            def _(dve):
                c = Chain(dve, "stage9_dve")
                for k in range(GROUPS2):
                    ts = slice(k * G2, (k + 1) * G2)
                    weights = alpha[:, ts, :]
                    by_head = [P, G2, HEADS]
                    dve.wait_ge(sides_in[k], 16 * G2)
                    dve.wait_ge(rows2_in[k], 16 * G2)
                    c.link(dve.tensor_tensor(weights, side_logits[:, ts, 0:HEADS], acc[:, ts, FEAT + HEADS:L2_COLS], ALU.add))
                    c.link(dve.scalar_tensor_tensor(out=weights, in0=weights, scalar=NEG_L2, in1=weights, op0=ALU.mult, op1=ALU.max))
                    c.link(dve.tensor_reduce(small[0][:, ts], weights, X_AXIS, ALU.max))
                    dve.tensor_tensor(weights, weights, small[0][:, ts].unsqueeze(2).broadcast_to(by_head), ALU.subtract
                                      ).then_inc(less2, 1)
                    dve.wait_ge(exp2, k + 1)
                    c.link(dve.tensor_reduce(small[1][:, ts], weights, X_AXIS, ALU.add))
                    c.link(dve.reciprocal(small[1][:, ts], small[1][:, ts]))
                    c.link(dve.tensor_tensor(weights, weights, small[1][:, ts].unsqueeze(2).broadcast_to(by_head), ALU.mult))
                    rows = acc[:, ts, 0:FEAT].rearrange("p t (h d) -> p t h d", h=HEADS)
                    all_heads = [P, G2, HEADS, HEAD_DIM]
                    c.link(dve.tensor_tensor(rows, rows, weights.unsqueeze(3).broadcast_to(all_heads), ALU.mult))
                    c.link(dve.tensor_reduce(mean_head, acc[:, ts, 0:FEAT].rearrange("p t (h d) -> p t d h", h=HEADS), X_AXIS, ALU.add))
                    tile_x = x[:, ts, :].rearrange("p t (h d) -> p t h d", h=HEADS)
                    c.link(dve.tensor_tensor(tile_x, tile_x, mean_head.unsqueeze(2).broadcast_to(all_heads), ALU.add))

        middle_sems = clear_sems()
        s3 = Norm(3)
        l3_loads = sem("l3_loads")
        we_ext = sb("we_ext", [EDGE_DIM, L3_COLS])
        attt = sb("attt", [P, CHUNKS])
        bt = sb("bt", [P, 2, CHUNKS])
        bias3 = sb("bias3", [1, 2 * L3_COLS])
        heads3_ready = sem("heads3_ready")
        folded3 = sem("folded3")
        fold3_read = sem("fold3_read")
        xl_linear = sb("xl_linear", [P, NODE_TILES, HEADS])
        rest_ring = item_vals[:, 0, 0:4 * L3_COLS].rearrange("p (s k f) -> p s k f", s=2, k=2)
        rest_ready = sem("rest_ready")
        split_steps = sem("split_steps")
        split_done = sem("split_done")
        l3_stored = sem("l3_stored")

        wt3 = [flat(acc[:])[:, k * CHUNKS * FEAT:(k + 1) * CHUNKS * FEAT].rearrange("p (c k) -> p c k", c=CHUNKS)
               for k in range(2)]
        wet = flat(acc[:])[:, 2048:2048 + CHUNKS * EDGE_DIM].rearrange("p (c k) -> p c k", c=CHUNKS)

        with nc.Block() as block:
            @block.sync
            def _(sp):
                for dst, name in ((wbuf[:, :, 0:FEAT], "l3_wl"), (wbuf[:, :, L3_COLS:L3_COLS + FEAT], "l3_wr"),
                                  (wt3[0], "l3_wlt"), (wt3[1], "l3_wrt"), (wet, "l3_wet"), (attt[:], "l3_attt"),
                                  (bt[:], "l3_bt"), (we_ext[:, 0:FEAT], "l3_we")):
                    sp.dma_start(dst, io[name]).then_inc(l3_loads, 16)
                sp.dma_start(bias3[:, 0:FEAT], io["l3_bias"][:, 0:FEAT]).then_inc(l3_loads, 16)
                sp.dma_start(bias3[:, L3_COLS:L3_COLS + FEAT], io["l3_bias"][:, FEAT:2 * FEAT]).then_inc(l3_loads, 16)
                sp.dma_start(row_b[:], io["l3_att"].broadcast_to([P, FEAT])).then_inc(l3_loads, 16)

                def store(t, slot, rnd):
                    sp.wait_ge(s3.out_free, t + 3)
                    sp.dma_start(l3_table[bass.ds(t * P, P), 0:FEAT],
                                 h[:, bass.ds(t, 1), :].rearrange("p a f -> p (a f)")).then_inc(l3_stored, 16)
                    sp.dma_start(l3_table[bass.ds(t * P, P), FEAT:L3_COLS],
                                 xl_linear[:, bass.ds(t, 1), :].rearrange("p a f -> p (a f)")).then_inc(l3_stored, 16)
                tile_loop(sp, NODE_TILES, 5, store)
                sp.wait_ge(l3_stored, 32 * NODE_TILES)

            @block.scalar
            def _(act):
                norm_rows(act, s3)

            @block.tensor
            def _(pe):
                pe.wait_ge(heads3_ready, 1)
                pe.wait_ge(l3_loads, 16 * 11)
                att_of = heads_of[:, :, 0:HEADS]
                for n in range(2):
                    for k in range(CHUNKS):
                        for f in range(CHUNKS):
                            at = (n * CHUNKS + k) * HEADS
                            pe.matmul(bank[6][:, at:at + HEADS], wt3[n][:, f, k * P:(k + 1) * P], att_of[:, f, :],
                                      start=(f == 0), stop=(f == CHUNKS - 1))
                    for f in range(CHUNKS):
                        pe.matmul(bank[7][0:1, n * HEADS:(n + 1) * HEADS], bt[:, n, f:f + 1], att_of[:, f, :],
                                  start=(f == 0), stop=(f == CHUNKS - 1))
                for f in range(CHUNKS):
                    ins = pe.matmul(bank[7][0:EDGE_DIM, 16:16 + HEADS], wet[:, f, :], att_of[:, f, :],
                                    start=(f == 0), stop=(f == CHUNKS - 1))
                ins.then_inc(folded3, 1)
                pe.wait_ge(fold3_read, 1)
                project(pe, s3, [(0, 0, L3_COLS), (1, L3_COLS, 2 * L3_COLS)], bias=bias3)

            @block.gpsimd
            def _(pool):
                def split(t, slot, rnd):
                    pool.wait_ge(rest_ready, t + 1)
                    part = [xr_parts[:, bass.ds(t, 1), k, :].rearrange("p a f -> p (a f)") for k in range(3)]
                    pool.tensor_copy(part[1], rest_ring[:, slot, 0, :]).then_inc(split_steps, 1)
                    hold(pool, "pool", split_steps, t * 2 + 1)
                    pool.tensor_tensor(rest_ring[:, slot, 1, :], rest_ring[:, slot, 0, :], part[1], ALU.subtract
                                       ).then_inc(split_steps, 1)
                    pool.wait_ge(split_steps, t * 2 + 2)
                    pool.tensor_copy(part[2], rest_ring[:, slot, 1, :]).then_inc(split_done, 1)
                tile_loop(pool, NODE_TILES, 2, split)

            @block.vector
            def _(dve):
                c = Chain(dve, "stage10_dve")
                c.link(dve.memset(heads_of[:], 0.0))
                dve.wait_ge(l3_loads, 16 * 11)
                half = P // 2
                for f in range(CHUNKS):
                    for n in range(2):
                        c.mark(dve.tensor_copy(heads_of[n * half:(n + 1) * half, f, 2 * f + n:2 * f + n + 1],
                                               attt[n * half:(n + 1) * half, f:f + 1]))
                dve.wait_ge(c.sem, c.n)
                dve.sem_inc(heads3_ready, 1)
                c.mark(dve.tensor_scalar(row_b[:], row_b[:], 1.0 - NEG_GAT, None, ALU.mult))
                dve.wait_ge(folded3, 1)
                for n in range(2):
                    at = n * CHUNKS * HEADS
                    c.mark(dve.tensor_scalar(wbuf[:, :, n * L3_COLS + FEAT:(n + 1) * L3_COLS],
                                             bank[6][:, at:at + CHUNKS * HEADS].rearrange("p (k n) -> p k n", k=CHUNKS),
                                             NEG_GAT, None, ALU.mult))
                    c.mark(dve.tensor_scalar(bias3[:, n * L3_COLS + FEAT:(n + 1) * L3_COLS],
                                             bank[7][0:1, n * HEADS:(n + 1) * HEADS], NEG_GAT, None, ALU.mult))
                c.link(dve.tensor_scalar(we_ext[:, FEAT:L3_COLS], bank[7][0:EDGE_DIM, 16:16 + HEADS], NEG_GAT, None, ALU.mult))
                dve.sem_inc(fold3_read, 1)
                norm_statistics(dve, c, s3)
                parts_made = c.sem
                before = c.n

                def keep(t, slot, rnd):
                    left, right = bank[2 + slot * 2], bank[3 + slot * 2]
                    first = xr_parts[:, bass.ds(t, 1), 0, :].rearrange("p a f -> p (a f)")
                    dve.tensor_copy(first, right[:, 0:L3_COLS]).then_inc(parts_made, 1)
                    dve.tensor_copy(h[:, bass.ds(t, 1), :].rearrange("p a f -> p (a f)"), left[:, 0:FEAT]).then_inc(parts_made, 1)
                    if not (isinstance(t, int) and t < 2):
                        dve.wait_ge(split_done, t - 1)
                    dve.wait_ge(parts_made, t * 2 + (before + 1))
                    dve.tensor_tensor(rest_ring[:, slot, 0, :], right[:, 0:L3_COLS], first, ALU.subtract).then_inc(rest_ready, 1)
                    dve.wait_ge(parts_made, t * 2 + (before + 2))
                    dve.wait_ge(rest_ready, t + 1)
                    dve.tensor_copy(xl_linear[:, bass.ds(t, 1), :].rearrange("p a f -> p (a f)"), left[:, FEAT:L3_COLS]
                                    ).then_inc(s3.out_free, 1)
                read_out(dve, s3, plain_cols(dve), keep)

        free_sems(middle_sems)

        own_logits = sb("own_logits", [P, NODE_TILES, HEADS])
        we_parts = sb("we_parts", [P, L3_COLS], BF16)
        we_part = flat(acc[:])[0:EDGE_DIM, 0:3 * L3_COLS // 2].bitcast(BF16).rearrange("p (k f) -> p k f", k=3)
        we_rest = flat(acc[:])[0:EDGE_DIM, 512:512 + 2 * L3_COLS].rearrange("p (k f) -> p k f", k=2)
        we_split = sem("we_split")
        we_placed = sem("we_placed")

        def add_terms(pe, into, places, tile, attrs, weights):
            for k in range(3):
                pe.matmul(into, places, xr_parts[:, bass.ds(tile, 1), k, :].rearrange("p a f -> p (a f)"),
                          start=(k == 0), stop=False)
            return pe.matmul(into, attrs, weights, start=False, stop=True)

        g3 = Gather("l3a")
        sum_ring = flat(sums_rhs[:])[:, 0:RING * L3_COLS].rearrange("p (u f) -> p u f", u=RING)
        relu_ring = flat(sums_rhs[:])[:, RING * L3_COLS:RING * L3_COLS + 4 * FEAT].rearrange("p (u f) -> p u f", u=4)
        attrs_turned = item_vals[:, 1, 0:RING * P // 2].bitcast(BF16).rearrange("p (u e) -> p u e", u=RING)
        pair_rows = attr_parts_d.rearrange("b p c -> (b p c)").rearrange("(k g e) -> k g e", g=EDGE_TILES, e=P)
        edge_tile = item_vals[0:1, 1, 1024:1024 + ITEMS].bitcast(I32)
        edge_tile_in = sem("edge_tile_in")
        nonlinear = sb("nonlinear", [P, RING, HEADS])
        rows_ring = sb("rows_ring", [P, 2, CHUNK_EDGES], BF16)
        rows3_in = [sem(f"rows3_in{u}") for u in range(2)]
        attrs3_in = [sem(f"attrs3_in{u}") for u in range(RING)]
        places3 = sem("places3")
        terms3 = sem("terms3")
        relued3 = sem("relued3")
        dotted3 = sem("dotted3")
        logits3 = sem("logits3")
        LAG = 2

        def item_rounds(eng, step, prepare=None):
            def one(t0, rnd):
                extra = (prepare(t0),) if prepare else ()
                for u in range(RING):
                    step(t0 + u, u, rnd, *extra)
            one(0, 0)
            with eng.Fori(1, ITEMS // RING - 1) as i:
                one(i * RING, i)
            one(ITEMS - RING, ITEMS // RING - 1)

        def at_least(t, n):
            return not isinstance(t, int) or t >= n

        def known_after(t, n):
            return not isinstance(t, int) or t + n < ITEMS

        with nc.Block() as block:
            @block.gpsimd
            def _(pool):
                gather_rows(pool, g3, l3_table, L3_COLS)

            @block.sync
            def _(sp):
                sp.dma_start(edge_tile, edge_tile_d.unsqueeze(0)).then_inc(edge_tile_in, 16)
                sp.wait_ge(edge_tile_in, 16)

                def load(t, u, rnd, tiles):
                    slot = u // CHUNK
                    if u % CHUNK == 0:
                        if at_least(t, RING):
                            sp.wait_ge(places3, rnd * 2 + (slot - 1))
                        sp.dma_start(rows_ring[:, slot, :],
                                     dst_rows_d[bass.ds(t * P, CHUNK_EDGES)].unsqueeze(0).broadcast_to([P, CHUNK_EDGES])
                                     ).then_inc(rows3_in[slot], 16)
                    if at_least(t, RING):
                        sp.wait_ge(terms3, t - (RING - 1))
                    sp.dma_start(attrs_turned[:, u, :], pair_rows[:, bass.ds(tiles[u], 1), :].rearrange("k a e -> k (a e)")
                                 ).then_inc(attrs3_in[u], 16)
                sp.wait_ge(we_split, 1)
                for b in range(PAIRS):
                    sp.dma_start(we_parts[b * EDGE_DIM:(b + 1) * EDGE_DIM, :], we_part[:, b % 3, :]).then_inc(we_placed, 16)
                item_rounds(sp, load, lambda t0: item_tiles(sp, t0, RING, edge_tile, EDGE_TILES - 1))

            @block.tensor
            def _(pe):
                def item(t, u, rnd, tiles):
                    slot = u // CHUNK
                    if u % CHUNK == 0:
                        pe.wait_ge(places3, rnd * 2 + (slot + 1))
                    pe.wait_ge(attrs3_in[u], rnd * 16 + 16)
                    if at_least(t, ACC_BANKS):
                        pe.wait_ge(g3.rows_used, t + (RING + 1 - ACC_BANKS))
                    add_terms(pe, bank[u % ACC_BANKS][:, 0:L3_COLS], place_ring[:, slot, 0, u % CHUNK * P:(u % CHUNK + 1) * P],
                              tiles[u], attrs_turned[:, u, :], we_parts[:]).then_inc(terms3, 1)
                pe.wait_ge(we_placed, 16 * PAIRS)
                item_rounds(pe, item, lambda t0: item_tiles(pe, t0, RING))

            @block.scalar
            def _(act):
                def item(t, u, rnd):
                    act.wait_ge(g3.rows_used, t + (RING + 1))
                    if at_least(t, 4):
                        act.wait_ge(dotted3, t - 3)
                    act.activation(relu_ring[:, u % 4, :], sum_ring[:, u, 0:FEAT], ACT.Relu).then_inc(relued3, 1)
                item_rounds(act, item)

            @block.vector
            def _(dve):
                c = Chain(dve, "stage12_dve")
                dve.sem_inc(g3.rows_used, RING)
                c.link(dve.tensor_copy(we_part[:, 0, :], we_ext[:]))
                c.link(dve.tensor_tensor(we_rest[:, 0, :], we_ext[:], we_part[:, 0, :], ALU.subtract))
                c.link(dve.tensor_copy(we_part[:, 1, :], we_rest[:, 0, :]))
                c.link(dve.tensor_tensor(we_rest[:, 1, :], we_rest[:, 0, :], we_part[:, 1, :], ALU.subtract))
                c.link(dve.tensor_copy(we_part[:, 2, :], we_rest[:, 1, :]))
                dve.sem_inc(we_split, 1)

                def places(chunk, slot, rnd):
                    dve.wait_ge(rows3_in[slot], rnd * 16 + 16)
                    if at_least(chunk, 2):
                        dve.wait_ge(terms3, chunk * CHUNK - CHUNK)
                    dve.tensor_scalar(place_ring[:, slot, 0, :], rows_ring[:, slot, :], p_index[:], None, ALU.is_equal
                                      ).then_inc(places3, 1)

                def dot(t, u):
                    dve.wait_ge(relued3, t + 1)
                    for hd in range(HEADS):
                        d = slice(hd * HEAD_DIM, (hd + 1) * HEAD_DIM)
                        ins = dve.tensor_tensor_reduce(out=relu_ring[:, u % 4, d], in0=relu_ring[:, u % 4, d], in1=row_b[:, d],
                                                       scale=1.0, scalar=0.0, op0=ALU.mult, op1=ALU.add,
                                                       accum_out=nonlinear[:, u, hd:hd + 1])
                    ins.then_inc(dotted3, 1)

                def finish(t0, slot):
                    dve.wait_ge(dotted3, t0 + CHUNK)
                    us = slice(slot * CHUNK, (slot + 1) * CHUNK)
                    dve.tensor_tensor(logits[:, bass.ds(t0, CHUNK), :], nonlinear[:, us, :], sum_ring[:, us, FEAT:L3_COLS], ALU.add
                                      ).then_inc(logits3, 1)

                def item(t, u, rnd):
                    slot = u // CHUNK
                    if u % CHUNK == 0 and known_after(t, CHUNK):
                        places(rnd * 2 + (slot + 1), 1 - slot, rnd + slot)
                    dve.wait_ge(g3.rows_in[u], rnd * 16 + 16)
                    dve.wait_ge(terms3, t + 1)
                    if at_least(t, RING):
                        dve.wait_ge(relued3, t - (RING - 1))
                        if u % CHUNK == 0:
                            dve.wait_ge(logits3, rnd * 2 + (slot - 1))
                    dve.tensor_tensor(sum_ring[:, u, :], g_ring[:, u, 0:L3_COLS], bank[u % ACC_BANKS][:, 0:L3_COLS], ALU.add
                                      ).then_inc(g3.rows_used, 1)
                    if at_least(t, LAG):
                        dot(t - LAG, (u - LAG) % RING)
                        if u % CHUNK == CHUNK - 1 and at_least(t, CHUNK):
                            finish(t - (2 * CHUNK - 1), 1 - slot)
                places(0, 0, 0)
                item_rounds(dve, item)
                for t in range(ITEMS - LAG, ITEMS):
                    dot(t, t % RING)
                finish(ITEMS - CHUNK, 1)

        seg3 = Segments("l3")
        masked3 = sem("masked3")
        less3 = sem("less3")
        exp3 = sem("exp3")

        with nc.Block() as block:
            @block.tensor
            def _(pe):
                segment_max_pe(pe, seg3, logits, HEADS, masked3)

            @block.scalar
            def _(act):
                act.wait_ge(less3, 1)
                act.activation(sums_rhs[:, :, 0:HEADS], logits, ACT.Exp).then_inc(exp3, 1)
                act.wait_ge(exp3, 1)

            @block.vector
            def _(dve):
                c = Chain(dve, "stage13_dve")
                by_head = [P, ITEMS, HEADS]
                c.link(dve.tensor_tensor(logits, logits, off_col[:].unsqueeze(2).broadcast_to(by_head), ALU.add))
                dve.sem_inc(masked3, 1)
                segment_max_dve(dve, c, seg3, maxima, HEADS)
                dve.tensor_tensor(logits, logits, maxima, ALU.subtract).then_inc(less3, 1)
                c.mark(dve.tensor_tensor(sums_rhs[:, :, HEADS:2 * HEADS], maxima, last_col[:].unsqueeze(2).broadcast_to(by_head), ALU.mult))

        g4 = Gather("l3b")
        weighted = flat(item_vals[:])[:, 0:RING * OUT_COLS].rearrange("p (u f) -> p u f", u=RING)
        onehot4 = sem("onehot4")
        summed4 = sem("summed4")
        acc_done4 = sem("acc_done4")
        beside4 = sem("beside4")
        own_memory = flat(item_vals[:])[:, RING * OUT_COLS:]
        own = own_memory[:, 0:L3_COLS]
        own_relu = own_memory[:, 264:264 + HEADS]
        attr_row = own_memory[:, 272:272 + EDGE_DIM]
        attr_turned = own_memory[0:EDGE_DIM, 288:288 + P]
        ident_b = sb("ident_b", [P, P], BF16)
        ident_ready = sem("ident_ready")
        attr_ready = sem("attr_ready")
        attr_flipped = sem("attr_flipped")
        attr_stored = sem("attr_stored")
        own_products = sem("own_products")
        own_added = sem("own_added")
        own_relued = sem("own_relued")
        own_dotted = sem("own_dotted")

        def rounds_with_tiles(eng, one):
            one(0, None, None)
            one(1, 0, None)
            with eng.Fori(2, NODE_TILES + 1) as i:
                one(i, i - 1, i - 2)
            one(NODE_TILES + 1, None, NODE_TILES - 1)
            with eng.Fori(NODE_TILES + 2, ROUNDS - 1) as i:
                one(i, None, None)
            one(ROUNDS - 1, None, None)

        with nc.Block() as block:
            @block.gpsimd
            def _(pool):
                gather_rows(pool, g4, l3_table, L3_COLS)

            @block.scalar
            def _(act):
                def beside(t, slot):
                    if at_least(t, 2):
                        hold(act, "act", summed4, t * CHUNK - CHUNK)
                    act.copy(weighted[:, slot * CHUNK:(slot + 1) * CHUNK, FEAT:OUT_COLS],
                             sums_rhs[:, bass.ds(t * CHUNK, CHUNK), :]).then_inc(beside4, 1)

                def one(rnd, begun, ended):
                    beside(rnd * 2, 0)
                    if ended is not None:
                        act.wait_ge(own_added, ended + 1)
                        act.activation(own[:, 0:FEAT], own[:, 0:FEAT], ACT.Relu).then_inc(own_relued, 1)
                    beside(rnd * 2 + 1, 1)
                rounds_with_tiles(act, one)

            @block.tensor
            def _(pe):
                def one(rnd, begun, ended):
                    for u in range(RING):
                        t = rnd * RING + u
                        if u % CHUNK == 0:
                            pe.wait_ge(beside4, rnd * 2 + (u // CHUNK + 1))
                        pe.wait_ge(onehot4, t + 1)
                        pe.wait_ge(g4.rows_used, t + (RING + 1))
                        if at_least(t, ACC_BANKS):
                            pe.wait_ge(acc_done4, t - (ACC_BANKS - 2))
                        pe.matmul(bank[u % ACC_BANKS][:, 0:OUT_COLS], onehot[:, u, :], weighted[:, u, :], start=True, stop=True
                                  ).then_inc(summed4, 1)
                        if begun is not None and u == 1:
                            pe.wait_ge(attr_ready, begun + 1)
                            pe.transpose(bank[6][0:EDGE_DIM, 0:P], attr_row, ident[:]).then_inc(attr_flipped, 1)
                        if begun is not None and u == 5:
                            pe.wait_ge(attr_stored, begun + 1)
                            add_terms(pe, bank[4][:, 0:L3_COLS], ident_b[:], begun, attr_turned, we_ext[:]).then_inc(own_products, 1)
                pe.wait_ge(ident_ready, 1)
                rounds_with_tiles(pe, one)

            @block.vector
            def _(dve):
                dve.sem_inc(g4.rows_used, RING)
                dve.tensor_copy(ident_b[:], ident[:]).then_inc(ident_ready, 1)

                def weigh(t, u, rnd):
                    dve.wait_ge(g4.rows_in[u], rnd * 16 + 16)
                    if at_least(t, RING):
                        dve.wait_ge(summed4, t - (RING - 1))
                    dve.tensor_tensor(weighted[:, u, 0:FEAT].rearrange("p (h d) -> p h d", h=HEADS),
                                      g_ring[:, u, 0:FEAT].rearrange("p (h d) -> p h d", h=HEADS),
                                      sums_rhs[:, bass.ds(t, 1), 0:HEADS].rearrange("p a h -> p (a h)").unsqueeze(2).broadcast_to([P, HEADS, HEAD_DIM]),
                                      ALU.mult).then_inc(g4.rows_used, 1)

                def own_steps(u, begun, ended):
                    if begun is not None and u == 0:
                        dve.tensor_copy(attr_row, loop_attr[:, bass.ds(begun, 1), :].rearrange("p a k -> p (a k)")
                                        ).then_inc(attr_ready, 1)
                    if ended is not None and u == 2:
                        dve.wait_ge(own_relued, ended + 1)
                        for hd in range(HEADS):
                            d = slice(hd * HEAD_DIM, (hd + 1) * HEAD_DIM)
                            ins = dve.tensor_tensor_reduce(out=own[:, d], in0=own[:, d], in1=row_b[:, d], scale=1.0, scalar=0.0,
                                                           op0=ALU.mult, op1=ALU.add, accum_out=own_relu[:, hd:hd + 1])
                        ins.then_inc(own_dotted, 1)
                    if begun is not None and u == 3:
                        dve.wait_ge(attr_flipped, begun + 1)
                        dve.tensor_copy(attr_turned, bank[6][0:EDGE_DIM, 0:P]).then_inc(attr_stored, 1)
                    if ended is not None and u == 4:
                        dve.wait_ge(own_dotted, ended * 2 + 1)
                        dve.tensor_tensor(own_logits[:, bass.ds(ended, 1), :].rearrange("p a h -> p (a h)"), own_relu,
                                          own[:, FEAT:L3_COLS], ALU.add).then_inc(own_dotted, 1)
                    if begun is not None and u == 6:
                        if ended is not None:
                            dve.wait_ge(own_dotted, ended * 2 + 2)
                        dve.wait_ge(own_products, begun + 1)
                        dve.tensor_tensor(own[:, 0:FEAT], bank[4][:, 0:FEAT],
                                          h[:, bass.ds(begun, 1), :].rearrange("p a f -> p (a f)"), ALU.add)
                        dve.tensor_tensor(own[:, FEAT:L3_COLS], bank[4][:, FEAT:L3_COLS],
                                          xl_linear[:, bass.ds(begun, 1), :].rearrange("p a h -> p (a h)"), ALU.add
                                          ).then_inc(own_added, 1)
                accumulate(dve, OUT_COLS, summed4, onehot4, acc_done4, extra=weigh, rounds=rounds_with_tiles, beside=own_steps)

        final_loads = sem("final_loads")
        shares_in = sem("shares_in")
        shares = sem("shares")
        bias_in = sem("bias_in")
        own_weighed = sem("own_weighed")
        sum_weighed = sem("sum_weighed")
        total = sem("total")
        biased = sem("biased")
        sigmoids = sem("sigmoids")
        silu = sem("silu")
        base = sem("base")
        normed = sem("normed")
        result = sem("result")
        written = sem("written")
        top_all, den, share_0, share_1 = [
            flat(item_vals[:])[:, 2560 + i * 128:2560 + i * 128 + NODE_TILES * HEADS].rearrange("p (t h) -> p t h", h=HEADS)
            for i in range(4)]
        share = [share_0, share_1]
        sig_ring = rings[:, 0:2 * FEAT].rearrange("p (s f) -> p s f", s=2)
        norm_ring = rings[:, 512:512 + 2 * FEAT].rearrange("p (s f) -> p s f", s=2)

        def rows_of(table, t, cols=FEAT):
            return table[:, bass.ds(t, 1), 0:cols].rearrange("p a f -> p (a f)")

        def heads_view(ap):
            return ap.rearrange("p (h d) -> p h d", h=HEADS)

        def head_scale(n, t):
            return share[n][:, bass.ds(t, 1), :].rearrange("p a h -> p (a h)").unsqueeze(2).broadcast_to([P, HEADS, HEAD_DIM])

        with nc.Block() as block:
            @block.sync
            def _(sp):
                sp.dma_start(row_b[:], io["l3_bias"][:, 2 * FEAT:3 * FEAT].broadcast_to([P, FEAT])).then_inc(final_loads, 16)

                def write(t, slot, rnd):
                    sp.wait_ge(result, t + 1)
                    sp.dma_start(out[bass.ds(t * P, P), :], rows_of(x, t)).then_inc(written, 16)
                tile_loop(sp, NODE_TILES - 1, 4, write)
                sp.wait_ge(result, NODE_TILES)
                sp.dma_start(out[(NODE_TILES - 1) * P:NODES, :], x[0:LAST_ROWS, NODE_TILES - 1, :]).then_inc(written, 16)
                sp.wait_ge(written, 16 * NODE_TILES)

            @block.gpsimd
            def _(pool):
                pool.wait_ge(shares, 1)

                def weigh(t, slot, rnd):
                    pool.tensor_tensor(heads_view(rows_of(h, t)), heads_view(rows_of(h, t)), head_scale(1, t), ALU.mult
                                       ).then_inc(own_weighed, 1)
                tile_loop(pool, NODE_TILES, 5, weigh)

            @block.scalar
            def _(act):
                act.wait_ge(shares_in, 1)
                act.activation(share[0], share[0], ACT.Exp)
                act.activation(share[1], share[1], ACT.Exp).then_inc(shares_in, 1)

                def norm(t, slot):
                    if at_least(t, 2):
                        hold(act, "act", base, t - 1)
                    act.activation(norm_ring[:, slot, :], rows_of(x, t), ACT.Relu, bias=shift[:, bass.ds(t, 1)],
                                   scale=rstd[:, bass.ds(t, 1)]).then_inc(normed, 1)

                def one(t, slot, rnd):
                    norm(t, slot)
                    if at_least(t, 2):
                        act.wait_ge(silu, t - 1)
                    hold(act, "act", biased, t + 1)
                    act.activation(sig_ring[:, slot, :], rows_of(acc, t), ACT.Sigmoid).then_inc(sigmoids, 1)
                one(0, 0, 0)
                one(1, 1, 0)
                tile_loop(act, NODE_TILES - 2, 2, one, first=2)

            @block.vector
            def _(dve):
                c = Chain(dve, "stage15_dve")
                edges_den = acc[:, :, FEAT:FEAT + HEADS]
                edges_top = acc[:, :, FEAT + HEADS:OUT_COLS]
                c.link(dve.tensor_scalar(den, edges_den, 0.0, -BIG, ALU.is_equal, ALU.mult))
                c.link(dve.tensor_tensor(den, den, edges_top, ALU.add))
                c.link(dve.tensor_tensor(top_all, den, own_logits[:], ALU.max))
                c.mark(dve.tensor_tensor(share[0], den, top_all, ALU.subtract))
                c.link(dve.tensor_tensor(share[1], own_logits[:], top_all, ALU.subtract))
                dve.sem_inc(shares_in, 1)
                dve.wait_ge(shares_in, 2)
                c.link(dve.tensor_tensor(den, edges_den, share[0], ALU.mult))
                c.link(dve.scalar_tensor_tensor(out=den, in0=den, scalar=1e-16, in1=share[1], op0=ALU.add, op1=ALU.add))
                c.link(dve.reciprocal(den, den))
                for n in range(2):
                    c.mark(dve.tensor_tensor(share[n], share[n], den, ALU.mult))
                dve.wait_ge(c.sem, c.n)
                dve.sem_inc(shares, 1)
                dve.wait_ge(final_loads, 16)

                def value(t):
                    rows = rows_of(acc, t)
                    dve.tensor_tensor(heads_view(rows), heads_view(rows), head_scale(0, t), ALU.mult).then_inc(sum_weighed, 1)
                    dve.wait_ge(own_weighed, t + 1)
                    dve.tensor_tensor(rows_of(h, t), rows_of(h, t), row_b[:], ALU.add).then_inc(total, 1)
                    dve.wait_ge(sum_weighed, t + 1)
                    dve.wait_ge(total, t + 1)
                    dve.tensor_tensor(rows, rows, rows_of(h, t), ALU.add).then_inc(biased, 1)

                def residual(t, slot):
                    dve.wait_ge(normed, t + 1)
                    dve.tensor_tensor(rows_of(x, t), rows_of(x, t), norm_ring[:, slot, :], ALU.add).then_inc(base, 1)
                    dve.wait_ge(sigmoids, t + 1)
                    dve.tensor_tensor(sig_ring[:, slot, :], sig_ring[:, slot, :], rows_of(acc, t), ALU.mult).then_inc(silu, 1)
                    dve.wait_ge(base, t + 1)
                    dve.wait_ge(silu, t + 1)
                    dve.tensor_tensor(rows_of(x, t), rows_of(x, t), sig_ring[:, slot, :], ALU.add).then_inc(result, 1)

                def both(t, slot, rnd):
                    value(t)
                    residual(t - 1, 1 - slot)
                value(0)
                tile_loop(dve, NODE_TILES - 1, 2, both, first=1)
                residual(NODE_TILES - 1, (NODE_TILES - 1) % 2)


def layouts(a):
    import numpy as np
    pad = EDGE_TILES * P - EDGES
    node_pad = NODE_TILES * P
    src = np.concatenate([a["src"], np.zeros(pad, a["src"].dtype)])
    beyond = np.full(pad + 1, node_pad, a["dst"].dtype)
    before = np.full(1, -1, a["dst"].dtype)
    dst = np.concatenate([before, a["dst"], beyond])
    dst_ext = np.stack([dst[g * P:g * P + P + 2] for g in range(EDGE_TILES)])
    attr = np.concatenate([a["edge_attr_16"], np.zeros((pad, EDGE_DIM), a["edge_attr_16"].dtype)])
    gate = np.concatenate([a["node_vec1"][:, 0], np.zeros(node_pad - NODES, a["node_vec1"].dtype)])

    def features_on_partitions(w):
        return np.ascontiguousarray(w.reshape(CHUNKS, P, -1).transpose(1, 0, 2))

    return {
        "x": a["x"],
        "dst_all": dst[1:-1].reshape(P, EDGE_TILES),
        "dst_ext": dst_ext,
        "src_tiles": src.reshape(EDGE_TILES, P),
        "edge_attr": attr.reshape(EDGE_TILES, P * EDGE_DIM),
        "attr_t": np.ascontiguousarray(attr.T).reshape(P, ATTR_COLS),
        "gate": np.ascontiguousarray(gate.reshape(NODE_TILES, P).T),
        "l2_src": np.ascontiguousarray(a["src"][:node_pad].reshape(NODE_TILES, P).T),
        "l2_dst": np.ascontiguousarray(a["dst"][:node_pad].reshape(NODE_TILES, P).T),
        "l0_w": features_on_partitions(a["L0_gnn_W"]),
        "l0_attn": np.concatenate([a["L0_gnn_attn_l"], a["L0_gnn_attn_r"], a["L0_gnn_bias"]]).reshape(1, 6),
        "l1_w": features_on_partitions(a["L1_gnn_weight"]),
        "l1_bias": a["L1_gnn_bias"].reshape(1, FEAT),
        "l1_norm": np.ascontiguousarray(np.stack([features_on_partitions(a["L1_gnn_" + k])[:, :, 0] for k in (
            "gamma", "beta", "running_mean", "running_var")], axis=1)),
        "l2_w": features_on_partitions(a["L2_gnn_weight"]),
        "l2_wt": features_on_partitions(a["L2_gnn_weight"].T),
        "l2_attn": np.ascontiguousarray(np.stack([a["L2_gnn_attn_l"].reshape(CHUNKS, P).T,
                                                  a["L2_gnn_attn_r"].reshape(CHUNKS, P).T], axis=1)),
        "l3_wl": features_on_partitions(a["L3_gnn_W_l"].T),
        "l3_wlt": features_on_partitions(a["L3_gnn_W_l"]),
        "l3_wr": features_on_partitions(a["L3_gnn_W_r"].T),
        "l3_wrt": features_on_partitions(a["L3_gnn_W_r"]),
        "l3_we": np.ascontiguousarray(a["L3_gnn_W_e"].T),
        "l3_wet": features_on_partitions(a["L3_gnn_W_e"]),
        "l3_bias": np.stack([a["L3_gnn_b_l"], a["L3_gnn_b_r"], a["L3_gnn_bias"]]).reshape(1, 3 * FEAT),
        "l3_bt": np.ascontiguousarray(np.stack([a["L3_gnn_b_l"].reshape(CHUNKS, P).T,
                                                a["L3_gnn_b_r"].reshape(CHUNKS, P).T], axis=1)),
        "l3_att": a["L3_gnn_att"].reshape(1, FEAT),
        "l3_attt": np.ascontiguousarray(a["L3_gnn_att"].reshape(CHUNKS, P).T),
    }


def kernel(**inputs):
    import numpy as np
    import concourse.bacc as bacc
    from concourse.bass_utils import run_bass_kernel_spmd
    arrays = layouts({k: np.asarray(v) for k, v in inputs.items()})
    nc = bacc.Bacc("TRN2", target_bir_lowering=False, num_devices=1)
    io = {k: nc.dram_tensor(f"in_{k}", v.shape, mybir.dt.from_np(v.dtype), kind="ExternalInput").ap()
          for k, v in arrays.items()}
    out = nc.dram_tensor("out", (NODES, FEAT), F32, kind="ExternalOutput").ap()
    build(nc, io, out)
    result = run_bass_kernel_spmd(nc, [{f"in_{k}": v for k, v in arrays.items()}], core_ids=[0])
    return result.results[0]["out"]
```

```python
from contextlib import ExitStack

import concourse.bass as bass
from concourse import mybir

F32 = mybir.dt.float32
BF16 = mybir.dt.bfloat16
I32 = mybir.dt.int32
ALU = mybir.AluOpType
ACT = mybir.ActivationFunctionType
X_AXIS = mybir.AxisListType.X

P = 128
NODES = 3125
EDGES = 53125
FEAT = 256
CHUNKS = FEAT // P
HEADS = 4
HEAD_DIM = FEAT // HEADS
EDGE_DIM = 16
NODE_TILES = -(-NODES // P)
LAST_ROWS = NODES - (NODE_TILES - 1) * P
EDGE_TILES = -(-EDGES // P)
ITEMS = EDGE_TILES + NODE_TILES - 1
BLOCKS = 4
IPB = ITEMS // BLOCKS
BIG = 1.0e30
LN_EPS = 1e-5
BN_EPS = 1e-5
GCN_COLS = FEAT + EDGE_DIM
L2_COLS = FEAT + 2 * HEADS
L3_COLS = FEAT + HEADS
OUT_COLS = FEAT + 2 * HEADS
NEG_GAT, NEG_L2 = 0.2, 0.01
PAIRS = P // EDGE_DIM
ATTR_COLS = EDGE_TILES * EDGE_DIM

assert IPB * BLOCKS == ITEMS and IPB <= P


def flat(ap):
    return ap.rearrange("p a b -> p (a b)")


def tile_loop(eng, count, unroll, body, first=0):
    main = count // unroll
    with eng.Fori(0, main) as i:
        for u in range(unroll):
            body(i * unroll + (first + u), (first + u) % unroll, i + (first + u) // unroll)
    for t in range(first + main * unroll, first + count):
        body(t, t % unroll, t // unroll)


def build(nc, io, out):
    ctx = ExitStack()

    def sb(name, shape, dt=F32):
        return ctx.enter_context(nc.sbuf_tensor(name, shape, dt))

    stage_sems = []

    def sem(name, kept=False):
        s = nc.alloc_semaphore(name=name)
        if not kept:
            stage_sems.append(s)
        return s

    def clear_sems():
        cleared = list(stage_sems)
        stage_sems.clear()
        for s in cleared:
            nc.sync.sem_clear(s)
        return cleared

    def free_sems(cleared):
        for s in cleared:
            nc.release_semaphore(s)

    def dram(name, shape, dt=F32):
        return nc.dram_tensor(name, shape, dt, kind="Internal").ap()

    class Chain:

        def __init__(self, eng, name):
            self.eng, self.sem, self.n = eng, sem(name), 0

        def mark(self, ins):
            self.n += 1
            ins.then_inc(self.sem, 1)

        def link(self, ins):
            self.mark(ins)
            self.eng.wait_ge(self.sem, self.n)

    idle = {e: sem(f"idle_{e}", kept=True) for e in ("act", "pool", "pe", "dve")}

    def hold(eng, who, s, value):
        eng.wait_ge(s, value)
        eng.sem_inc(idle[who], 1)

    with ctx:
        bank = [ctx.enter_context(nc.psum_tensor(f"bank{i}", [P, 512], F32)) for i in range(8)]
        x = sb("x", [P, NODE_TILES, FEAT])
        h = sb("h", [P, NODE_TILES, FEAT])
        acc = sb("acc", [P, NODE_TILES, GCN_COLS])
        xr_parts = sb("xr_parts", [P, NODE_TILES, 3, L3_COLS], BF16)
        ident = sb("ident", [P, P])
        ones = sb("ones", [P, P])
        p_index = sb("p_index", [P, 1])
        iota_b = sb("iota_b", [P, P], BF16)
        iota_t = sb("iota_t", [P, NODE_TILES])
        dst_col = sb("dst_col", [P, ITEMS])
        on_col = sb("on_col", [P, ITEMS])
        last_col = sb("last_col", [P, ITEMS])
        hi_col = sb("hi_col", [P, ITEMS])
        tile_col = sb("tile_col", [P, ITEMS])
        src_idx = sb("src_idx", [P, ITEMS], I32)
        item_tile = sb("item_tile", [1, ITEMS], I32)
        off_col = sb("off_col", [P, ITEMS])
        starts = sb("starts", [IPB, BLOCKS, P])
        keeps = sb("keeps", [IPB, BLOCKS, P])
        lasts = sb("lasts", [IPB, BLOCKS, P])
        starts_row = sb("starts_row", [1, ITEMS])
        keeps_row = sb("keeps_row", [1, ITEMS])
        tile_onehot = sb("tile_onehot", [IPB, BLOCKS, NODE_TILES])
        item_vals = sb("item_vals", [P, 2, ITEMS * HEADS])
        logits = item_vals[:, 0, :].rearrange("p (w h) -> p w h", h=HEADS)
        maxima = item_vals[:, 1, :].rearrange("p (w h) -> p w h", h=HEADS)
        sums_rhs = sb("sums_rhs", [P, ITEMS, 2 * HEADS])
        idx_ring = sb("idx_ring", [P, 2, 8], I32)
        stat = sb("stat", [P, 2, 6])
        moments = sb("moments", [P, 2, 2])
        rstd = sb("rstd", [P, NODE_TILES])
        shift = sb("shift", [P, NODE_TILES])
        small = [sb(f"small{i}", [P, NODE_TILES]) for i in range(4)]
        eps_col = sb("eps_col", [P, 1])
        dinv = sb("dinv", [P, NODE_TILES])
        g_ring = sb("g_ring", [P, 8, GCN_COLS])
        rings = flat(g_ring[:])
        h_ring = rings[:, 0:2 * FEAT].rearrange("p (s f) -> p s f", s=2)
        ht_ring = rings[:, 512:1024].rearrange("p (s k n) -> p s k n", s=2, k=CHUNKS)
        wbuf = sb("wbuf", [P, CHUNKS, 2 * L3_COLS])
        row_ring = rings[:, 1024:1024 + 2 * L2_COLS].rearrange("p (s f) -> p s f", s=2)
        spare = xr_parts[:].rearrange("p t k f -> p (t k f)")[:, 0:4 * 4096].bitcast(F32)
        work = [spare[:, i * 2048:(i + 1) * 2048] for i in range(4)] + [flat(h[:])[:, 0:2048]]

        item_tile_d = dram("item_tile_d", [ITEMS])
        edge_tile_d = dram("edge_tile_d", [ITEMS], I32)
        dst_rows_d = dram("dst_rows_d", [ITEMS * P], BF16)
        src_rows_d = dram("src_rows_d", [ITEMS * P], BF16)
        edge_attr_d = dram("edge_attr_d", [ITEMS * P, EDGE_DIM])
        attr_parts_d = dram("attr_parts_d", [PAIRS, P, ATTR_COLS], BF16)
        gcn_table = dram("gcn_table", [NODE_TILES * P, FEAT])
        l2_table = dram("l2_table", [NODE_TILES * P, L2_COLS])
        l3_table = dram("l3_table", [NODE_TILES * P, L3_COLS])

        loads = sem("loads", kept=True)
        dst_loaded = sem("dst_loaded")
        consts_i = sem("consts_i")
        pool_chain_s = sem("pool_chain")
        counts_ready = sem("counts_ready")
        sums_ready = sem("sums_ready")
        tile_ready = sem("tile_ready")
        tile_stored = sem("tile_stored")
        group_ready = sem("group_ready")
        lists_in = [sem(f"lists_in{b}", kept=True) for b in range(BLOCKS)]
        attrs_in = [sem(f"attrs_in{b}", kept=True) for b in range(BLOCKS)]
        attrs_out = [sem(f"attrs_out{b}", kept=True) for b in range(BLOCKS)]
        rows_ready = sem("rows_ready")
        rows_stored = sem("rows_stored")
        cols_ready = sem("cols_ready")
        cols_used = sem("cols_used")
        tile_back = sem("tile_back")
        edge_tile_stored = sem("edge_tile_stored")
        conv_done = sem("conv_done")

        starts_i = work[0][0:NODE_TILES, 0:EDGE_TILES].bitcast(I32)
        tile_starts = work[0][0:NODE_TILES, 512:512 + EDGE_TILES]
        counted = work[0][0:NODE_TILES, 1024:1024 + EDGE_TILES]
        threshold = work[0][0:NODE_TILES, 1536:1537]
        tile_count = work[0][0:NODE_TILES, 1540:1541]
        spread_counts = work[0][0:NODE_TILES, 1544:1544 + NODE_TILES]
        iota_i = sb("iota_i", [P, P], I32)
        items_i = sb("items_i", [IPB, BLOCKS], I32)
        items_f = sb("items_f", [IPB, BLOCKS])
        pidx_i = sb("pidx_i", [P, 1], I32)
        below = sb("below", [P, NODE_TILES])
        passed = work[1][0:IPB, 0:BLOCKS * NODE_TILES].rearrange("p (b t) -> p b t", b=BLOCKS)
        tile_of = sb("tile_of", [IPB, BLOCKS])
        base_of = sb("base_of", [IPB, BLOCKS])
        group_i = sb("group_i", [IPB, BLOCKS], I32)
        lists = flat(h[:])[0:IPB, 2048:6400]
        dst_ext_i = lists[:, 0:520].bitcast(I32).rearrange("p (b e) -> p b e", b=BLOCKS)
        dst_ext = lists[:, 520:1040].rearrange("p (b e) -> p b e", b=BLOCKS)
        src_i = lists[:, 1040:1552].bitcast(I32).rearrange("p (b e) -> p b e", b=BLOCKS)
        lo_i = work[1][0:IPB, 512:1024].bitcast(I32).rearrange("p (b e) -> p b e", b=BLOCKS)
        hi_i = work[1][0:IPB, 1024:1536].bitcast(I32).rearrange("p (b e) -> p b e", b=BLOCKS)
        src_f = work[2][0:IPB, 0:512].rearrange("p (b e) -> p b e", b=BLOCKS)
        hi_f = work[2][0:IPB, 512:1024].rearrange("p (b e) -> p b e", b=BLOCKS)
        loc = work[2][0:IPB, 1024:1536].rearrange("p (b e) -> p b e", b=BLOCKS)
        on = work[2][0:IPB, 1536:2048].rearrange("p (b e) -> p b e", b=BLOCKS)
        tmp = work[1][0:IPB, 1536:2048].rearrange("p (b e) -> p b e", b=BLOCKS)
        lo_b = lists[:, 1600:1856].bitcast(BF16).rearrange("p (b e) -> p b e", b=BLOCKS)
        loc_b = lists[:, 1856:2112].bitcast(BF16).rearrange("p (b e) -> p b e", b=BLOCKS)
        attr_stage = [work[3][0:IPB, :], flat(acc[:])[0:IPB, 0:2048]]
        item_least = sb("item_least", [IPB, 2, BLOCKS])

        with nc.Block() as block:
            @block.sync
            def _(sp):
                sp.dma_start(starts_i, io["tile_starts"].broadcast_to([NODE_TILES, EDGE_TILES])).then_inc(dst_loaded, 16)
                for t in range(5):
                    n = NODE_TILES // 5
                    if t < 4:
                        sp.dma_start(x[:, t * n:(t + 1) * n, :],
                                     io["x"][t * n * P:(t + 1) * n * P, :].rearrange("(t p) f -> p t f", p=P)
                                     ).then_inc(loads, 16)
                sp.dma_start(x[:, 20:24, :],
                             io["x"][20 * P:24 * P, :].rearrange("(t p) f -> p t f", p=P)).then_inc(loads, 16)
                sp.wait_ge(conv_done, 1)
                sp.dma_start(x[0:LAST_ROWS, NODE_TILES - 1, :], io["x"][(NODE_TILES - 1) * P:NODES, :]
                             ).then_inc(loads, 16)
                sp.wait_ge(tile_ready, 1)
                with nc.allow_non_contiguous_dma(reason="440 numbers, once"):
                    sp.dma_start(item_tile_d.rearrange("(b p) -> p b", b=BLOCKS), tile_of[:]).then_inc(tile_stored, 16)
                sp.wait_ge(tile_stored, 16)
                sp.dma_start(tile_col[:], item_tile_d.unsqueeze(0).broadcast_to([P, ITEMS])).then_inc(tile_back, 16)
                sp.wait_ge(group_ready, 1)
                with nc.allow_non_contiguous_dma(reason="440 numbers, once"):
                    sp.dma_start(edge_tile_d.rearrange("(b p) -> p b", b=BLOCKS), group_i[:]).then_inc(edge_tile_stored, 16)
                sp.wait_ge(edge_tile_stored, 16)
                sp.wait_ge(rows_ready, 2)
                for d, s in ((dst_rows_d, loc_b), (src_rows_d, lo_b)):
                    sp.dma_start(d.rearrange("(b p e) -> p b e", b=BLOCKS, e=P), s).then_inc(rows_stored, 16)
                sp.wait_ge(rows_stored, 32)
                sp.wait_ge(loads, 16 * 6)

            @block.gpsimd
            def _(pool):
                pool.iota(iota_i[:], [[1, P]], base=0, channel_multiplier=0).then_inc(consts_i, 1)
                pool.iota(pidx_i[:], [[0, 1]], base=0, channel_multiplier=1).then_inc(consts_i, 1)
                pool.iota(items_i[:], [[IPB, BLOCKS]], base=0, channel_multiplier=1).then_inc(consts_i, 1)
                pool.memset(ident[:], 0.0).then_inc(pool_chain_s, 1)
                pool.wait_ge(pool_chain_s, 1)
                pool.affine_select(out=ident[:], in_=ident[:], compare_op=ALU.not_equal, fill=1.0, base=0,
                                   pattern=[[-1, P]], channel_multiplier=1).then_inc(consts_i, 1)
                pool.wait_ge(group_ready, 1)
                for b in range(BLOCKS):
                    rows = bass.IndirectOffsetOnAxis(ap=group_i[:, b:b + 1], axis=0)
                    pool.indirect_dma_start(dst_ext_i[:, b, :], None, io["dst_ext"], rows).then_inc(lists_in[b], 16)
                    pool.indirect_dma_start(src_i[:, b, :], None, io["src_tiles"], rows).then_inc(lists_in[b], 16)

            @block.vector
            def _(dve):
                c = Chain(dve, "stage1_dve")
                c.mark(dve.memset(ones[:], 1.0))
                c.mark(dve.memset(eps_col[:], LN_EPS))
                dve.memset(x[:, NODE_TILES - 1, :], 0.0).then_inc(conv_done, 1)
                dve.wait_ge(consts_i, 4)
                c.mark(dve.tensor_copy(iota_b[:], iota_i[:]))
                c.mark(dve.tensor_copy(iota_t[:], iota_i[:, 0:NODE_TILES]))
                c.mark(dve.tensor_copy(p_index[:], pidx_i[:]))
                c.mark(dve.tensor_copy(items_f[:], items_i[:]))
                dve.wait_ge(dst_loaded, 16)
                c.mark(dve.tensor_copy(tile_starts, starts_i))
                dve.wait_ge(c.sem, c.n)
                c.link(dve.tensor_scalar(threshold, p_index[0:NODE_TILES, :], float(P), float(P), ALU.mult, ALU.add))
                c.link(dve.tensor_scalar(counted, tile_starts, threshold, 0.0, ALU.is_lt, ALU.add, accum_out=tile_count))
                c.link(dve.tensor_scalar(spread_counts, ident[0:NODE_TILES, 0:NODE_TILES], tile_count, None, ALU.mult))
                dve.sem_inc(counts_ready, 1)
                dve.wait_ge(sums_ready, 1)
                last = NODE_TILES - 1
                c.link(dve.tensor_scalar(below[:, 0:last], bank[0][:, 0:last], -1.0, 0.0, ALU.add, ALU.max))
                c.link(dve.tensor_tensor(below[:, 0:last], below[:, 0:last], iota_t[:, 0:last], ALU.add))
                c.link(dve.tensor_tensor(passed[:, :, 0:last], items_f[:].unsqueeze(2).broadcast_to([IPB, BLOCKS, last]),
                                         below[0:IPB, 0:last].unsqueeze(1).broadcast_to([IPB, BLOCKS, last]), ALU.is_gt))
                c.link(dve.tensor_reduce(tile_of[:], passed[:, :, 0:last], X_AXIS, ALU.add))
                dve.sem_inc(tile_ready, 1)
                c.link(dve.tensor_tensor(group_i[:], items_f[:], tile_of[:], ALU.subtract))
                dve.sem_inc(group_ready, 1)
                c.mark(dve.tensor_tensor(tile_onehot[:], tile_of[:].unsqueeze(2).broadcast_to([IPB, BLOCKS, NODE_TILES]),
                                         iota_t[0:IPB, :].unsqueeze(1).broadcast_to([IPB, BLOCKS, NODE_TILES]), ALU.is_equal))
                c.link(dve.tensor_scalar(base_of[:], tile_of[:], float(P), None, ALU.mult))
                for b in range(BLOCKS):
                    dve.wait_ge(lists_in[b], 32)
                c.link(dve.tensor_copy(dst_ext, dst_ext_i))
                cur = dst_ext[:, :, 1:P + 1]
                c.mark(dve.tensor_copy(src_f, src_i))
                c.mark(dve.tensor_scalar(lo_i, src_i, P - 1, None, ALU.bitwise_and))
                c.mark(dve.tensor_scalar(hi_i, src_i, 7, None, ALU.arith_shift_right))
                c.link(dve.tensor_tensor(loc, cur, base_of[:].unsqueeze(2).broadcast_to([IPB, BLOCKS, P]), ALU.subtract))
                dve.tensor_copy(lo_b, lo_i).then_inc(rows_ready, 1)
                c.mark(dve.tensor_copy(hi_f, hi_i))
                c.link(dve.tensor_scalar(tmp, loc, 0.0, None, ALU.is_ge))
                c.link(dve.scalar_tensor_tensor(out=on, in0=loc, scalar=float(P), in1=tmp, op0=ALU.is_lt, op1=ALU.mult))
                c.link(dve.scalar_tensor_tensor(out=loc, in0=loc, scalar=1.0, in1=on, op0=ALU.add, op1=ALU.mult))
                c.link(dve.tensor_scalar(loc, loc, -1.0, None, ALU.add))
                dve.tensor_copy(loc_b, loc).then_inc(rows_ready, 1)
                c.link(dve.tensor_tensor(tmp, cur, dst_ext[:, :, 0:P], ALU.not_equal))
                c.link(dve.scalar_tensor_tensor(out=starts[:], in0=tmp, scalar=-BIG, in1=on, op0=ALU.mult, op1=ALU.mult))
                c.link(dve.tensor_tensor(tmp, cur, dst_ext[:, :, 2:P + 2], ALU.not_equal))
                c.link(dve.tensor_tensor(lasts[:], tmp, on, ALU.mult))
                c.link(dve.tensor_scalar(keeps[:], lasts[:], -1.0, 1.0, ALU.mult, ALU.add))
                c.mark(dve.tensor_reduce(item_least[:, 0, :], starts[:], X_AXIS, ALU.min))
                c.link(dve.tensor_reduce(item_least[:, 1, :], keeps[:], X_AXIS, ALU.min))
                dve.sem_inc(cols_ready, 1)
                for n, table in enumerate((dst_col, on_col, last_col, src_idx, hi_col)):
                    dve.wait_ge(cols_used, n + 1)
                    c.mark(dve.tensor_copy(table[:], bank[1 + n][:, 0:ITEMS]))
                dve.wait_ge(cols_used, 6)
                c.mark(dve.tensor_copy(starts_row[:], bank[6][0:1, 0:ITEMS]))
                c.mark(dve.tensor_copy(keeps_row[:], bank[7][0:1, 0:ITEMS]))
                dve.wait_ge(c.sem, c.n)
                c.mark(dve.tensor_scalar(off_col[:], on_col[:], BIG, -BIG, ALU.mult, ALU.add))
                dve.wait_ge(tile_back, 16)
                c.link(dve.tensor_copy(item_tile[:], tile_col[0:1, :]))

            @block.tensor
            def _(pe):
                pe.wait_ge(counts_ready, 1)
                pe.matmul(bank[0][:, 0:NODE_TILES], ones[0:NODE_TILES, :], spread_counts, start=True, stop=True
                          ).then_inc(sums_ready, 1)
                pe.wait_ge(cols_ready, 1)
                for n, rows in enumerate((loc, on, lasts[:], src_f, hi_f)):
                    for b in range(BLOCKS):
                        ins = pe.transpose(bank[1 + n][:, b * IPB:(b + 1) * IPB], rows[:, b, :], ident[0:IPB, 0:IPB])
                    ins.then_inc(cols_used, 1)
                for n in range(2):
                    for b in range(BLOCKS):
                        ins = pe.transpose(bank[6 + n][0:1, b * IPB:(b + 1) * IPB], item_least[:, n, b:b + 1],
                                           ident[0:IPB, 0:IPB])
                ins.then_inc(cols_used, 1)

        class Norm:

            def __init__(self, layer):
                self.stats_ready = sem(f"stats_ready{layer}")
                self.var_ready = sem(f"var_ready{layer}")
                self.std_ready = sem(f"std_ready{layer}")
                self.rstd_ready = sem(f"rstd_ready{layer}")
                self.norm_ready = sem(f"norm_ready{layer}")
                self.rows_ready = sem(f"rows_ready{layer}")
                self.turned = sem(f"turned{layer}")
                self.cols_ready = sem(f"cols_ready{layer}")
                self.projected = sem(f"projected{layer}")
                self.out_free = sem(f"out_free{layer}")

        def pipelined(eng, steps):
            for i in range(NODE_TILES + max(lag for lag, _ in steps)):
                for lag, fn in steps:
                    if 0 <= i - lag < NODE_TILES:
                        t = i - lag
                        fn(t, t % 2, t // 2)

        LAG_SCALE, LAG_COLS, LAG_OUT = 2, 4, 6

        def column(table, t):
            return table[:, t:t + 1]

        def to_columns(eng, s, copy_cols):
            def cols(t, slot, rnd):
                eng.wait_ge(s.turned, t + 1)
                if t >= 2:
                    eng.wait_ge(s.projected, t - 1)
                copy_cols(slot).then_inc(s.cols_ready, 1)
            return cols

        def from_products(eng, s, finish):
            def products(t, slot, rnd):
                eng.wait_ge(s.projected, t + 1)
                finish(t, slot, rnd)
            return products

        def norm_tiles(dve, s, updates, copy_cols, finish, later=()):
            n = len(updates)

            def stats(t, slot, rnd):
                if updates:
                    updated, base = updates[-1][1]
                    dve.wait_ge(updated, t + base + 1)
                dve.bn_stats(stat[:, slot, :],
                             x[:, t, :]).then_inc(s.stats_ready, 1)

            def variance(t, slot, rnd):
                if t >= 2:
                    dve.wait_ge(s.norm_ready, t - 1)
                dve.wait_ge(s.stats_ready, t + 1)
                dve.bn_aggr(moments[:, slot, :], stat[:, slot, :]).then_inc(s.var_ready, 1)

            def scale(t, slot, rnd):
                dve.wait_ge(s.std_ready, t + 1)
                dve.reciprocal(column(rstd, t), column(small[2], t)).then_inc(s.rstd_ready, 1)

            def minus_mean(t, slot, rnd):
                dve.wait_ge(s.rstd_ready, t + 1)
                dve.scalar_tensor_tensor(out=column(shift, t), in0=moments[:, slot, 0:1], scalar=-1.0, in1=column(rstd, t),
                                         op0=ALU.mult, op1=ALU.mult).then_inc(s.norm_ready, 1)

            dve.sem_inc(s.out_free, 2)
            steps = [(k, fn) for k, (fn, _) in enumerate(updates)]
            pipelined(dve, steps[:1] + ([(n + LAG_OUT, from_products(dve, s, finish))] if finish else []) + steps[1:] + [
                (n, stats), (n + LAG_SCALE, scale)] + (
                [(n + LAG_COLS, to_columns(dve, s, copy_cols))] if copy_cols else []) + [
                (n + LAG_SCALE, minus_mean), (n, variance)] + list(later))

        def norm_rows(act, s, keep=None, later=()):
            def root(t, slot, rnd):
                act.wait_ge(s.var_ready, t + 1)
                act.activation(column(small[2], t), moments[:, slot, 1:2], ACT.Sqrt, bias=eps_col[:]).then_inc(s.std_ready, 1)

            def rows(t, slot, rnd):
                tile_x = x[:, t, :]
                kw = dict(bias=column(shift, t), scale=column(rstd, t))
                act.wait_ge(s.norm_ready, t + 1)
                if keep is None and t >= 2:
                    act.wait_ge(s.turned, t - 1)
                act.activation(h_ring[:, slot, :] if keep is None else keep[:, t, :], tile_x, ACT.Relu, **kw
                               ).then_inc(s.rows_ready, 1)
            pipelined(act, [(0, root), (LAG_SCALE, rows)] + list(later))

        def project(pe, s, groups, keep=None):
            def turn(t, slot, rnd):
                pe.wait_ge(s.rows_ready, t + 1)
                if t >= 2:
                    pe.wait_ge(s.cols_ready, t - 1)
                for k in range(CHUNKS):
                    rows = h_ring[:, slot, :] if keep is None else keep[:, t, :]
                    ins = pe.transpose(bank[slot][:, k * P:(k + 1) * P], rows[:, k * P:(k + 1) * P], ident[:])
                ins.then_inc(s.turned, 1)

            def multiply(t, slot, rnd):
                pe.wait_ge(s.cols_ready, t + 1)
                pe.wait_ge(s.out_free, t + 1)
                for b, lo, hi in groups:
                    for k in range(CHUNKS):
                        ins = pe.matmul(bank[2 + slot * len(groups) + b][:, 0:hi - lo], ht_ring[:, slot, k, :],
                                        wbuf[:, k, lo:hi], start=(k == 0), stop=(k == CHUNKS - 1))
                ins.then_inc(s.projected, 1)
            pipelined(pe, [(0, turn), (1, multiply)])

        def plain_cols(dve):
            return lambda slot: dve.tensor_copy(flat(ht_ring[:, slot, :, :]), bank[slot][:, 0:FEAT])

        run_max = flat(acc[:])[0:IPB, 0:2048].rearrange("p (g e) -> p g e", e=P)
        seg_max = flat(acc[:])[0:IPB, 2048:4096].rearrange("p (g e) -> p g e", e=P)
        lasts_max = flat(acc[:])[0:IPB, 4096:6144].rearrange("p (g e) -> p g e", e=P)
        ends = flat(acc[:])[0:IPB, 6144:6160]
        carries = flat(acc[:])[0:IPB, 6160:6176]
        states = flat(sums_rhs[:])[0:1, 0:HEADS * (ITEMS + 1)].rearrange("p (h w) -> p h w", h=HEADS)

        class Segments:
            def __init__(self, name):
                self.rows = sem(f"seg_rows_{name}")
                self.ends = sem(f"seg_ends_{name}")
                self.turned = sem(f"seg_turned_{name}")
                self.states = sem(f"seg_states_{name}")
                self.carried = sem(f"seg_carried_{name}")
                self.found = sem(f"seg_found_{name}")
                self.cols = sem(f"seg_cols_{name}")

        def segment_max_pe(pe, s, values, heads, ready):
            pe.wait_ge(ready, 1)
            for hd in range(heads):
                for b in range(BLOCKS):
                    ins = pe.transpose(bank[hd][0:IPB, b * P:(b + 1) * P], values[:, b * IPB:(b + 1) * IPB, hd], ident[:])
                ins.then_inc(s.rows, 1)
            for way in range(2):
                pe.wait_ge(s.ends, way + 1)
                for hd in range(heads):
                    for b in range(BLOCKS):
                        g = hd * BLOCKS + b
                        ins = pe.transpose(bank[4 + hd][0:1, b * IPB:(b + 1) * IPB], ends[:, g:g + 1], ident[0:IPB, 0:IPB])
                ins.then_inc(s.turned, 1)
                pe.wait_ge(s.states, way + 1)
                for hd in range(heads):
                    for b in range(BLOCKS):
                        g = hd * BLOCKS + b
                        at = b * IPB + way
                        ins = pe.transpose(bank[4][0:IPB, g:g + 1], states[:, hd, at:at + IPB], ident[0:1, 0:1])
                ins.then_inc(s.carried, 1)
            pe.wait_ge(s.found, 1)
            for hd in range(heads):
                for b in range(BLOCKS):
                    ins = pe.transpose(bank[hd][:, b * IPB:(b + 1) * IPB], seg_max[:, hd * BLOCKS + b, :],
                                       ident[0:IPB, 0:IPB])
                ins.then_inc(s.cols, 1)

        def segment_max_dve(dve, c, s, result, heads):
            groups = [(hd, b) for hd in range(heads) for b in range(BLOCKS)]
            n = len(groups)

            def forward(initial):
                for g, (hd, b) in enumerate(groups):
                    c.mark(dve.tensor_tensor_scan(run_max[:, g, :], starts[:, b, :], bank[hd][0:IPB, b * P:(b + 1) * P],
                                                  initial(g), ALU.add, ALU.max))
                dve.wait_ge(c.sem, c.n)

            def backward(initial):
                for g, (hd, b) in enumerate(groups):
                    c.mark(dve.tensor_tensor_scan(seg_max[:, g, ::-1], keeps[:, b, ::-1], lasts_max[:, g, ::-1],
                                                  initial(g), ALU.mult, ALU.add))
                dve.wait_ge(c.sem, c.n)

            dve.wait_ge(s.rows, heads)
            forward(lambda g: -BIG)
            dve.tensor_copy(ends[:, 0:n], run_max[:, 0:n, P - 1]).then_inc(s.ends, 1)
            c.link(dve.memset(states[:, 0:heads, 0:1], -BIG))
            dve.wait_ge(s.turned, 1)
            for hd in range(heads):
                c.mark(dve.tensor_tensor_scan(states[:, hd, 1:ITEMS + 1], starts_row[:], bank[4 + hd][0:1, 0:ITEMS],
                                              -BIG, ALU.add, ALU.max))
            dve.wait_ge(c.sem, c.n)
            dve.sem_inc(s.states, 1)
            dve.wait_ge(s.carried, 1)
            c.link(dve.tensor_copy(carries[:, 0:n], bank[4][0:IPB, 0:n]))
            forward(lambda g: carries[:, g:g + 1])
            for hd in range(heads):
                c.mark(dve.tensor_tensor(lasts_max[:, hd * BLOCKS:(hd + 1) * BLOCKS, :], lasts[:],
                                         run_max[:, hd * BLOCKS:(hd + 1) * BLOCKS, :], ALU.mult))
            dve.wait_ge(c.sem, c.n)
            backward(lambda g: 0.0)
            dve.tensor_copy(ends[:, 0:n], seg_max[:, 0:n, 0]).then_inc(s.ends, 1)
            c.link(dve.memset(states[:, 0:heads, ITEMS:ITEMS + 1], 0.0))
            dve.wait_ge(s.turned, 2)
            for hd in range(heads):
                c.mark(dve.tensor_tensor_scan(states[:, hd, 0:ITEMS][:, ::-1], keeps_row[:, ::-1],
                                              bank[4 + hd][0:1, 0:ITEMS][:, ::-1], 0.0, ALU.mult, ALU.add))
            dve.wait_ge(c.sem, c.n)
            dve.sem_inc(s.states, 1)
            dve.wait_ge(s.carried, 2)
            c.link(dve.tensor_copy(carries[:, 0:n], bank[4][0:IPB, 0:n]))
            backward(lambda g: carries[:, g:g + 1])
            dve.sem_inc(s.found, 1)
            for hd in range(heads):
                dve.wait_ge(s.cols, hd + 1)
                c.mark(dve.tensor_copy(result[:, :, hd], bank[hd][:, 0:ITEMS]))
            dve.wait_ge(c.sem, c.n)

        s0 = Norm(0)
        l0_loads = sem("l0_loads")
        attn = sb("attn", [P, 6])
        gate = sb("gate", [P, NODE_TILES])
        z = sb("z", [P, NODE_TILES, 2])
        node_vals = sb("node_vals", [P, 4, NODE_TILES])
        node_rest = sb("node_rest", [P, 2, 4 * NODE_TILES])
        node_parts = sb("node_parts", [P, 3, 4 * NODE_TILES], BF16)

        with nc.Block() as block:
            @block.sync
            def _(sp):
                sp.dma_start(wbuf[:, :, 0:2], io["l0_w"]).then_inc(l0_loads, 16)
                sp.dma_start(attn[:], io["l0_attn"].broadcast_to([P, 6])).then_inc(l0_loads, 16)
                sp.dma_start(gate[:], io["gate"]).then_inc(l0_loads, 16)
                for b in range(BLOCKS):
                    sp.wait_ge(attrs_in[b], 16)
                    sp.dma_start(edge_attr_d[b * IPB * P:(b + 1) * IPB * P, :].rearrange("(p e) f -> p (e f)", e=P),
                                 attr_stage[b % 2]).then_inc(attrs_out[b], 16)
                for b in range(BLOCKS):
                    sp.wait_ge(attrs_out[b], 16)
                sp.wait_ge(l0_loads, 48)

            @block.gpsimd
            def _(pool):
                for b in range(BLOCKS):
                    if b >= 2:
                        pool.wait_ge(attrs_out[b - 2], 16)
                    pool.indirect_dma_start(attr_stage[b % 2], None, io["edge_attr"],
                                            bass.IndirectOffsetOnAxis(ap=group_i[:, b:b + 1], axis=0)).then_inc(attrs_in[b], 16)

            @block.scalar
            def _(act):
                norm_rows(act, s0, keep=h)

            @block.tensor
            def _(pe):
                pe.wait_ge(l0_loads, 48)
                project(pe, s0, [(0, 0, 2)], keep=h)

            @block.vector
            def _(dve):
                c = Chain(dve, "stage2_dve")

                def keep_z(t, slot, rnd):
                    dve.tensor_copy(z[:, bass.ds(t, 1), :].rearrange("p a k -> p (a k)"), bank[2 + slot][:, 0:2]
                                    ).then_inc(s0.out_free, 1)
                norm_tiles(dve, s0, [], plain_cols(dve), keep_z)
                dve.wait_ge(s0.out_free, 2 + NODE_TILES)
                dve.wait_ge(l0_loads, 48)
                for k in range(2):
                    c.mark(dve.tensor_copy(node_vals[:, 1 + k, :], z[:, :, k]))
                for row, at in ((0, 0), (3, 2)):
                    c.link(dve.tensor_scalar(node_vals[:, row, :], z[:, :, 0], attn[:, at:at + 1], None, ALU.mult))
                    c.link(dve.scalar_tensor_tensor(out=node_vals[:, row, :], in0=z[:, :, 1], scalar=attn[:, at + 1:at + 2],
                                                    in1=node_vals[:, row, :], op0=ALU.mult, op1=ALU.add))
                whole = flat(node_vals[:])
                c.link(dve.tensor_copy(node_parts[:, 0, :], whole))
                c.link(dve.tensor_tensor(node_rest[:, 0, :], whole, node_parts[:, 0, :], ALU.subtract))
                c.link(dve.tensor_copy(node_parts[:, 1, :], node_rest[:, 0, :]))
                c.link(dve.tensor_tensor(node_rest[:, 1, :], node_rest[:, 0, :], node_parts[:, 1, :], ALU.subtract))
                c.link(dve.tensor_copy(node_parts[:, 2, :], node_rest[:, 1, :]))

        CHUNK = 4
        CHUNK_EDGES = CHUNK * P
        EDGE_CHUNKS = ITEMS // CHUNK
        VALS = 3 * NODE_TILES
        ROW_SLOTS = 4
        edge_rows = flat(acc[:])[:, 3072:3072 + ROW_SLOTS * CHUNK_EDGES].bitcast(BF16).rearrange(
            "p (s k e) -> p s k e", s=ROW_SLOTS, k=2)
        place_ring = sb("place_ring", [P, 2, 2, CHUNK_EDGES], BF16)
        picked = flat(acc[:])[:, 200:800].rearrange("p (s u v n) -> p s u v n", s=2, u=CHUNK, v=3)
        er_parts = flat(acc[:])[:, 800:800 + 3 * ITEMS // 2].bitcast(BF16).rearrange("p (w k) -> p w k", k=3)
        er_rest = spare[:, 0:2 * ITEMS].rearrange("p (k w) -> p k w", k=2)
        er_picked = spare[:, 2048:2048 + 3 * ITEMS].rearrange("p (w k) -> p w k", k=3)
        er_edges = spare[:, 3584:3584 + ITEMS]
        er_turned = spare[0:NODE_TILES, 1024:1024 + P]
        tiles_turned = spare[0:NODE_TILES, 1280:1280 + ITEMS]
        er_items = bank[7][:, 0:ITEMS]
        edge_vals = maxima
        er_turned_ready = sem("er_turned_ready")
        er_rows_ready = sem("er_rows_ready")
        er_items_ready = sem("er_items_ready")
        er_split = sem("er_split")
        rows_in = [sem(f"rows_in{u}") for u in range(ROW_SLOTS)]
        place_ready = sem("place_ready")
        vals_ready = sem("vals_ready")
        masks_done = sem("masks_done")
        picks_done = sem("picks_done")
        reduced = sem("reduced")

        SPLIT = 512
        SPLITS = ATTR_COLS // SPLIT
        split_memory = spare[:, 4096:]
        attr_in = split_memory[:, 0:2 * SPLIT].rearrange("p (s c) -> p s c", s=2)
        attr_rest = split_memory[:, 1024:1024 + 4 * SPLIT].rearrange("p (s k c) -> p s k c", s=2, k=2)
        attr_parts = flat(acc[:])[:, 1536:1536 + 3 * SPLIT].bitcast(BF16).rearrange("p (s k c) -> p s k c", s=2, k=3)
        attr_loaded = [sem(f"attr_loaded{u}") for u in range(2)]
        part_ready = sem("part_ready")
        MASKS = EDGE_CHUNKS // SPLITS
        off_tile = flat(g_ring[:])[:, 0:400].rearrange("p (s k u n) -> p s k u n", s=2, k=2, u=CHUNK)
        tile_mask = flat(g_ring[:])[:, 400:400 + MASKS * CHUNK * NODE_TILES].rearrange("p (s u n) -> p s u n", s=MASKS, u=CHUNK)
        distances = sem("distances")
        rest_made = sem("rest_made")
        parts_out = [sem(f"parts_out{u}") for u in range(2)]

        with nc.Block() as block:
            @block.scalar
            def _(act):
                def load_attrs(t, slot):
                    act.dma_start(attr_in[:, slot, :], io["attr_t"][:, bass.ds(t * SPLIT, SPLIT)]).then_inc(attr_loaded[slot], 16)

                def part(t, slot, rnd, k):
                    if k == 0:
                        act.wait_ge(attr_loaded[slot], rnd * 16 + 16)
                        if not (isinstance(t, int) and t < 2):
                            act.wait_ge(parts_out[slot], rnd * 48)
                        act.copy(attr_parts[:, slot, 0, :], attr_in[:, slot, :]).then_inc(part_ready, 1)
                    else:
                        act.wait_ge(rest_made, t * 2 + k)
                        act.copy(attr_parts[:, slot, k, :], attr_rest[:, slot, k - 1, :]).then_inc(part_ready, 1)

                def store_part(t, slot, k):
                    lo, hi = k * 3, min(k * 3 + 3, PAIRS)
                    act.wait_ge(part_ready, t * 3 + (k + 1))
                    act.dma_start(attr_parts_d[lo:hi, :, bass.ds(t * SPLIT, SPLIT)].rearrange("b p c -> p b c"),
                                  attr_parts[:, slot, k:k + 1, :].broadcast_to([P, hi - lo, SPLIT])).then_inc(parts_out[slot], 16)

                def mask(t, slot):
                    if not (isinstance(t, int) and t < MASKS):
                        act.wait_ge(picks_done, t - (MASKS - 1))
                    act.wait_ge(distances, t * 2 + 2)
                    act.activation(tile_mask[:, slot, :, :], off_tile[:, slot % 2, 1, :, :], ACT.Relu, scale=-1.0, bias=ones[:, 0:1]
                                   ).then_inc(masks_done, 1)

                def masks_and_split(t, slot, rnd, more=True):
                    part(t, slot, rnd, 0)
                    for m in range(MASKS):
                        mask(t * MASKS + m, m)
                        if m == 2:
                            store_part(t, slot, 0)
                        if m == 5:
                            part(t, slot, rnd, 1)
                        if m == 6:
                            store_part(t, slot, 1)
                    part(t, slot, rnd, 2)
                    store_part(t, slot, 2)
                    if more:
                        load_attrs(t + 2, slot)
                load_attrs(0, 0)
                load_attrs(1, 1)
                masks_and_split(0, 0, 0)
                masks_and_split(1, 1, 0)
                tile_loop(act, SPLITS - 5, 2, masks_and_split, first=2)
                for t in range(SPLITS - 3, SPLITS):
                    masks_and_split(t, t % 2, t // 2, more=t + 2 < SPLITS)
                for t in range(MASKS * SPLITS, EDGE_CHUNKS):
                    mask(t, t % MASKS)
                for u in range(2):
                    act.wait_ge(parts_out[u], (SPLITS + 1 - u) // 2 * 48)

            @block.gpsimd
            def _(pool):
                def rest(t, slot, k):
                    pool.wait_ge(part_ready, t * 3 + (k + 1))
                    pool.tensor_tensor(attr_rest[:, slot, k, :], (attr_in[:, slot, :], attr_rest[:, slot, 0, :])[k],
                                       attr_parts[:, slot, k, :], ALU.subtract).then_inc(rest_made, 1)

                def distance(t, slot):
                    if not (isinstance(t, int) and t < 2):
                        hold(pool, "pool", masks_done, t - 1)
                    pool.tensor_tensor(off_tile[:, slot, 0, :, :],
                                       hi_col[:, bass.ds(t * CHUNK, CHUNK)].unsqueeze(2).broadcast_to([P, CHUNK, NODE_TILES]),
                                       iota_t[:].unsqueeze(1).broadcast_to([P, CHUNK, NODE_TILES]), ALU.subtract
                                       ).then_inc(distances, 1)
                    pool.wait_ge(distances, t * 2 + 1)
                    pool.tensor_tensor(off_tile[:, slot, 1, :, :], off_tile[:, slot, 0, :, :], off_tile[:, slot, 0, :, :], ALU.mult
                                       ).then_inc(distances, 1)

                def distances_and_rest(t, slot, rnd):
                    for m in range(MASKS):
                        distance(t * MASKS + m, m % 2)
                        if m == 3:
                            rest(t, slot, 0)
                    rest(t, slot, 1)
                distances_and_rest(0, 0, 0)
                distances_and_rest(1, 1, 0)
                tile_loop(pool, SPLITS - 2, 2, distances_and_rest, first=2)
                for t in range(MASKS * SPLITS, EDGE_CHUNKS):
                    distance(t, t % 2)

            @block.sync
            def _(sp):
                def load(t, slot, rnd):
                    if not (isinstance(t, int) and t < ROW_SLOTS):
                        sp.wait_ge(place_ready, t - (ROW_SLOTS - 1))
                    for k, d in enumerate((src_rows_d, dst_rows_d)):
                        sp.dma_start(edge_rows[:, slot, k, :],
                                     d[bass.ds(t * CHUNK_EDGES, CHUNK_EDGES)].unsqueeze(0).broadcast_to([P, CHUNK_EDGES])
                                     ).then_inc(rows_in[slot], 16)
                for t in range(ROW_SLOTS):
                    load(t, t, 0)
                tile_loop(sp, EDGE_CHUNKS - ROW_SLOTS, ROW_SLOTS, load, first=ROW_SLOTS)

            @block.tensor
            def _(pe):
                pe.transpose(bank[6][0:NODE_TILES, 0:P], node_vals[:, 3, :], ident[:])
                for b in range(BLOCKS):
                    ins = pe.transpose(bank[4][0:NODE_TILES, b * IPB:(b + 1) * IPB], tile_onehot[:, b, :], ident[0:IPB, 0:IPB])
                ins.then_inc(er_turned_ready, 1)
                pe.wait_ge(er_rows_ready, 1)
                pe.matmul(er_items, er_turned, tiles_turned, start=True, stop=True).then_inc(er_items_ready, 1)
                pe.wait_ge(er_split, 1)

                def pick(t, slot, rnd):
                    pe.wait_ge(place_ready, t + 1)
                    if not (isinstance(t, int) and t < 2):
                        pe.wait_ge(picks_done, t - 1)
                    for u in range(CHUNK):
                        e = slice(u * P, (u + 1) * P)
                        for part in range(3):
                            pe.matmul(bank[slot][:, u * VALS:(u + 1) * VALS], place_ring[:, slot, 0, e],
                                      node_parts[:, part, 0:VALS], start=(part == 0), stop=(part == 2))
                        ins = pe.matmul(bank[slot][:, CHUNK * VALS + u * 3:CHUNK * VALS + u * 3 + 3], place_ring[:, slot, 1, e],
                                        er_parts[:, bass.ds(t * CHUNK + u, 1), :].rearrange("p a k -> p (a k)"), start=True, stop=True)
                    ins.then_inc(vals_ready, 1)
                pick(0, 0, 0)
                pick(1, 1, 0)
                tile_loop(pe, EDGE_CHUNKS - 2, 2, pick, first=2)

            @block.vector
            def _(dve):
                c = Chain(dve, "stage3_dve")
                dve.wait_ge(er_turned_ready, 1)
                c.mark(dve.tensor_copy(er_turned, bank[6][0:NODE_TILES, 0:P]))
                c.link(dve.tensor_copy(tiles_turned, bank[4][0:NODE_TILES, 0:ITEMS]))
                dve.sem_inc(er_rows_ready, 1)
                dve.wait_ge(er_items_ready, 1)
                c.link(dve.tensor_copy(er_parts[:, :, 0], er_items))
                c.link(dve.tensor_tensor(er_rest[:, 0, :], er_items, er_parts[:, :, 0], ALU.subtract))
                c.link(dve.tensor_copy(er_parts[:, :, 1], er_rest[:, 0, :]))
                c.link(dve.tensor_tensor(er_rest[:, 1, :], er_rest[:, 0, :], er_parts[:, :, 1], ALU.subtract))
                c.link(dve.tensor_copy(er_parts[:, :, 2], er_rest[:, 1, :]))
                dve.sem_inc(er_split, 1)

                def places(t, slot, row_slot, rnd):
                    dve.wait_ge(rows_in[row_slot], rnd * 32 + 32)
                    if not (isinstance(t, int) and t < 2):
                        dve.wait_ge(vals_ready, t - 1)
                    dve.tensor_scalar(place_ring[:, slot, :, :].rearrange("p k e -> p (k e)"),
                                      edge_rows[:, row_slot, :, :].rearrange("p k e -> p (k e)"),
                                      p_index[:], None, ALU.is_equal).then_inc(place_ready, 1)

                def pick(t, mask_slot):
                    slot = mask_slot % 2
                    dve.wait_ge(vals_ready, t + 1)
                    dve.wait_ge(masks_done, t + 1)
                    if not (isinstance(t, int) and t < 2):
                        dve.wait_ge(reduced, t - 1)
                    dve.tensor_tensor(picked[:, slot, :, :, :], bank[slot][:, 0:CHUNK * VALS].rearrange("p (u v n) -> p u v n", u=CHUNK, v=3),
                                      tile_mask[:, mask_slot, :, :].unsqueeze(2).broadcast_to([P, CHUNK, 3, NODE_TILES]), ALU.mult)
                    dve.tensor_copy(er_picked[:, bass.ds(t * CHUNK, CHUNK), :].rearrange("p u k -> p (u k)"),
                                    bank[slot][:, CHUNK * VALS:CHUNK * VALS + CHUNK * 3]).then_inc(picks_done, 1)

                def add(t, slot):
                    hold(dve, "dve", picks_done, t + 1)
                    dve.tensor_reduce(edge_vals[:, bass.ds(t * CHUNK, CHUNK), 0:3], picked[:, slot, :, :, :], X_AXIS, ALU.add
                                      ).then_inc(reduced, 1)

                def three(t, u, rnd):
                    places(t, u % 2, u % ROW_SLOTS, rnd * (MASKS // ROW_SLOTS) + u // ROW_SLOTS)
                    pick(t - 1, (u - 1) % MASKS)
                    add(t - 2, u % 2)
                places(0, 0, 0, 0)
                places(1, 1, 1, 0)
                pick(0, 0)
                three(2, 2, 0)
                three(3, 3, 0)
                tile_loop(dve, EDGE_CHUNKS - 4, MASKS, three, first=4)
                pick(EDGE_CHUNKS - 1, (EDGE_CHUNKS - 1) % MASKS)
                for t in (EDGE_CHUNKS - 2, EDGE_CHUNKS - 1):
                    add(t, t % 2)

        seg0 = Segments("l0")
        sum_parts = flat(item_vals[:])[:, 0:ITEMS * 6].bitcast(BF16).rearrange("p (w k v) -> p w k v", k=3, v=4)
        sum_rests = [flat(acc[:])[:, k * ITEMS * 4:(k + 1) * ITEMS * 4].rearrange("p (w v) -> p w v", v=4) for k in range(2)]
        masked0 = sem("masked0")
        less0 = sem("less0")
        exp0 = sem("exp0")
        scores = logits[:, :, 0:1]
        top = logits[:, :, 1:2]

        with nc.Block() as block:
            @block.tensor
            def _(pe):
                segment_max_pe(pe, seg0, scores, 1, masked0)

            @block.scalar
            def _(act):
                act.wait_ge(less0, 1)
                act.activation(sums_rhs[:, :, 0], logits[:, :, 2], ACT.Exp).then_inc(exp0, 1)

            @block.vector
            def _(dve):
                c = Chain(dve, "stage4_dve")
                el, z0, z1 = (edge_vals[:, :, k] for k in range(3))
                c.link(dve.tensor_tensor(er_edges, er_picked[:, :, 0], er_picked[:, :, 1], ALU.add))
                c.link(dve.tensor_tensor(er_edges, er_edges, er_picked[:, :, 2], ALU.add))
                score = logits[:, :, 0]
                c.link(dve.tensor_tensor(score, er_edges, el, ALU.add))
                c.link(dve.scalar_tensor_tensor(out=score, in0=score, scalar=NEG_GAT, in1=score, op0=ALU.mult, op1=ALU.max))
                c.link(dve.tensor_tensor(score, score, off_col[:], ALU.add))
                dve.sem_inc(masked0, 1)
                segment_max_dve(dve, c, seg0, top, 1)
                dve.tensor_tensor(logits[:, :, 2], score, logits[:, :, 1], ALU.subtract).then_inc(less0, 1)
                c.mark(dve.memset(sums_rhs[:, :, 3], 1.0))
                dve.wait_ge(exp0, 1)
                c.mark(dve.tensor_tensor(sums_rhs[:, :, 1], sums_rhs[:, :, 0], z0, ALU.mult))
                c.link(dve.tensor_tensor(sums_rhs[:, :, 2], sums_rhs[:, :, 0], z1, ALU.mult))
                c.link(dve.tensor_copy(sum_parts[:, :, 0, :], sums_rhs[:, :, 0:4]))
                c.link(dve.tensor_tensor(sum_rests[0], sums_rhs[:, :, 0:4], sum_parts[:, :, 0, :], ALU.subtract))
                c.link(dve.tensor_copy(sum_parts[:, :, 1, :], sum_rests[0]))
                c.link(dve.tensor_tensor(sum_rests[1], sum_rests[0], sum_parts[:, :, 1, :], ALU.subtract))
                c.link(dve.tensor_copy(sum_parts[:, :, 2, :], sum_rests[1]))

        onehot = sb("onehot", [P, 8, P])
        GROUP = 8
        onehot_b = flat(onehot[:]).bitcast(BF16).rearrange("p (u n) -> p u n", n=P)
        sums_by_part = spare[:, 0:ITEMS * 12].rearrange("p (w k v) -> p w k v", k=3, v=4)
        item_sums = sum_rests[0]
        onehot_ready = sem("onehot_ready")
        sums_ready0 = sem("sums_ready0")
        sums_free0 = sem("sums_free0")
        values_ring = rings[:, 0:2 * GROUP * 6].bitcast(BF16).rearrange("p (s f) -> p s f", s=2)
        values_ready = sem("values_ready")

        with nc.Block() as block:
            @block.vector
            def _(dve):
                c = Chain(dve, "stage5_dve")

                def make(t, slot, rnd):
                    if not (isinstance(t, int) and t < 2):
                        dve.wait_ge(sums_ready0, t - 1)
                    dve.tensor_tensor(onehot_b[:, slot * GROUP:(slot + 1) * GROUP, :],
                                      iota_b[:].unsqueeze(1).broadcast_to([P, GROUP, P]),
                                      dst_col[:, bass.ds(t * GROUP, GROUP)].unsqueeze(2).broadcast_to([P, GROUP, P]),
                                      ALU.is_equal).then_inc(onehot_ready, 1)
                make(0, 0, 0)
                make(1, 1, 0)
                tile_loop(dve, ITEMS // GROUP - 2, 2, make, first=2)
                dve.wait_ge(sums_free0, 2 + ITEMS // GROUP)
                c.link(dve.tensor_tensor(item_sums, sums_by_part[:, :, 2, :], sums_by_part[:, :, 1, :], ALU.add))
                c.link(dve.tensor_tensor(item_sums, item_sums, sums_by_part[:, :, 0, :], ALU.add))

            @block.tensor
            def _(pe):
                def add_up(t, slot, rnd):
                    pe.wait_ge(onehot_ready, t + 1)
                    pe.wait_ge(sums_free0, t + 1)
                    pe.wait_ge(values_ready, t + 1)
                    for u in range(GROUP):
                        ins = pe.matmul(bank[slot][:, u * 12:u * 12 + 12], onehot_b[:, slot * GROUP + u, :],
                                        values_ring[:, slot, u * 12:u * 12 + 12], start=True, stop=True)
                    ins.then_inc(sums_ready0, 1)
                tile_loop(pe, ITEMS // GROUP, 2, add_up)

            @block.scalar
            def _(act):
                act.sem_inc(sums_free0, 2)

                def stage_values(t, slot):
                    act.copy(values_ring[:, slot, :], sum_parts[:, bass.ds(t * GROUP, GROUP), :, :].rearrange("p w k v -> p (w k v)")
                             ).then_inc(values_ready, 1)

                def keep(t, slot, rnd):
                    if not (isinstance(t, int) and t + 1 >= ITEMS // GROUP):
                        stage_values(t + 1, 1 - slot)
                    hold(act, "act", sums_ready0, t + 1)
                    act.copy(sums_by_part[:, bass.ds(t * GROUP, GROUP), :, :].rearrange("p a k v -> p (a k v)"),
                             bank[slot][:, 0:GROUP * 12]).then_inc(sums_free0, 1)
                stage_values(0, 0)
                tile_loop(act, ITEMS // GROUP, 2, keep)

        s1 = Norm(1)
        l1_loads = sem("l1_loads")
        turned_sums = sem("turned_sums")
        sums_rows = sem("sums_rows")
        node_sums = sem("node_sums")
        squares = sem("squares")
        roots = sem("roots")
        gates_in = sem("gates_in")
        gates = sem("gates")
        norm1 = sb("norm1", [P, 4, CHUNKS])
        bn_scale = sb("bn_scale", [P, CHUNKS])
        bn_shift = sb("bn_shift", [P, CHUNKS])
        bn_root = sb("bn_root", [P, CHUNKS])
        bn_in = sb("bn_in", [P, CHUNKS])
        item_rows = work[1][0:IPB, :].rearrange("p (v b n) -> p v b n", v=4, b=BLOCKS)
        by_node = bank[4][:, 0:4 * NODE_TILES].rearrange("p (v t) -> p v t", v=4)
        degree1 = sb("degree1", [P, NODE_TILES])
        degree_root = sb("degree_root", [P, NODE_TILES])
        gate_arg = sb("gate_arg", [P, NODE_TILES])
        gate_out = sb("gate_out", [P, NODE_TILES])
        gated = sem("gated")
        gcn_stored = sem("gcn_stored")

        with nc.Block() as block:
            @block.sync
            def _(sp):
                sp.dma_start(wbuf[:, :, 0:FEAT], io["l1_w"]).then_inc(l1_loads, 16)
                sp.dma_start(norm1[:], io["l1_norm"]).then_inc(l1_loads, 16)

                def store(t, slot, rnd):
                    sp.wait_ge(s1.out_free, t + 3)
                    sp.dma_start(gcn_table[bass.ds(t * P, P), :],
                                 h[:, bass.ds(t, 1), :].rearrange("p a f -> p (a f)")).then_inc(gcn_stored, 16)
                tile_loop(sp, NODE_TILES, 5, store)
                sp.wait_ge(gcn_stored, 16 * NODE_TILES)

            @block.tensor
            def _(pe):
                for v in range(4):
                    for b in range(BLOCKS):
                        ins = pe.transpose(bank[v][0:IPB, b * P:(b + 1) * P], item_sums[:, b * IPB:(b + 1) * IPB, v], ident[:])
                    ins.then_inc(turned_sums, 1)
                for v in range(4):
                    pe.wait_ge(sums_rows, v + 1)
                    for b in range(BLOCKS):
                        ins = pe.matmul(by_node[:, v, :], item_rows[:, v, b, :], tile_onehot[:, b, :],
                                        start=(b == 0), stop=(b == BLOCKS - 1))
                ins.then_inc(node_sums, 1)
                pe.wait_ge(l1_loads, 32)
                project(pe, s1, [(0, 0, FEAT)])

            @block.scalar
            def _(act):
                act.wait_ge(squares, 1)
                act.activation(degree_root[:], degree1[:], ACT.Sqrt)
                act.activation(bn_root[:], bn_in[:], ACT.Sqrt).then_inc(roots, 1)
                act.wait_ge(gates_in, 1)
                act.activation(gate_out[:], gate_arg[:], ACT.Sigmoid).then_inc(gates, 1)
                norm_rows(act, s1)

            @block.vector
            def _(dve):
                c = Chain(dve, "stage6_dve")
                for v in range(4):
                    dve.wait_ge(turned_sums, v + 1)
                    dve.tensor_copy(item_rows[:, v, :, :].rearrange("p b n -> p (b n)"), bank[v][0:IPB, :]).then_inc(sums_rows, 1)
                dve.wait_ge(l1_loads, 32)
                c.mark(dve.tensor_scalar(bn_in[:], norm1[:, 3, :], BN_EPS, None, ALU.add))
                dve.wait_ge(node_sums, 1)
                c.mark(dve.tensor_scalar(small[0][:], by_node[:, 0, :], 0.0, None, ALU.is_equal))
                c.link(dve.tensor_scalar(degree1[:], by_node[:, 3, :], 1.0, None, ALU.add))
                dve.sem_inc(squares, 1)
                c.link(dve.tensor_tensor(small[0][:], small[0][:], by_node[:, 0, :], ALU.add))
                c.link(dve.reciprocal(small[0][:], small[0][:]))
                for k in range(2):
                    c.link(dve.tensor_tensor(small[1 + k][:], by_node[:, 1 + k, :], small[0][:], ALU.mult))
                    c.link(dve.tensor_scalar(small[1 + k][:], small[1 + k][:], attn[:, 4 + k:5 + k], 0.0, ALU.add, ALU.max))
                c.link(dve.tensor_tensor(gate_arg[:], gate[:], small[1][:], ALU.mult))
                c.link(dve.tensor_tensor(gate_arg[:], gate_arg[:], small[2][:], ALU.add))
                dve.sem_inc(gates_in, 1)
                dve.wait_ge(roots, 1)
                c.mark(dve.reciprocal(dinv[:], degree_root[:]))
                c.link(dve.reciprocal(bn_scale[:], bn_root[:]))
                c.link(dve.tensor_tensor(bn_scale[:], bn_scale[:], norm1[:, 0, :], ALU.mult))
                c.link(dve.tensor_tensor(bn_shift[:], bn_scale[:], norm1[:, 2, :], ALU.mult))
                c.link(dve.tensor_tensor(bn_shift[:], norm1[:, 1, :], bn_shift[:], ALU.subtract))
                dve.wait_ge(gates, 1)

                def add_gated(t, slot, rnd):
                    tile_x = x[:, bass.ds(t, 1), :].rearrange("p a f -> p (a f)")
                    dve.scalar_tensor_tensor(out=tile_x, in0=h[:, bass.ds(t, 1), :].rearrange("p a f -> p (a f)"),
                                             scalar=gate_out[:, bass.ds(t, 1)], in1=tile_x,
                                             op0=ALU.mult, op1=ALU.add).then_inc(gated, 1)

                def batch_norm(slot):
                    for k in range(CHUNKS):
                        ins = dve.tensor_scalar(ht_ring[:, slot, k, :], bank[slot][:, k * P:(k + 1) * P],
                                                bn_scale[:, k:k + 1], bn_shift[:, k:k + 1], ALU.mult, ALU.add)
                    return ins

                def scale(t, slot, rnd):
                    dve.tensor_scalar(h[:, bass.ds(t, 1), :].rearrange("p a f -> p (a f)"), bank[2 + slot][:, 0:FEAT],
                                      dinv[:, bass.ds(t, 1)], None, ALU.mult).then_inc(s1.out_free, 1)
                norm_tiles(dve, s1, [(add_gated, (gated, 0))], batch_norm, scale)

        RING = 8

        early_sems = clear_sems()

        class Gather:

            def __init__(self, name):
                self.index_ready = sem(f"index_ready_{name}")
                self.rows_in = [sem(f"g_rows_in_{name}{u}", kept=True) for u in range(RING)]
                self.rows_used = sem(f"g_rows_used_{name}")

        def gather_rows(pool, g, table, cols, begin=True, go_on=True):
            def stage_indices(t, slot):
                pool.tensor_copy(idx_ring[:, slot, :], src_idx[:, bass.ds(t * RING, RING)]).then_inc(g.index_ready, 1)

            def one_round(t, slot, rnd):
                hold(pool, "pool", g.index_ready, t + 1)
                for u in range(RING):
                    if not (isinstance(t, int) and t == 0):
                        hold(pool, "pool", g.rows_used, t * RING + (u + 1))
                    if u == RING - 1 and not (isinstance(t, int) and t == ITEMS // RING - 1):
                        stage_indices(t + 1, 1 - slot)
                    pool.indirect_dma_start(g_ring[:, u, 0:cols], None, table,
                                            bass.IndirectOffsetOnAxis(ap=idx_ring[:, slot, u:u + 1], axis=0)
                                            ).then_inc(g.rows_in[u], 16)
            if begin:
                stage_indices(0, 0)
                one_round(0, 0, 0)
            if go_on:
                rounds = ITEMS // RING
                tile_loop(pool, rounds - 2, 2, one_round, first=1)
                one_round(rounds - 1, (rounds - 1) % 2, (rounds - 1) // 2)

        g1 = Gather("l1")
        ACC_BANKS = 4
        attrs_landed = [sem(f"attrs_landed{u}") for u in range(2)]
        onehot1 = sem("onehot1")
        acc_done1 = sem("acc_done1")

        def onehots(dve, t, u, used, ready, base):
            if not (isinstance(t, int) and t < 8):
                dve.wait_ge(used, t + (base - 7))
            dve.tensor_scalar(onehot[:, u, :], iota_b[:], dst_col[:, bass.ds(t, 1)], None, ALU.is_equal
                              ).then_inc(ready, 1)

        def item_tiles(eng, t0, n, table=None, top=NODE_TILES - 1):
            _, tiles = nc.values_load_multi_w_load_instructions((table or item_tile)[0:1, bass.ds(t0, n)], engines=(eng.engine,),
                                                                min_val=0, max_val=top,
                                                                skip_runtime_bounds_check_because="they count tiles passed")
            return tiles

        AHEAD = 4

        ROUNDS = ITEMS // RING

        def all_rounds(eng, one):
            one(0, None, None)
            with eng.Fori(1, ROUNDS - 1) as i:
                one(i, None, None)
            one(ROUNDS - 1, None, None)

        def accumulate(dve, cols, used, ready, done, extra=None, base=0, rounds=all_rounds, beside=None):
            dve.memset(acc[:], 0.0).then_inc(done, 1)
            for t in range(AHEAD):
                if ready is not None:
                    onehots(dve, t, t, used, ready, base)
                if extra is not None:
                    extra(t, t, 0)

            def one(rnd, begun, ended):
                t0 = rnd * RING
                tiles = item_tiles(dve, t0, RING)
                for u in range(RING):
                    t = t0 + u
                    if not (isinstance(t, int) and t + AHEAD >= ITEMS):
                        if extra is not None:
                            extra(t + AHEAD, (u + AHEAD) % RING, rnd + (u + AHEAD) // RING)
                        if ready is not None:
                            onehots(dve, t + AHEAD, (u + AHEAD) % RING, used, ready, base)
                    into = acc[:, bass.ds(tiles[u], 1), 0:cols].rearrange("p a f -> p (a f)")
                    dve.wait_ge(used, t + (base + 1))
                    dve.wait_ge(done, t + 1)
                    dve.tensor_tensor(into, into, bank[u % ACC_BANKS][:, 0:cols], ALU.add).then_inc(done, 1)
                    if beside is not None:
                        beside(u, begun, ended)
            rounds(dve, one)

        with nc.Block() as block:
            @block.gpsimd
            def _(pool):
                gather_rows(pool, g1, gcn_table, FEAT)

            @block.sync
            def _(sp):
                def load(t, slot, rnd):
                    sp.wait_ge(g1.rows_used, t * CHUNK + CHUNK)
                    sp.dma_start(g_ring[:, slot * CHUNK:(slot + 1) * CHUNK, FEAT:GCN_COLS],
                                 edge_attr_d[bass.ds(t * CHUNK_EDGES, CHUNK_EDGES), :].rearrange("(u e) f -> e u f", e=P)
                                 ).then_inc(attrs_landed[slot], 16)
                tile_loop(sp, EDGE_CHUNKS, 2, load)

            @block.tensor
            def _(pe):
                pe.sem_inc(g1.rows_used, RING)

                def sums(t, u, rnd):
                    if u % CHUNK == 0:
                        pe.wait_ge(attrs_landed[u // CHUNK], rnd * 16 + 16)
                    pe.wait_ge(onehot1, t + 1)
                    pe.wait_ge(g1.rows_in[u], rnd * 16 + 16)
                    if not (isinstance(t, int) and t < ACC_BANKS):
                        pe.wait_ge(acc_done1, t - (ACC_BANKS - 2))
                    pe.matmul(bank[u % ACC_BANKS][:, 0:GCN_COLS], onehot[:, u, :], g_ring[:, u, :], start=True, stop=True
                              ).then_inc(g1.rows_used, 1)
                for u in range(RING):
                    sums(u, u, 0)
                tile_loop(pe, ITEMS - RING, RING, sums, first=RING)

            @block.vector
            def _(dve):
                accumulate(dve, GCN_COLS, g1.rows_used, onehot1, acc_done1, base=RING)

        free_sems(early_sems)

        s2 = Norm(2)
        l2_loads = sem("l2_loads")
        self_added = sem("self_added")
        scaled_in = sem("scaled_in")
        x2_done = sem("x2_done")
        heads_of = sb("heads_of", [P, CHUNKS, 2 * HEADS])
        attn2 = sb("attn2", [P, 2, CHUNKS])
        heads_ready = sem("heads_ready")
        folded = sem("folded")
        fold_read = sem("fold_read")
        row_b = sb("row_b", [P, FEAT])
        rows_out = [sem(f"rows_out{u}") for u in range(2)]
        logit_table = dram("logit_table", [NODE_TILES * P, 2 * HEADS])
        loop_attr = sb("loop_attr", [P, NODE_TILES, EDGE_DIM])
        wt = [work[2][:, 0:CHUNKS * FEAT].rearrange("p (c k) -> p c k", c=CHUNKS),
              work[3][:, 0:CHUNKS * FEAT].rearrange("p (c k) -> p c k", c=CHUNKS)]

        with nc.Block() as block:
            @block.sync
            def _(sp):
                for dst, name in ((wbuf[:, :, 0:FEAT], "l2_w"), (wt[0], "l2_wt"), (attn2[:], "l2_attn")):
                    sp.dma_start(dst, io[name]).then_inc(l2_loads, 16)
                sp.dma_start(row_b[:], io["l1_bias"].broadcast_to([P, FEAT])).then_inc(l2_loads, 16)

                def store(t, slot, rnd):
                    sp.wait_ge(s2.out_free, t + 3)
                    sp.dma_start(l2_table[bass.ds(t * P, P), :], row_ring[:, slot, :]).then_inc(rows_out[slot], 16)
                    sp.dma_start(logit_table[bass.ds(t * P, P), :], row_ring[:, slot, FEAT:L2_COLS]).then_inc(rows_out[slot], 16)
                tile_loop(sp, NODE_TILES, 2, store)
                sp.wait_ge(rows_out[0], 32 * ((NODE_TILES + 1) // 2))
                sp.wait_ge(rows_out[1], 32 * (NODE_TILES // 2))

            @block.gpsimd
            def _(pool):
                def add_self(t, slot, rnd):
                    rows = acc[:, bass.ds(t, 1), 0:FEAT].rearrange("p a f -> p (a f)")
                    pool.tensor_tensor(rows, rows, h[:, bass.ds(t, 1), :].rearrange("p a f -> p (a f)"), ALU.add
                                       ).then_inc(self_added, 1)
                tile_loop(pool, NODE_TILES, 5, add_self)

            @block.scalar
            def _(act):
                def keep(t, slot, rnd):
                    if t >= 2:
                        act.wait_ge(rows_out[slot], rnd * 32)
                    act.copy(row_ring[:, slot, :], bank[2 + slot][:, 0:L2_COLS]).then_inc(s2.out_free, 1)
                turned_copy = to_columns(act, s2, lambda slot: act.copy(flat(ht_ring[:, slot, :, :]), bank[slot][:, 0:FEAT]))
                norm_rows(act, s2, later=[(LAG_SCALE + 1, turned_copy), (LAG_SCALE + 2, from_products(act, s2, keep))])

            @block.tensor
            def _(pe):
                pe.wait_ge(heads_ready, 1)
                pe.wait_ge(l2_loads, 64)
                for k in range(CHUNKS):
                    for f in range(CHUNKS):
                        ins = pe.matmul(bank[6][:, k * 8:k * 8 + 2 * HEADS], wt[0][:, f, k * P:(k + 1) * P],
                                        heads_of[:, f, :], start=(f == 0), stop=(f == CHUNKS - 1))
                ins.then_inc(folded, 1)
                pe.wait_ge(fold_read, 1)
                project(pe, s2, [(0, 0, L2_COLS)])

            @block.vector
            def _(dve):
                c = Chain(dve, "stage8_dve")
                c.link(dve.memset(heads_of[:], 0.0))
                dve.wait_ge(l2_loads, 64)
                half = P // 2
                for side in range(2):
                    for f in range(CHUNKS):
                        for n in range(2):
                            c.mark(dve.tensor_copy(heads_of[n * half:(n + 1) * half, f, side * HEADS + 2 * f + n:side * HEADS + 2 * f + n + 1],
                                                   attn2[n * half:(n + 1) * half, side, f:f + 1]))
                dve.wait_ge(c.sem, c.n)
                dve.sem_inc(heads_ready, 1)
                dve.wait_ge(folded, 1)
                dve.tensor_copy(wbuf[:, :, FEAT:L2_COLS], bank[6][:, 0:16].rearrange("p (k n) -> p k n", k=CHUNKS)).then_inc(fold_read, 1)
                c.link(dve.tensor_scalar(small[0][:], degree1[:], -1.0, 1.0, ALU.add, ALU.max))
                c.link(dve.reciprocal(small[0][:], small[0][:]))
                c.link(dve.tensor_tensor(loop_attr[:], acc[:, :, FEAT:GCN_COLS],
                                         small[0][:].unsqueeze(2).broadcast_to([P, NODE_TILES, EDGE_DIM]), ALU.mult))

                def scale(t, slot, rnd):
                    rows = acc[:, bass.ds(t, 1), 0:FEAT].rearrange("p a f -> p (a f)")
                    dve.wait_ge(self_added, t + 1)
                    dve.scalar_tensor_tensor(out=rows, in0=rows, scalar=dinv[:, bass.ds(t, 1)], in1=row_b[:],
                                             op0=ALU.mult, op1=ALU.add).then_inc(scaled_in, 1)

                def add(t, slot, rnd):
                    rows = acc[:, bass.ds(t, 1), 0:FEAT].rearrange("p a f -> p (a f)")
                    tile_x = x[:, bass.ds(t, 1), :].rearrange("p a f -> p (a f)")
                    dve.wait_ge(scaled_in, t + 1)
                    dve.scalar_tensor_tensor(out=tile_x, in0=rows, scalar=0.0, in1=tile_x,
                                             op0=ALU.max, op1=ALU.add).then_inc(x2_done, 1)

                norm_tiles(dve, s2, [(scale, (scaled_in, 0)), (add, (x2_done, 0))], None, None)

        middle_sems = clear_sems()
        idx2_in = sem("idx2_in")
        idx2 = sb("idx2", [P, 2, NODE_TILES], I32)
        side_logits = sb("side_logits", [P, NODE_TILES, 2 * HEADS])
        GROUPS2 = 5
        G2 = NODE_TILES // GROUPS2
        sides_in = [sem(f"sides_in{k}", kept=True) for k in range(GROUPS2)]
        rows2_in = [sem(f"rows2_in{k}", kept=True) for k in range(GROUPS2)]
        alpha = sb("alpha", [P, NODE_TILES, HEADS])
        less2 = sem("less2")
        exp2 = sem("exp2")
        l3_loads = sem("l3_loads")
        we_ext = sb("we_ext", [EDGE_DIM, L3_COLS])
        attt = sb("attt", [P, CHUNKS])
        bt = sb("bt", [P, 2, CHUNKS])
        bias3 = sb("bias3", [1, 2 * L3_COLS])
        heads3_ready = sem("heads3_ready")
        folded3 = sem("folded3")
        fold3_read = sem("fold3_read")
        bias_spread = sem("bias_spread")
        fold_memory = item_vals[:, 1, :]
        wt3 = [fold_memory[:, k * CHUNKS * FEAT:(k + 1) * CHUNKS * FEAT].rearrange("p (c k) -> p c k", c=CHUNKS) for k in range(2)]
        wet = fold_memory[:, 1024:1024 + CHUNKS * EDGE_DIM].rearrange("p (c k) -> p c k", c=CHUNKS)
        bias_rows = fold_memory[:, 1088:1088 + 2 * L3_COLS].rearrange("p (n f) -> p n f", n=2)
        mean_head = flat(g_ring[:])[:, 0:G2 * HEAD_DIM].rearrange("p (t d) -> p t d", t=G2)

        with nc.Block() as block:
            @block.sync
            def _(sp):
                sp.dma_start(idx2[:, 0, :], io["l2_src"]).then_inc(idx2_in, 16)
                sp.dma_start(idx2[:, 1, :], io["l2_dst"]).then_inc(idx2_in, 16)
                for dst, name in ((wbuf[:, :, 0:FEAT], "l3_wl"), (wbuf[:, :, L3_COLS:L3_COLS + FEAT], "l3_wr"),
                                  (wt3[0], "l3_wlt"), (wt3[1], "l3_wrt"), (wet, "l3_wet"), (attt[:], "l3_attt"),
                                  (bt[:], "l3_bt"), (we_ext[:, 0:FEAT], "l3_we")):
                    sp.dma_start(dst, io[name]).then_inc(l3_loads, 16)
                sp.dma_start(bias3[:, 0:FEAT], io["l3_bias"][:, 0:FEAT]).then_inc(l3_loads, 16)
                sp.dma_start(bias3[:, L3_COLS:L3_COLS + FEAT], io["l3_bias"][:, FEAT:2 * FEAT]).then_inc(l3_loads, 16)
                sp.dma_start(row_b[:], io["l3_att"].broadcast_to([P, FEAT])).then_inc(l3_loads, 16)

            @block.tensor
            def _(pe):
                pe.wait_ge(heads3_ready, 1)
                pe.wait_ge(l3_loads, 16 * 11)
                att_of = heads_of[:, :, 0:HEADS]
                for n in range(2):
                    for k in range(CHUNKS):
                        for f in range(CHUNKS):
                            at = (n * CHUNKS + k) * HEADS
                            pe.matmul(bank[6][:, at:at + HEADS], wt3[n][:, f, k * P:(k + 1) * P], att_of[:, f, :],
                                      start=(f == 0), stop=(f == CHUNKS - 1))
                    for f in range(CHUNKS):
                        pe.matmul(bank[7][0:1, n * HEADS:(n + 1) * HEADS], bt[:, n, f:f + 1], att_of[:, f, :],
                                  start=(f == 0), stop=(f == CHUNKS - 1))
                for f in range(CHUNKS):
                    ins = pe.matmul(bank[7][0:EDGE_DIM, 16:16 + HEADS], wet[:, f, :], att_of[:, f, :],
                                    start=(f == 0), stop=(f == CHUNKS - 1))
                ins.then_inc(folded3, 1)
                pe.wait_ge(fold3_read, 1)
                for n in range(2):
                    ins = pe.matmul(bank[4 + n][:, 0:L3_COLS], ones[0:1, :], bias3[0:1, n * L3_COLS:(n + 1) * L3_COLS],
                                    start=True, stop=True)
                ins.then_inc(bias_spread, 1)

            @block.gpsimd
            def _(pool):
                pool.wait_ge(idx2_in, 32)
                for k in range(GROUPS2):
                    for t in range(k * G2, (k + 1) * G2):
                        pool.indirect_dma_start(side_logits[:, t, :], None, logit_table,
                                                bass.IndirectOffsetOnAxis(ap=idx2[:, 0, t:t + 1], axis=0)).then_inc(sides_in[k], 16)
                    for t in range(k * G2, (k + 1) * G2):
                        pool.indirect_dma_start(acc[:, t, 0:L2_COLS], None, l2_table,
                                                bass.IndirectOffsetOnAxis(ap=idx2[:, 1, t:t + 1], axis=0)).then_inc(rows2_in[k], 16)

            @block.scalar
            def _(act):
                for k in range(GROUPS2):
                    ts = slice(k * G2, (k + 1) * G2)
                    act.wait_ge(less2, k + 1)
                    act.activation(alpha[:, ts, :], alpha[:, ts, :], ACT.Exp).then_inc(exp2, 1)

            @block.vector
            def _(dve):
                c = Chain(dve, "stage9_dve")
                c.link(dve.memset(heads_of[:], 0.0))
                dve.wait_ge(l3_loads, 16 * 11)
                half = P // 2
                for f in range(CHUNKS):
                    for n in range(2):
                        c.mark(dve.tensor_copy(heads_of[n * half:(n + 1) * half, f, 2 * f + n:2 * f + n + 1],
                                               attt[n * half:(n + 1) * half, f:f + 1]))
                dve.wait_ge(c.sem, c.n)
                dve.sem_inc(heads3_ready, 1)
                c.mark(dve.tensor_scalar(row_b[:], row_b[:], 1.0 - NEG_GAT, None, ALU.mult))
                dve.wait_ge(folded3, 1)
                for n in range(2):
                    at = n * CHUNKS * HEADS
                    c.mark(dve.tensor_scalar(wbuf[:, :, n * L3_COLS + FEAT:(n + 1) * L3_COLS],
                                             bank[6][:, at:at + CHUNKS * HEADS].rearrange("p (k n) -> p k n", k=CHUNKS),
                                             NEG_GAT, None, ALU.mult))
                    c.mark(dve.tensor_scalar(bias3[:, n * L3_COLS + FEAT:(n + 1) * L3_COLS],
                                             bank[7][0:1, n * HEADS:(n + 1) * HEADS], NEG_GAT, None, ALU.mult))
                c.link(dve.tensor_scalar(we_ext[:, FEAT:L3_COLS], bank[7][0:EDGE_DIM, 16:16 + HEADS], NEG_GAT, None, ALU.mult))
                dve.sem_inc(fold3_read, 1)
                dve.wait_ge(bias_spread, 1)
                for n in range(2):
                    c.mark(dve.tensor_copy(bias_rows[:, n, :], bank[4 + n][:, 0:L3_COLS]))
                for k in range(GROUPS2):
                    ts = slice(k * G2, (k + 1) * G2)
                    weights = alpha[:, ts, :]
                    by_head = [P, G2, HEADS]
                    dve.wait_ge(sides_in[k], 16 * G2)
                    dve.wait_ge(rows2_in[k], 16 * G2)
                    c.link(dve.tensor_tensor(weights, side_logits[:, ts, 0:HEADS], acc[:, ts, FEAT + HEADS:L2_COLS], ALU.add))
                    c.link(dve.scalar_tensor_tensor(out=weights, in0=weights, scalar=NEG_L2, in1=weights, op0=ALU.mult, op1=ALU.max))
                    c.link(dve.tensor_reduce(small[0][:, ts], weights, X_AXIS, ALU.max))
                    dve.tensor_tensor(weights, weights, small[0][:, ts].unsqueeze(2).broadcast_to(by_head), ALU.subtract
                                      ).then_inc(less2, 1)
                    dve.wait_ge(exp2, k + 1)
                    c.link(dve.tensor_reduce(small[1][:, ts], weights, X_AXIS, ALU.add))
                    c.link(dve.reciprocal(small[1][:, ts], small[1][:, ts]))
                    c.link(dve.tensor_tensor(weights, weights, small[1][:, ts].unsqueeze(2).broadcast_to(by_head), ALU.mult))
                    rows = acc[:, ts, 0:FEAT].rearrange("p t (h d) -> p t h d", h=HEADS)
                    all_heads = [P, G2, HEADS, HEAD_DIM]
                    c.link(dve.tensor_tensor(rows, rows, weights.unsqueeze(3).broadcast_to(all_heads), ALU.mult))
                    c.link(dve.tensor_reduce(mean_head, acc[:, ts, 0:FEAT].rearrange("p t (h d) -> p t d h", h=HEADS), X_AXIS, ALU.add))
                    tile_x = x[:, ts, :].rearrange("p t (h d) -> p t h d", h=HEADS)
                    c.link(dve.tensor_tensor(tile_x, tile_x, mean_head.unsqueeze(2).broadcast_to(all_heads), ALU.add))

        s3 = Norm(3)
        xl_linear = sb("xl_linear", [P, NODE_TILES, HEADS])
        right_ring, rest_ring, last_ring = [
            item_vals[:, 0, k * 2 * L3_COLS:(k + 1) * 2 * L3_COLS].rearrange("p (s f) -> p s f", s=2) for k in range(3)]
        right_ready = sem("right_ready")
        left_ready = sem("left_ready")
        parts_made = [sem(f"parts_made{k}") for k in range(3)]
        rest_ready = sem("rest_ready")
        last_ready = sem("last_ready")
        l3_stored = sem("l3_stored")

        with nc.Block() as block:
            @block.sync
            def _(sp):
                def store(t, slot, rnd):
                    sp.wait_ge(s3.out_free, t + 3)
                    sp.dma_start(l3_table[bass.ds(t * P, P), 0:FEAT],
                                 h[:, bass.ds(t, 1), :].rearrange("p a f -> p (a f)")).then_inc(l3_stored, 16)
                    sp.dma_start(l3_table[bass.ds(t * P, P), FEAT:L3_COLS],
                                 xl_linear[:, bass.ds(t, 1), :].rearrange("p a f -> p (a f)")).then_inc(l3_stored, 16)
                tile_loop(sp, NODE_TILES, 5, store)
                sp.wait_ge(l3_stored, 32 * NODE_TILES)

            @block.scalar
            def _(act):
                def part(k):
                    def copy(t, slot, rnd):
                        act.wait_ge((right_ready, rest_ready, last_ready)[k], t + 1)
                        act.copy(xr_parts[:, t, k, :], (right_ring, rest_ring, last_ring)[k][:, slot, :]).then_inc(parts_made[k], 1)
                    return copy
                norm_rows(act, s3, later=[(LAG_OUT + k, part(k)) for k in range(3)])

            @block.tensor
            def _(pe):
                project(pe, s3, [(0, 0, L3_COLS), (1, L3_COLS, 2 * L3_COLS)])

            @block.gpsimd
            def _(pool):
                def less(t, slot, rnd):
                    pool.wait_ge(parts_made[1], t + 1)
                    if t >= 2:
                        pool.wait_ge(parts_made[2], t - 1)
                    pool.tensor_tensor(last_ring[:, slot, :], rest_ring[:, slot, :], xr_parts[:, t, 1, :], ALU.subtract
                                       ).then_inc(last_ready, 1)
                pipelined(pool, [(0, less)])

            @block.vector
            def _(dve):
                def add_bias(t, slot, rnd):
                    left, right = bank[2 + slot * 2], bank[3 + slot * 2]
                    if t >= 2:
                        dve.wait_ge(rest_ready, t - 1)
                    dve.tensor_tensor(right_ring[:, slot, :], right[:, 0:L3_COLS], bias_rows[:, 1, :], ALU.add).then_inc(right_ready, 1)
                    dve.tensor_tensor(h[:, t, :], left[:, 0:FEAT], bias_rows[:, 0, 0:FEAT], ALU.add).then_inc(left_ready, 1)
                    dve.wait_ge(right_ready, t + 1)
                    dve.wait_ge(left_ready, t + 1)
                    dve.tensor_tensor(xl_linear[:, t, :], left[:, FEAT:L3_COLS], bias_rows[:, 0, FEAT:L3_COLS], ALU.add
                                      ).then_inc(s3.out_free, 1)

                def less(t, slot, rnd):
                    dve.wait_ge(parts_made[0], t + 1)
                    if t >= 2:
                        dve.wait_ge(last_ready, t - 1)
                    dve.tensor_tensor(rest_ring[:, slot, :], right_ring[:, slot, :], xr_parts[:, t, 0, :], ALU.subtract
                                      ).then_inc(rest_ready, 1)
                norm_tiles(dve, s3, [], plain_cols(dve), add_bias, later=[(LAG_OUT + 1, less)])

        free_sems(middle_sems)

        own_logits = sb("own_logits", [P, NODE_TILES, HEADS])
        we_parts = sb("we_parts", [P, L3_COLS], BF16)
        we_part = flat(acc[:])[0:EDGE_DIM, 0:3 * L3_COLS // 2].bitcast(BF16).rearrange("p (k f) -> p k f", k=3)
        we_rest = flat(acc[:])[0:EDGE_DIM, 512:512 + 2 * L3_COLS].rearrange("p (k f) -> p k f", k=2)
        we_split = sem("we_split")
        we_placed = sem("we_placed")

        def add_terms(pe, into, places, tile, attrs, weights):
            for k in range(3):
                pe.matmul(into, places, xr_parts[:, bass.ds(tile, 1), k, :].rearrange("p a f -> p (a f)"),
                          start=(k == 0), stop=False)
            return pe.matmul(into, attrs, weights, start=False, stop=True)

        g3 = Gather("l3a")
        sum_ring = flat(sums_rhs[:])[:, 0:RING * L3_COLS].rearrange("p (u f) -> p u f", u=RING)
        relu_ring = flat(sums_rhs[:])[:, RING * L3_COLS:RING * L3_COLS + 4 * FEAT].rearrange("p (u f) -> p u f", u=4)
        attrs_turned = item_vals[:, 1, 0:RING * P // 2].bitcast(BF16).rearrange("p (u e) -> p u e", u=RING)
        pair_rows = attr_parts_d.rearrange("b p c -> (b p c)").rearrange("(k g e) -> k g e", g=EDGE_TILES, e=P)
        edge_tile = item_vals[0:1, 1, 1024:1024 + ITEMS].bitcast(I32)
        edge_tile_in = sem("edge_tile_in")
        nonlinear = sb("nonlinear", [P, RING, HEADS])
        rows_ring = sb("rows_ring", [P, 2, CHUNK_EDGES], BF16)
        rows3_in = [sem(f"rows3_in{u}") for u in range(2)]
        attrs3_in = [sem(f"attrs3_in{u}") for u in range(RING)]
        places3 = sem("places3")
        terms3 = sem("terms3")
        relued3 = sem("relued3")
        dotted3 = sem("dotted3")
        logits3 = sem("logits3")
        LAG = 2

        def item_rounds(eng, step, prepare=None):
            def one(t0, rnd):
                extra = (prepare(t0),) if prepare else ()
                for u in range(RING):
                    step(t0 + u, u, rnd, *extra)
            one(0, 0)
            with eng.Fori(1, ITEMS // RING - 1) as i:
                one(i * RING, i)
            one(ITEMS - RING, ITEMS // RING - 1)

        def at_least(t, n):
            return not isinstance(t, int) or t >= n

        def known_after(t, n):
            return not isinstance(t, int) or t + n < ITEMS

        with nc.Block() as block:
            @block.gpsimd
            def _(pool):
                gather_rows(pool, g3, l3_table, L3_COLS)

            @block.sync
            def _(sp):
                sp.dma_start(edge_tile, edge_tile_d.unsqueeze(0)).then_inc(edge_tile_in, 16)
                sp.wait_ge(edge_tile_in, 16)

                def load(t, u, rnd, tiles):
                    slot = u // CHUNK
                    if u % CHUNK == 0:
                        if at_least(t, RING):
                            sp.wait_ge(places3, rnd * 2 + (slot - 1))
                        sp.dma_start(rows_ring[:, slot, :],
                                     dst_rows_d[bass.ds(t * P, CHUNK_EDGES)].unsqueeze(0).broadcast_to([P, CHUNK_EDGES])
                                     ).then_inc(rows3_in[slot], 16)
                    if at_least(t, RING):
                        sp.wait_ge(terms3, t - (RING - 1))
                    sp.dma_start(attrs_turned[:, u, :], pair_rows[:, bass.ds(tiles[u], 1), :].rearrange("k a e -> k (a e)")
                                 ).then_inc(attrs3_in[u], 16)
                sp.wait_ge(we_split, 1)
                for b in range(PAIRS):
                    sp.dma_start(we_parts[b * EDGE_DIM:(b + 1) * EDGE_DIM, :], we_part[:, b % 3, :]).then_inc(we_placed, 16)
                item_rounds(sp, load, lambda t0: item_tiles(sp, t0, RING, edge_tile, EDGE_TILES - 1))

            @block.tensor
            def _(pe):
                def item(t, u, rnd, tiles):
                    slot = u // CHUNK
                    if u % CHUNK == 0:
                        pe.wait_ge(places3, rnd * 2 + (slot + 1))
                    pe.wait_ge(attrs3_in[u], rnd * 16 + 16)
                    if at_least(t, ACC_BANKS):
                        pe.wait_ge(g3.rows_used, t + (RING + 1 - ACC_BANKS))
                    add_terms(pe, bank[u % ACC_BANKS][:, 0:L3_COLS], place_ring[:, slot, 0, u % CHUNK * P:(u % CHUNK + 1) * P],
                              tiles[u], attrs_turned[:, u, :], we_parts[:]).then_inc(terms3, 1)
                pe.wait_ge(we_placed, 16 * PAIRS)
                item_rounds(pe, item, lambda t0: item_tiles(pe, t0, RING))

            @block.scalar
            def _(act):
                def item(t, u, rnd):
                    act.wait_ge(g3.rows_used, t + (RING + 1))
                    if at_least(t, 4):
                        act.wait_ge(dotted3, t - 3)
                    act.activation(relu_ring[:, u % 4, :], sum_ring[:, u, 0:FEAT], ACT.Relu).then_inc(relued3, 1)
                item_rounds(act, item)

            @block.vector
            def _(dve):
                c = Chain(dve, "stage12_dve")
                dve.sem_inc(g3.rows_used, RING)
                c.link(dve.tensor_copy(we_part[:, 0, :], we_ext[:]))
                c.link(dve.tensor_tensor(we_rest[:, 0, :], we_ext[:], we_part[:, 0, :], ALU.subtract))
                c.link(dve.tensor_copy(we_part[:, 1, :], we_rest[:, 0, :]))
                c.link(dve.tensor_tensor(we_rest[:, 1, :], we_rest[:, 0, :], we_part[:, 1, :], ALU.subtract))
                c.link(dve.tensor_copy(we_part[:, 2, :], we_rest[:, 1, :]))
                dve.sem_inc(we_split, 1)

                def places(chunk, slot, rnd):
                    dve.wait_ge(rows3_in[slot], rnd * 16 + 16)
                    if at_least(chunk, 2):
                        dve.wait_ge(terms3, chunk * CHUNK - CHUNK)
                    dve.tensor_scalar(place_ring[:, slot, 0, :], rows_ring[:, slot, :], p_index[:], None, ALU.is_equal
                                      ).then_inc(places3, 1)

                def dot(t, u):
                    dve.wait_ge(relued3, t + 1)
                    for hd in range(HEADS):
                        d = slice(hd * HEAD_DIM, (hd + 1) * HEAD_DIM)
                        ins = dve.tensor_tensor_reduce(out=relu_ring[:, u % 4, d], in0=relu_ring[:, u % 4, d], in1=row_b[:, d],
                                                       scale=1.0, scalar=0.0, op0=ALU.mult, op1=ALU.add,
                                                       accum_out=nonlinear[:, u, hd:hd + 1])
                    ins.then_inc(dotted3, 1)

                def finish(t0, slot):
                    dve.wait_ge(dotted3, t0 + CHUNK)
                    us = slice(slot * CHUNK, (slot + 1) * CHUNK)
                    dve.tensor_tensor(logits[:, bass.ds(t0, CHUNK), :], nonlinear[:, us, :], sum_ring[:, us, FEAT:L3_COLS], ALU.add
                                      ).then_inc(logits3, 1)

                def item(t, u, rnd):
                    slot = u // CHUNK
                    if u % CHUNK == 0 and known_after(t, CHUNK):
                        places(rnd * 2 + (slot + 1), 1 - slot, rnd + slot)
                    dve.wait_ge(g3.rows_in[u], rnd * 16 + 16)
                    dve.wait_ge(terms3, t + 1)
                    if at_least(t, RING):
                        dve.wait_ge(relued3, t - (RING - 1))
                        if u % CHUNK == 0:
                            dve.wait_ge(logits3, rnd * 2 + (slot - 1))
                    dve.tensor_tensor(sum_ring[:, u, :], g_ring[:, u, 0:L3_COLS], bank[u % ACC_BANKS][:, 0:L3_COLS], ALU.add
                                      ).then_inc(g3.rows_used, 1)
                    if at_least(t, LAG):
                        dot(t - LAG, (u - LAG) % RING)
                        if u % CHUNK == CHUNK - 1 and at_least(t, CHUNK):
                            finish(t - (2 * CHUNK - 1), 1 - slot)
                places(0, 0, 0)
                item_rounds(dve, item)
                for t in range(ITEMS - LAG, ITEMS):
                    dot(t, t % RING)
                finish(ITEMS - CHUNK, 1)

        seg3 = Segments("l3")
        g4 = Gather("l3b")
        masked3 = sem("masked3")
        less3 = sem("less3")
        exp3 = sem("exp3")

        with nc.Block() as block:
            @block.gpsimd
            def _(pool):
                gather_rows(pool, g4, l3_table, L3_COLS, go_on=False)

            @block.tensor
            def _(pe):
                segment_max_pe(pe, seg3, logits, HEADS, masked3)

            @block.scalar
            def _(act):
                act.wait_ge(less3, 1)
                act.activation(sums_rhs[:, :, 0:HEADS], logits, ACT.Exp).then_inc(exp3, 1)
                act.wait_ge(exp3, 1)

            @block.vector
            def _(dve):
                c = Chain(dve, "stage13_dve")
                by_head = [P, ITEMS, HEADS]
                c.link(dve.tensor_tensor(logits, logits, off_col[:].unsqueeze(2).broadcast_to(by_head), ALU.add))
                dve.sem_inc(masked3, 1)
                segment_max_dve(dve, c, seg3, maxima, HEADS)
                dve.tensor_tensor(logits, logits, maxima, ALU.subtract).then_inc(less3, 1)
                c.mark(dve.tensor_tensor(sums_rhs[:, :, HEADS:2 * HEADS], maxima, last_col[:].unsqueeze(2).broadcast_to(by_head), ALU.mult))

        weighted = flat(item_vals[:])[:, 0:RING * OUT_COLS].rearrange("p (u f) -> p u f", u=RING)
        onehot4 = sem("onehot4")
        summed4 = sem("summed4")
        acc_done4 = sem("acc_done4")
        beside4 = sem("beside4")
        own_memory = flat(item_vals[:])[:, RING * OUT_COLS:]
        own = own_memory[:, 0:L3_COLS]
        own_relu = own_memory[:, 264:264 + HEADS]
        attr_row = own_memory[:, 272:272 + EDGE_DIM]
        attr_turned = own_memory[0:EDGE_DIM, 288:288 + P]
        ident_b = sb("ident_b", [P, P], BF16)
        far = own_memory[:, 416:416 + 2 * P].rearrange("p (s n) -> p s n", s=2)
        far_ready = sem("far_ready")
        ident_ready = sem("ident_ready")
        attr_ready = sem("attr_ready")
        attr_flipped = sem("attr_flipped")
        attr_stored = sem("attr_stored")
        own_products = sem("own_products")
        own_added = sem("own_added")
        own_relued = sem("own_relued")
        own_dotted = sem("own_dotted")

        def rounds_with_tiles(eng, one):
            one(0, None, None)
            one(1, 0, None)
            with eng.Fori(2, NODE_TILES + 1) as i:
                one(i, i - 1, i - 2)
            one(NODE_TILES + 1, None, NODE_TILES - 1)
            with eng.Fori(NODE_TILES + 2, ROUNDS - 1) as i:
                one(i, None, None)
            one(ROUNDS - 1, None, None)

        with nc.Block() as block:
            @block.gpsimd
            def _(pool):
                gather_rows(pool, g4, l3_table, L3_COLS, begin=False)

            @block.scalar
            def _(act):
                def beside(t, slot):
                    if at_least(t, 2):
                        hold(act, "act", summed4, t * CHUNK - CHUNK)
                    act.copy(weighted[:, slot * CHUNK:(slot + 1) * CHUNK, FEAT:OUT_COLS],
                             sums_rhs[:, bass.ds(t * CHUNK, CHUNK), :]).then_inc(beside4, 1)

                def square(t, u):
                    if at_least(t, 2):
                        hold(act, "act", onehot4, t - 1)
                    act.activation(far[:, u % 2, :], iota_b[:], ACT.Square, bias=dst_col[:, bass.ds(t, 1)], scale=-1.0
                                   ).then_inc(far_ready, 1)

                def finish(t, u):
                    if at_least(t, RING):
                        act.wait_ge(summed4, t - (RING - 1))
                    act.wait_ge(far_ready, t + 1)
                    act.activation(onehot[:, u, :], far[:, u % 2, :], ACT.Relu, bias=ones[:, 0:1], scale=-1.0
                                   ).then_inc(onehot4, 1)

                def onehots_of(rnd, us):
                    for u in us:
                        t = rnd * RING + u
                        if known_after(t, 1):
                            square(t + 1, u + 1)
                        finish(t, u)
                square(0, 0)

                def one(rnd, begun, ended):
                    beside(rnd * 2, 0)
                    onehots_of(rnd, range(0, CHUNK))
                    if ended is not None:
                        act.wait_ge(own_added, ended + 1)
                        act.activation(own[:, 0:FEAT], own[:, 0:FEAT], ACT.Relu).then_inc(own_relued, 1)
                    beside(rnd * 2 + 1, 1)
                    onehots_of(rnd, range(CHUNK, RING))
                rounds_with_tiles(act, one)

            @block.tensor
            def _(pe):
                def one(rnd, begun, ended):
                    for u in range(RING):
                        t = rnd * RING + u
                        if u % CHUNK == 0:
                            pe.wait_ge(beside4, rnd * 2 + (u // CHUNK + 1))
                        pe.wait_ge(onehot4, t + 1)
                        pe.wait_ge(g4.rows_used, t + (RING + 1))
                        if at_least(t, ACC_BANKS):
                            pe.wait_ge(acc_done4, t - (ACC_BANKS - 2))
                        pe.matmul(bank[u % ACC_BANKS][:, 0:OUT_COLS], onehot[:, u, :], weighted[:, u, :], start=True, stop=True
                                  ).then_inc(summed4, 1)
                        if begun is not None and u == 1:
                            pe.wait_ge(attr_ready, begun + 1)
                            pe.transpose(bank[6][0:EDGE_DIM, 0:P], attr_row, ident[:]).then_inc(attr_flipped, 1)
                        if begun is not None and u == 5:
                            pe.wait_ge(attr_stored, begun + 1)
                            add_terms(pe, bank[4][:, 0:L3_COLS], ident_b[:], begun, attr_turned, we_ext[:]).then_inc(own_products, 1)
                pe.wait_ge(ident_ready, 1)
                rounds_with_tiles(pe, one)

            @block.vector
            def _(dve):
                dve.sem_inc(g4.rows_used, RING)
                dve.tensor_copy(ident_b[:], ident[:]).then_inc(ident_ready, 1)

                def weigh(t, u, rnd):
                    dve.wait_ge(g4.rows_in[u], rnd * 16 + 16)
                    if at_least(t, RING):
                        dve.wait_ge(summed4, t - (RING - 1))
                    dve.tensor_tensor(weighted[:, u, 0:FEAT].rearrange("p (h d) -> p h d", h=HEADS),
                                      g_ring[:, u, 0:FEAT].rearrange("p (h d) -> p h d", h=HEADS),
                                      sums_rhs[:, bass.ds(t, 1), 0:HEADS].rearrange("p a h -> p (a h)").unsqueeze(2).broadcast_to([P, HEADS, HEAD_DIM]),
                                      ALU.mult).then_inc(g4.rows_used, 1)

                def own_steps(u, begun, ended):
                    if begun is not None and u == 0:
                        dve.tensor_copy(attr_row, loop_attr[:, bass.ds(begun, 1), :].rearrange("p a k -> p (a k)")
                                        ).then_inc(attr_ready, 1)
                    if ended is not None and u == 2:
                        dve.wait_ge(own_relued, ended + 1)
                        for hd in range(HEADS):
                            d = slice(hd * HEAD_DIM, (hd + 1) * HEAD_DIM)
                            ins = dve.tensor_tensor_reduce(out=own[:, d], in0=own[:, d], in1=row_b[:, d], scale=1.0, scalar=0.0,
                                                           op0=ALU.mult, op1=ALU.add, accum_out=own_relu[:, hd:hd + 1])
                        ins.then_inc(own_dotted, 1)
                    if begun is not None and u == 3:
                        dve.wait_ge(attr_flipped, begun + 1)
                        dve.tensor_copy(attr_turned, bank[6][0:EDGE_DIM, 0:P]).then_inc(attr_stored, 1)
                    if ended is not None and u == 4:
                        dve.wait_ge(own_dotted, ended * 2 + 1)
                        dve.tensor_tensor(own_logits[:, bass.ds(ended, 1), :].rearrange("p a h -> p (a h)"), own_relu,
                                          own[:, FEAT:L3_COLS], ALU.add).then_inc(own_dotted, 1)
                    if begun is not None and u == 6:
                        if ended is not None:
                            dve.wait_ge(own_dotted, ended * 2 + 2)
                        dve.wait_ge(own_products, begun + 1)
                        dve.tensor_tensor(own[:, 0:FEAT], bank[4][:, 0:FEAT],
                                          h[:, bass.ds(begun, 1), :].rearrange("p a f -> p (a f)"), ALU.add)
                        dve.tensor_tensor(own[:, FEAT:L3_COLS], bank[4][:, FEAT:L3_COLS],
                                          xl_linear[:, bass.ds(begun, 1), :].rearrange("p a h -> p (a h)"), ALU.add
                                          ).then_inc(own_added, 1)
                accumulate(dve, OUT_COLS, summed4, None, acc_done4, extra=weigh, rounds=rounds_with_tiles, beside=own_steps)

        final_loads = sem("final_loads")
        shares_in = sem("shares_in")
        shares = sem("shares")
        bias_in = sem("bias_in")
        own_weighed = sem("own_weighed")
        sum_weighed = sem("sum_weighed")
        own_biased = sem("own_biased")
        biased = sem("biased")
        sigmoids = sem("sigmoids")
        silu = sem("silu")
        base = sem("base")
        normed = sem("normed")
        result = sem("result")
        written = sem("written")
        top_all, den, share_0, share_1 = [
            flat(item_vals[:])[:, 2560 + i * 128:2560 + i * 128 + NODE_TILES * HEADS].rearrange("p (t h) -> p t h", h=HEADS)
            for i in range(4)]
        share = [share_0, share_1]
        sig_ring = rings[:, 0:2 * FEAT].rearrange("p (s f) -> p s f", s=2)
        norm_ring = rings[:, 512:512 + 2 * FEAT].rearrange("p (s f) -> p s f", s=2)

        def rows_of(table, t, cols=FEAT):
            return table[:, bass.ds(t, 1), 0:cols].rearrange("p a f -> p (a f)")

        def heads_view(ap):
            return ap.rearrange("p (h d) -> p h d", h=HEADS)

        def head_scale(n, t):
            return share[n][:, t, :].unsqueeze(2).broadcast_to([P, HEADS, HEAD_DIM])

        with nc.Block() as block:
            @block.sync
            def _(sp):
                sp.dma_start(row_b[:], io["l3_bias"][:, 2 * FEAT:3 * FEAT].broadcast_to([P, FEAT])).then_inc(final_loads, 16)

                def write(t, slot, rnd):
                    sp.wait_ge(result, t + 1)
                    sp.dma_start(out[bass.ds(t * P, P), :], rows_of(x, t)).then_inc(written, 16)
                tile_loop(sp, NODE_TILES - 1, 4, write)
                sp.wait_ge(result, NODE_TILES)
                sp.dma_start(out[(NODE_TILES - 1) * P:NODES, :], x[0:LAST_ROWS, NODE_TILES - 1, :]).then_inc(written, 16)
                sp.wait_ge(written, 16 * NODE_TILES)

            @block.gpsimd
            def _(pool):
                def weigh(t, slot, rnd):
                    pool.tensor_tensor(heads_view(h[:, t, :]), heads_view(h[:, t, :]), head_scale(1, t), ALU.mult
                                       ).then_inc(own_weighed, 1)

                def add_bias(t, slot, rnd):
                    pool.wait_ge(own_weighed, t + 1)
                    pool.tensor_tensor(h[:, t, :], h[:, t, :], row_b[:], ALU.add).then_inc(own_biased, 1)
                pool.wait_ge(final_loads, 16)
                pool.wait_ge(shares, 1)
                pipelined(pool, [(0, weigh), (1, add_bias)])

            @block.scalar
            def _(act):
                act.wait_ge(shares_in, 1)
                act.activation(share[0], share[0], ACT.Exp)
                act.activation(share[1], share[1], ACT.Exp).then_inc(shares_in, 1)

                def norm(t, slot, rnd):
                    if t >= 2:
                        act.wait_ge(base, t - 1)
                    act.activation(norm_ring[:, slot, :], x[:, t, :], ACT.Relu, bias=column(shift, t), scale=column(rstd, t)
                                   ).then_inc(normed, 1)

                def sigmoid(t, slot, rnd):
                    if t >= 2:
                        act.wait_ge(result, t - 1)
                    act.wait_ge(biased, t + 1)
                    act.activation(sig_ring[:, slot, :], acc[:, t, 0:FEAT], ACT.Sigmoid).then_inc(sigmoids, 1)
                pipelined(act, [(0, norm), (2, sigmoid)])

            @block.vector
            def _(dve):
                c = Chain(dve, "stage15_dve")
                edges_den = acc[:, :, FEAT:FEAT + HEADS]
                edges_top = acc[:, :, FEAT + HEADS:OUT_COLS]
                c.link(dve.tensor_scalar(den, edges_den, 0.0, -BIG, ALU.is_equal, ALU.mult))
                c.link(dve.tensor_tensor(den, den, edges_top, ALU.add))
                c.link(dve.tensor_tensor(top_all, den, own_logits[:], ALU.max))
                c.mark(dve.tensor_tensor(share[0], den, top_all, ALU.subtract))
                c.link(dve.tensor_tensor(share[1], own_logits[:], top_all, ALU.subtract))
                dve.sem_inc(shares_in, 1)
                dve.wait_ge(shares_in, 2)
                c.link(dve.tensor_tensor(den, edges_den, share[0], ALU.mult))
                c.link(dve.scalar_tensor_tensor(out=den, in0=den, scalar=1e-16, in1=share[1], op0=ALU.add, op1=ALU.add))
                c.link(dve.reciprocal(den, den))
                for n in range(2):
                    c.mark(dve.tensor_tensor(share[n], share[n], den, ALU.mult))
                dve.wait_ge(c.sem, c.n)
                dve.sem_inc(shares, 1)

                def weigh(t, slot, rnd):
                    rows = heads_view(acc[:, t, 0:FEAT])
                    dve.tensor_tensor(rows, rows, head_scale(0, t), ALU.mult).then_inc(sum_weighed, 1)

                def add_own(t, slot, rnd):
                    dve.wait_ge(own_biased, t + 1)
                    dve.wait_ge(sum_weighed, t + 1)
                    dve.tensor_tensor(acc[:, t, 0:FEAT], acc[:, t, 0:FEAT], h[:, t, :], ALU.add).then_inc(biased, 1)

                def add_norm(t, slot, rnd):
                    dve.wait_ge(normed, t + 1)
                    dve.tensor_tensor(x[:, t, :], x[:, t, :], norm_ring[:, slot, :], ALU.add).then_inc(base, 1)

                def times(t, slot, rnd):
                    dve.wait_ge(sigmoids, t + 1)
                    dve.tensor_tensor(sig_ring[:, slot, :], sig_ring[:, slot, :], acc[:, t, 0:FEAT], ALU.mult).then_inc(silu, 1)

                def add_silu(t, slot, rnd):
                    dve.wait_ge(base, t + 1)
                    dve.wait_ge(silu, t + 1)
                    dve.tensor_tensor(x[:, t, :], x[:, t, :], sig_ring[:, slot, :], ALU.add).then_inc(result, 1)
                pipelined(dve, [(0, weigh), (3, add_silu), (1, add_own), (1, add_norm), (2, times)])


def layouts(a):
    import numpy as np
    pad = EDGE_TILES * P - EDGES
    node_pad = NODE_TILES * P
    src = np.concatenate([a["src"], np.zeros(pad, a["src"].dtype)])
    beyond = np.full(pad + 1, node_pad, a["dst"].dtype)
    before = np.full(1, -1, a["dst"].dtype)
    dst = np.concatenate([before, a["dst"], beyond])
    dst_ext = np.stack([dst[g * P:g * P + P + 2] for g in range(EDGE_TILES)])
    attr = np.concatenate([a["edge_attr_16"], np.zeros((pad, EDGE_DIM), a["edge_attr_16"].dtype)])
    gate = np.concatenate([a["node_vec1"][:, 0], np.zeros(node_pad - NODES, a["node_vec1"].dtype)])

    def features_on_partitions(w):
        return np.ascontiguousarray(w.reshape(CHUNKS, P, -1).transpose(1, 0, 2))

    return {
        "x": a["x"],
        "tile_starts": dst[1:-1].reshape(EDGE_TILES, P)[:, 0].reshape(1, EDGE_TILES),
        "dst_ext": dst_ext,
        "src_tiles": src.reshape(EDGE_TILES, P),
        "edge_attr": attr.reshape(EDGE_TILES, P * EDGE_DIM),
        "attr_t": np.ascontiguousarray(attr.T).reshape(P, ATTR_COLS),
        "gate": np.ascontiguousarray(gate.reshape(NODE_TILES, P).T),
        "l2_src": np.ascontiguousarray(a["src"][:node_pad].reshape(NODE_TILES, P).T),
        "l2_dst": np.ascontiguousarray(a["dst"][:node_pad].reshape(NODE_TILES, P).T),
        "l0_w": features_on_partitions(a["L0_gnn_W"]),
        "l0_attn": np.concatenate([a["L0_gnn_attn_l"], a["L0_gnn_attn_r"], a["L0_gnn_bias"]]).reshape(1, 6),
        "l1_w": features_on_partitions(a["L1_gnn_weight"]),
        "l1_bias": a["L1_gnn_bias"].reshape(1, FEAT),
        "l1_norm": np.ascontiguousarray(np.stack([features_on_partitions(a["L1_gnn_" + k])[:, :, 0] for k in (
            "gamma", "beta", "running_mean", "running_var")], axis=1)),
        "l2_w": features_on_partitions(a["L2_gnn_weight"]),
        "l2_wt": features_on_partitions(a["L2_gnn_weight"].T),
        "l2_attn": np.ascontiguousarray(np.stack([a["L2_gnn_attn_l"].reshape(CHUNKS, P).T,
                                                  a["L2_gnn_attn_r"].reshape(CHUNKS, P).T], axis=1)),
        "l3_wl": features_on_partitions(a["L3_gnn_W_l"].T),
        "l3_wlt": features_on_partitions(a["L3_gnn_W_l"]),
        "l3_wr": features_on_partitions(a["L3_gnn_W_r"].T),
        "l3_wrt": features_on_partitions(a["L3_gnn_W_r"]),
        "l3_we": np.ascontiguousarray(a["L3_gnn_W_e"].T),
        "l3_wet": features_on_partitions(a["L3_gnn_W_e"]),
        "l3_bias": np.stack([a["L3_gnn_b_l"], a["L3_gnn_b_r"], a["L3_gnn_bias"]]).reshape(1, 3 * FEAT),
        "l3_bt": np.ascontiguousarray(np.stack([a["L3_gnn_b_l"].reshape(CHUNKS, P).T,
                                                a["L3_gnn_b_r"].reshape(CHUNKS, P).T], axis=1)),
        "l3_att": a["L3_gnn_att"].reshape(1, FEAT),
        "l3_attt": np.ascontiguousarray(a["L3_gnn_att"].reshape(CHUNKS, P).T),
    }


def kernel(**inputs):
    import numpy as np
    import concourse.bacc as bacc
    from concourse.bass_utils import run_bass_kernel_spmd
    arrays = layouts({k: np.asarray(v) for k, v in inputs.items()})
    nc = bacc.Bacc("TRN2", target_bir_lowering=False, num_devices=1)
    io = {k: nc.dram_tensor(f"in_{k}", v.shape, mybir.dt.from_np(v.dtype), kind="ExternalInput").ap()
          for k, v in arrays.items()}
    out = nc.dram_tensor("out", (NODES, FEAT), F32, kind="ExternalOutput").ap()
    build(nc, io, out)
    result = run_bass_kernel_spmd(nc, [{f"in_{k}": v for k, v in arrays.items()}], core_ids=[0])
    return result.results[0]["out"]
```
